# Optimizing a Trainium2 kernel written in Bass

```python
import numpy as np
import jax
import jax.numpy as jnp

def _softmax(x, axis=-1):
    return jax.nn.softmax(x, axis=axis)

def _gelu(x):
    return jax.nn.gelu(x, approximate=True)

def _silu(x):
    return jax.nn.silu(x)

def _sigmoid(x):
    return jax.nn.sigmoid(x)

def _layernorm(x, axis=-1, eps=1e-05):
    m = jnp.mean(x, axis=axis, keepdims=True)
    v = jnp.var(x, axis=axis, keepdims=True)
    return (x - m) / jnp.sqrt(v + eps)

def _scatter_add(tgt, idx, src, axis=0):
    return tgt.at[idx].add(src)

def _segment_sum(src, seg, n):
    return jax.ops.segment_sum(src, seg, n)
kernel_name = 'mk_perceiver_d2_seqx_r2_b53e89'

def setup_inputs(seed: int=0):
    np.random.seed(seed)
    _w = jnp.asarray

    def _rec_inputs():
        import jax
        import jax.numpy as jnp
        _rk = jax.random.key(seed)
        x = -0.000125 + 0.9999 * jax.random.normal(jax.random.fold_in(_rk, 1), (32, 32, 512), jnp.float32)
        _lenS = 32 - jax.random.randint(jax.random.fold_in(_rk, 7), (32,), 0, max(1, 32 // 4) + 1, jnp.int32)
        _lenS2 = 257 - jax.random.randint(jax.random.fold_in(_rk, 8), (32,), 0, max(1, 257 // 4) + 1, jnp.int32)
        _ctx_1024P = jax.random.normal(jax.random.fold_in(_rk, 11), (32, 16, 512), jnp.float32)
        _ctx_1024c = jax.random.dirichlet(jax.random.fold_in(_rk, 511), 0.3 * jnp.ones((16,), jnp.float32), (32, 257))
        _ctx_1024t = jnp.einsum('bsk,bkd->bsd', _ctx_1024c, _ctx_1024P)
        _ctx_1024t = _ctx_1024t * jax.lax.rsqrt(jnp.mean(jnp.square(_ctx_1024t)) + 1e-12) * 0.953939
        ctx_1024 = -1.78809e-06 + 0.0312453 * (_ctx_1024t + 0.3 * jax.random.normal(jax.random.fold_in(_rk, 611), (32, 257, 512), jnp.float32))
        return (x, ctx_1024)
    x, ctx_1024 = _rec_inputs()

    def _L0_xattn_setup():
        import jax, jax.numpy as jnp
        import numpy as np
        E, T, H, F = (16, 1024, 512, 2048)
        key = jax.random.key(seed)
        kx, k1, k2, k3 = jax.random.split(key, 4)
        s = 1.0 / np.sqrt(H)
        return {'x': jax.random.normal(kx, (E, T, H), dtype=jnp.float32), 'w1': jax.random.normal(k1, (E, F, H), dtype=jnp.float32) * s, 'v1': jax.random.normal(k2, (E, F, H), dtype=jnp.float32) * s, 'w2': jax.random.normal(k3, (E, F, H), dtype=jnp.float32) * s}
    _L0_xattn_all = _L0_xattn_setup()
    _L0_xattn_in = {k: v for k, v in _L0_xattn_all.items() if k in ()}
    del _L0_xattn_all

    def _L0_attn_setup():
        import jax, jax.numpy as jnp
        import numpy as np
        DIM = 512
        N_HEADS = 16
        HEAD_DIM = DIM // N_HEADS
        B, T = (2, 1024)
        ROPE_THETA = 32.0
        EPS = 1e-06

        def precompute_freqs_1d(dim, seq_len, theta):
            freqs = theta ** (-jnp.arange(0, dim, 2, dtype=jnp.float32) / dim)
            t = jnp.arange(seq_len, dtype=jnp.float32)
            ang = t[:, None] * freqs[None, :]
            return (jnp.cos(ang), jnp.sin(ang))

        def _rms_norm(t, w):
            var = jnp.mean(t * t, axis=-1, keepdims=True)
            return t * jax.lax.rsqrt(var + EPS) * w

        def _rope(q, k, cos, sin):
            cos = cos[None, None]
            sin = sin[None, None]
            q1, q2 = jnp.split(q, 2, axis=-1)
            k1, k2 = jnp.split(k, 2, axis=-1)
            q_out = jnp.concatenate([q1 * cos - q2 * sin, q2 * cos + q1 * sin], axis=-1)
            k_out = jnp.concatenate([k1 * cos - k2 * sin, k2 * cos + k1 * sin], axis=-1)
            return (q_out, k_out)
        key = jax.random.key(seed)
        k1, k2, k3, k4, k5 = jax.random.split(key, 5)
        x = jax.random.normal(k1, (B, T, DIM), dtype=jnp.float32)
        w_qkv = jax.random.normal(k2, (3 * DIM, DIM), dtype=jnp.float32) * DIM ** (-0.5)
        w_proj = jax.random.normal(k3, (DIM, DIM), dtype=jnp.float32) * DIM ** (-0.5)
        q_norm_w = 1.0 + 0.1 * jax.random.normal(k4, (HEAD_DIM,), dtype=jnp.float32)
        k_norm_w = 1.0 + 0.1 * jax.random.normal(k5, (HEAD_DIM,), dtype=jnp.float32)
        return {'x': x, 'w_qkv': w_qkv, 'w_proj': w_proj, 'q_norm_w': q_norm_w, 'k_norm_w': k_norm_w}
    _L0_attn_all = _L0_attn_setup()
    _L0_attn_in = {k: v for k, v in _L0_attn_all.items() if k in ('w_qkv', 'w_proj', 'q_norm_w', 'k_norm_w')}
    del _L0_attn_all

    def _L0_ffn_setup():
        import jax, jax.numpy as jnp
        import numpy as np
        import math
        E = 32
        K = 2
        CF = 1.2
        D = 512
        F = 2048
        key = jax.random.key(seed)
        ks = jax.random.split(key, 7)
        s = 0.02
        return {'x': jax.random.normal(ks[0], (4, 1024, D), jnp.float32), 'gate_w': jax.random.normal(ks[1], (D, E), jnp.float32) * s, 'gate_b': jnp.zeros((E,), jnp.float32), 'w1': jax.random.normal(ks[2], (E, D, F), jnp.float32) * s, 'b1': jnp.zeros((E, F), jnp.float32), 'w2': jax.random.normal(ks[3], (E, F, D), jnp.float32) * s, 'b2': jnp.zeros((E, D), jnp.float32)}
    _L0_ffn_all = _L0_ffn_setup()
    _L0_ffn_in = {k: v for k, v in _L0_ffn_all.items() if k in ('gate_w', 'gate_b', 'w1', 'b1', 'w2', 'b2')}
    del _L0_ffn_all

    def _L1_xattn_setup():
        import jax, jax.numpy as jnp
        import numpy as np
        HID = 512
        HEADS = 16

        def _split_heads(x, h):
            b, s, d = x.shape
            return x.reshape(b, s, h, d // h).transpose(0, 2, 1, 3)
        key = jax.random.key(seed)
        ks = jax.random.split(key, 10)
        s = 0.02
        return {'x1': jax.random.normal(ks[0], (4, 1024, HID), jnp.float32), 'x2': jax.random.normal(ks[1], (4, 1024, HID), jnp.float32), 'Wq': jax.random.normal(ks[2], (HID, HID), jnp.float32) * s, 'bq': jnp.zeros((HID,), jnp.float32), 'Wk': jax.random.normal(ks[3], (HID, HID), jnp.float32) * s, 'bk': jnp.zeros((HID,), jnp.float32), 'Wv': jax.random.normal(ks[4], (HID, HID), jnp.float32) * s, 'bv': jnp.zeros((HID,), jnp.float32), 'Wo': jax.random.normal(ks[5], (HID, HID), jnp.float32) * s, 'bo': jnp.zeros((HID,), jnp.float32)}
    _L1_xattn_all = _L1_xattn_setup()
    _L1_xattn_in = {k: v for k, v in _L1_xattn_all.items() if k in ('Wq', 'bq', 'Wk', 'bk', 'Wv', 'bv', 'Wo', 'bo')}
    del _L1_xattn_all

    def _L1_attn_setup():
        import jax, jax.numpy as jnp
        import numpy as np
        import math
        D_MODEL = 512
        N_HEADS = 16
        EPS_GN = 1e-05

        def channel_group_norm(x, gamma, beta, num_groups, eps=EPS_GN):
            B, T, D = x.shape
            g = num_groups
            xt = x.transpose(0, 2, 1).reshape(B, g, D // g, T)
            mu = xt.mean(axis=(2, 3), keepdims=True)
            var = xt.var(axis=(2, 3), keepdims=True)
            xn = ((xt - mu) / jnp.sqrt(var + eps)).reshape(B, D, T)
            xn = xn * gamma[None, :, None] + beta[None, :, None]
            return xn.transpose(0, 2, 1)

        def l2_normalize(x, eps=1e-12):
            n = jnp.linalg.norm(x, axis=-1, keepdims=True)
            return x / jnp.maximum(n, eps)

        def decay_gammas(num_heads, dtype=jnp.float32):
            return 1.0 - jnp.exp(jnp.linspace(math.log(1.0 / 32.0), math.log(1.0 / 512.0), num_heads)).astype(dtype)
        key = jax.random.key(seed)
        ks = jax.random.split(key, 16)
        B, T, D = (4, 512, D_MODEL)
        s = 1.0 / math.sqrt(D)
        inp = {'x': jax.random.normal(ks[0], (B, T, D), jnp.float32), 'norm_g': jnp.ones((D,), jnp.float32), 'norm_b': jnp.zeros((D,), jnp.float32), 'qw': jax.random.normal(ks[1], (D, D), jnp.float32) * s, 'kw': jax.random.normal(ks[2], (D, D), jnp.float32) * s, 'vw': jax.random.normal(ks[3], (D, D), jnp.float32) * s, 'ow': jax.random.normal(ks[4], (D, D), jnp.float32) * s, 'ob': jnp.zeros((D,), jnp.float32), 'ffn_norm_g': jnp.ones((D,), jnp.float32), 'ffn_norm_b': jnp.zeros((D,), jnp.float32), 'w1': jax.random.normal(ks[5], (2 * D, D), jnp.float32) * s, 'b1': jnp.zeros((2 * D,), jnp.float32), 'w2': jax.random.normal(ks[6], (D, 2 * D), jnp.float32) * (1.0 / math.sqrt(2 * D)), 'b2': jnp.zeros((D,), jnp.float32)}
        return inp
    _L1_attn_all = _L1_attn_setup()
    _L1_attn_in = {k: v for k, v in _L1_attn_all.items() if k in ('norm_g', 'norm_b', 'qw', 'kw', 'vw', 'ow', 'ob', 'ffn_norm_g', 'ffn_norm_b', 'w1', 'b1', 'w2', 'b2')}
    del _L1_attn_all

    def _L1_ffn_setup():
        import jax, jax.numpy as jnp
        import numpy as np
        B, N, D = (4, 1024, 512)
        SPARSITY = 0.01
        key = jax.random.key(seed)
        k1, k2, k3 = jax.random.split(key, 3)
        x = jax.random.normal(k1, (B, N, D), dtype=jnp.float32)
        spatial = jax.random.normal(k2, (D, D), dtype=jnp.float32) * 0.02
        freq = jnp.fft.fft(spatial, axis=-1)
        k = int(D * SPARSITY)
        mag = jnp.abs(freq)
        kth = jax.lax.top_k(mag, k)[0][:, -1:]
        w_sparse = jnp.where(mag >= kth, freq, 0.0 + 0j)
        bias = jax.random.normal(k3, (D,), dtype=jnp.float32) * 0.01
        return {'x': x, 'w_freq_real': jnp.real(w_sparse).astype(jnp.float32), 'w_freq_imag': jnp.imag(w_sparse).astype(jnp.float32), 'bias': bias}
    _L1_ffn_all = _L1_ffn_setup()
    _L1_ffn_in = {k: v for k, v in _L1_ffn_all.items() if k in ('w_freq_real', 'w_freq_imag', 'bias')}
    del _L1_ffn_all
    return {'x': x, 'ctx_1024': ctx_1024, 'L0_attn_w_qkv': _L0_attn_in['w_qkv'], 'L0_attn_w_proj': _L0_attn_in['w_proj'], 'L0_attn_q_norm_w': _L0_attn_in['q_norm_w'], 'L0_attn_k_norm_w': _L0_attn_in['k_norm_w'], 'L0_ffn_gate_w': _L0_ffn_in['gate_w'], 'L0_ffn_gate_b': _L0_ffn_in['gate_b'], 'L0_ffn_w1': _L0_ffn_in['w1'], 'L0_ffn_b1': _L0_ffn_in['b1'], 'L0_ffn_w2': _L0_ffn_in['w2'], 'L0_ffn_b2': _L0_ffn_in['b2'], 'L1_xattn_Wq': _L1_xattn_in['Wq'], 'L1_xattn_bq': _L1_xattn_in['bq'], 'L1_xattn_Wk': _L1_xattn_in['Wk'], 'L1_xattn_bk': _L1_xattn_in['bk'], 'L1_xattn_Wv': _L1_xattn_in['Wv'], 'L1_xattn_bv': _L1_xattn_in['bv'], 'L1_xattn_Wo': _L1_xattn_in['Wo'], 'L1_xattn_bo': _L1_xattn_in['bo'], 'L1_attn_norm_g': _L1_attn_in['norm_g'], 'L1_attn_norm_b': _L1_attn_in['norm_b'], 'L1_attn_qw': _L1_attn_in['qw'], 'L1_attn_kw': _L1_attn_in['kw'], 'L1_attn_vw': _L1_attn_in['vw'], 'L1_attn_ow': _L1_attn_in['ow'], 'L1_attn_ob': _L1_attn_in['ob'], 'L1_attn_ffn_norm_g': _L1_attn_in['ffn_norm_g'], 'L1_attn_ffn_norm_b': _L1_attn_in['ffn_norm_b'], 'L1_attn_w1': _L1_attn_in['w1'], 'L1_attn_b1': _L1_attn_in['b1'], 'L1_attn_w2': _L1_attn_in['w2'], 'L1_attn_b2': _L1_attn_in['b2'], 'L1_ffn_w_freq_real': _L1_ffn_in['w_freq_real'], 'L1_ffn_w_freq_imag': _L1_ffn_in['w_freq_imag'], 'L1_ffn_bias': _L1_ffn_in['bias']}

def reference(x, ctx_1024, L0_attn_w_qkv, L0_attn_w_proj, L0_attn_q_norm_w, L0_attn_k_norm_w, L0_ffn_gate_w, L0_ffn_gate_b, L0_ffn_w1, L0_ffn_b1, L0_ffn_w2, L0_ffn_b2, L1_xattn_Wq, L1_xattn_bq, L1_xattn_Wk, L1_xattn_bk, L1_xattn_Wv, L1_xattn_bv, L1_xattn_Wo, L1_xattn_bo, L1_attn_norm_g, L1_attn_norm_b, L1_attn_qw, L1_attn_kw, L1_attn_vw, L1_attn_ow, L1_attn_ob, L1_attn_ffn_norm_g, L1_attn_ffn_norm_b, L1_attn_w1, L1_attn_b1, L1_attn_w2, L1_attn_b2, L1_ffn_w_freq_real, L1_ffn_w_freq_imag, L1_ffn_bias):
    import jax
    import jax.numpy as jnp

    def _L0_xattn_ref(x, w1, v1, w2):
        import jax, jax.numpy as jnp
        import numpy as np
        E, T, H, F = (16, 1024, 512, 2048)
        x1 = jnp.einsum('eth,efh->etf', x, w1)
        x2 = jnp.einsum('eth,efh->etf', x, v1)
        h = jax.nn.gelu(x1, approximate=True) * x2
        return jnp.einsum('etf,efh->eth', h, w2)

    def _L0_attn_ref(x, w_qkv, w_proj, q_norm_w, k_norm_w):
        import jax, jax.numpy as jnp
        import numpy as np
        DIM = 512
        N_HEADS = 16
        HEAD_DIM = DIM // N_HEADS
        B, T = (2, 1024)
        ROPE_THETA = 32.0
        EPS = 1e-06

        def precompute_freqs_1d(dim, seq_len, theta):
            freqs = theta ** (-jnp.arange(0, dim, 2, dtype=jnp.float32) / dim)
            t = jnp.arange(seq_len, dtype=jnp.float32)
            ang = t[:, None] * freqs[None, :]
            return (jnp.cos(ang), jnp.sin(ang))

        def _rms_norm(t, w):
            var = jnp.mean(t * t, axis=-1, keepdims=True)
            return t * jax.lax.rsqrt(var + EPS) * w

        def _rope(q, k, cos, sin):
            cos = cos[None, None]
            sin = sin[None, None]
            q1, q2 = jnp.split(q, 2, axis=-1)
            k1, k2 = jnp.split(k, 2, axis=-1)
            q_out = jnp.concatenate([q1 * cos - q2 * sin, q2 * cos + q1 * sin], axis=-1)
            k_out = jnp.concatenate([k1 * cos - k2 * sin, k2 * cos + k1 * sin], axis=-1)
            return (q_out, k_out)
        Bc, Tc, C = x.shape
        scale = HEAD_DIM ** (-0.5)
        qkv = x @ w_qkv.T
        qkv = qkv.reshape(Bc, Tc, 3, N_HEADS, HEAD_DIM).transpose(2, 0, 3, 1, 4)
        q, k, v = (qkv[0], qkv[1], qkv[2])
        q = _rms_norm(q, q_norm_w)
        k = _rms_norm(k, k_norm_w)
        cos, sin = precompute_freqs_1d(HEAD_DIM, Tc, ROPE_THETA)
        q, k = _rope(q, k, cos, sin)
        attn = jnp.einsum('bhqd,bhkd->bhqk', q, k) * scale
        causal = jnp.triu(jnp.ones((Tc, Tc), dtype=bool), k=1)
        attn = jnp.where(causal, -jnp.inf, attn)
        attn = jax.nn.softmax(attn, axis=-1)
        out = jnp.einsum('bhqk,bhkd->bhqd', attn, v)
        out = out.transpose(0, 2, 1, 3).reshape(Bc, Tc, C)
        return out @ w_proj.T

    def _L0_ffn_ref(x, gate_w, gate_b, w1, b1, w2, b2):
        import jax, jax.numpy as jnp
        import numpy as np
        import math
        E = 32
        K = 2
        CF = 1.2
        D = 512
        F = 2048
        orig_shape = x.shape
        xt = x.reshape(-1, D)
        T = xt.shape[0]
        C = int(math.ceil(T * K / E * CF))
        logits = xt @ gate_w + gate_b
        probs = jax.nn.softmax(logits, axis=-1)
        top_w, top_i = jax.lax.top_k(probs, K)
        w = top_w / jnp.sum(top_w, axis=-1, keepdims=True)
        flat_e = top_i.reshape(-1)
        oh = jax.nn.one_hot(flat_e, E, dtype=jnp.int32)
        pos_all = jnp.cumsum(oh, axis=0) - 1
        pos = jnp.take_along_axis(pos_all, flat_e[:, None], axis=1)[:, 0]
        valid = pos < C
        pos_d = jnp.where(valid, pos, C)
        x_rep = jnp.repeat(xt, K, axis=0)
        xe = jnp.zeros((E, C, D), x.dtype).at[flat_e, pos_d].add(x_rep, mode='drop')
        he = jax.nn.gelu(jnp.einsum('ecd,edf->ecf', xe, w1) + b1[:, None, :], approximate=False)
        ye = jnp.einsum('ecf,efd->ecd', he, w2) + b2[:, None, :]
        y_flat = ye[flat_e, jnp.minimum(pos, C - 1)] * valid[:, None].astype(x.dtype)
        y = (y_flat.reshape(T, K, D) * w[..., None]).sum(axis=1)
        return y.reshape(orig_shape)

    def _L1_xattn_ref(x1, x2, Wq, bq, Wk, bk, Wv, bv, Wo, bo):
        import jax, jax.numpy as jnp
        import numpy as np
        HID = 512
        HEADS = 16

        def _split_heads(x, h):
            b, s, d = x.shape
            return x.reshape(b, s, h, d // h).transpose(0, 2, 1, 3)
        q = _split_heads(x1 @ Wq.T + bq, HEADS)
        k = _split_heads(x2 @ Wk.T + bk, HEADS)
        v = _split_heads(x2 @ Wv.T + bv, HEADS)
        dh = q.shape[-1]
        scores = jnp.einsum('bhqd,bhkd->bhqk', q, k) / jnp.sqrt(jnp.float32(dh))
        attn = jax.nn.softmax(scores, axis=-1)
        out = jnp.einsum('bhqk,bhkd->bhqd', attn, v)
        b, h, sq, _ = out.shape
        out = out.transpose(0, 2, 1, 3).reshape(b, sq, h * dh)
        return out @ Wo.T + bo

    def _L1_attn_ref(x, norm_g, norm_b, qw, kw, vw, ow, ob, ffn_norm_g, ffn_norm_b, w1, b1, w2, b2):
        import jax, jax.numpy as jnp
        import numpy as np
        import math
        D_MODEL = 512
        N_HEADS = 16
        EPS_GN = 1e-05

        def channel_group_norm(x, gamma, beta, num_groups, eps=EPS_GN):
            B, T, D = x.shape
            g = num_groups
            xt = x.transpose(0, 2, 1).reshape(B, g, D // g, T)
            mu = xt.mean(axis=(2, 3), keepdims=True)
            var = xt.var(axis=(2, 3), keepdims=True)
            xn = ((xt - mu) / jnp.sqrt(var + eps)).reshape(B, D, T)
            xn = xn * gamma[None, :, None] + beta[None, :, None]
            return xn.transpose(0, 2, 1)

        def l2_normalize(x, eps=1e-12):
            n = jnp.linalg.norm(x, axis=-1, keepdims=True)
            return x / jnp.maximum(n, eps)

        def decay_gammas(num_heads, dtype=jnp.float32):
            return 1.0 - jnp.exp(jnp.linspace(math.log(1.0 / 32.0), math.log(1.0 / 512.0), num_heads)).astype(dtype)
        B, T, D = x.shape
        H = N_HEADS
        dh = D // H
        residual = x
        xn = channel_group_norm(x, norm_g, norm_b, H)
        q = l2_normalize(xn @ qw.T)
        k = l2_normalize(xn @ kw.T)
        v = xn @ vw.T

        def heads(t):
            return t.reshape(B, T, H, dh).transpose(0, 2, 1, 3)
        qh, kh, vh = (heads(q), heads(k), heads(v))
        gammas = decay_gammas(H)
        n = jnp.arange(T)[:, None]
        m = jnp.arange(T)[None, :]
        diff = n - m
        causal = diff >= 0
        exponent = jnp.where(causal, diff, 0).astype(jnp.float32)
        dmask = jnp.where(causal[None], gammas[:, None, None] ** exponent[None], 0.0)
        scale = 1.0 / math.sqrt(dh)
        sim = jnp.einsum('bhnd,bhmd->bhnm', qh, kh) * scale
        sim = sim * dmask[None]
        yh = jnp.einsum('bhnm,bhmd->bhnd', sim, vh)
        y = yh.transpose(0, 2, 1, 3).reshape(B, T, D)
        y = y @ ow.T + ob
        x = residual + y
        residual = x
        xn = channel_group_norm(x, ffn_norm_g, ffn_norm_b, H)
        h = jax.nn.silu(xn @ w1.T + b1)
        x = residual + (h @ w2.T + b2)
        return x

    def _L1_ffn_ref(x, w_freq_real, w_freq_imag, bias):
        import jax, jax.numpy as jnp
        import numpy as np
        B, N, D = (4, 1024, 512)
        SPARSITY = 0.01
        w = jax.lax.complex(w_freq_real, w_freq_imag)
        x_freq = jnp.fft.fft(x, axis=-1)
        y_freq = jnp.einsum('bnd,do->bno', x_freq, w)
        y = jnp.real(jnp.fft.ifft(y_freq, axis=-1))
        return y + bias
    x = x + _L0_xattn_ref(_layernorm(x, axis=-1), ctx_1024, ctx_1024, ctx_1024)
    x = x + _L0_attn_ref(_layernorm(x, axis=-1), L0_attn_w_qkv, L0_attn_w_proj, L0_attn_q_norm_w, L0_attn_k_norm_w)
    x = x + _L0_ffn_ref(_layernorm(x, axis=-1), L0_ffn_gate_w, L0_ffn_gate_b, L0_ffn_w1, L0_ffn_b1, L0_ffn_w2, L0_ffn_b2)
    x = x + _L1_xattn_ref(_layernorm(x, axis=-1), ctx_1024, L1_xattn_Wq, L1_xattn_bq, L1_xattn_Wk, L1_xattn_bk, L1_xattn_Wv, L1_xattn_bv, L1_xattn_Wo, L1_xattn_bo)
    x = x + _L1_attn_ref(_layernorm(x, axis=-1), L1_attn_norm_g, L1_attn_norm_b, L1_attn_qw, L1_attn_kw, L1_attn_vw, L1_attn_ow, L1_attn_ob, L1_attn_ffn_norm_g, L1_attn_ffn_norm_b, L1_attn_w1, L1_attn_b1, L1_attn_w2, L1_attn_b2)
    x = x + _L1_ffn_ref(_layernorm(x, axis=-1), L1_ffn_w_freq_real, L1_ffn_w_freq_imag, L1_ffn_bias)
    return x

_drawn_inputs = setup_inputs


def setup_inputs(seed=0):
    import zlib

    import numpy as np

    out = dict(_drawn_inputs(seed))
    spreads = {'L0_ffn_gate_b': (0.0, 0.1),
     'L0_ffn_b1': (0.0, 0.399),
     'L0_ffn_b2': (0.0, 0.1),
     'L1_xattn_bq': (0.0, 2.0),
     'L1_xattn_bk': (0.0, 2.0),
     'L1_xattn_bv': (0.0, 0.295),
     'L1_xattn_bo': (0.0, 0.1),
     'L1_attn_norm_g': (1.0, 0.6),
     'L1_attn_norm_b': (0.0, 0.8),
     'L1_attn_ob': (0.0, 0.274),
     'L1_attn_ffn_norm_g': (1.0, 0.2),
     'L1_attn_ffn_norm_b': (0.0, 0.364),
     'L1_attn_b1': (0.0, 0.35),
     'L1_attn_b2': (0.0, 0.295)}
    factors = {'L0_attn_k_norm_w': 2.865,
     'L1_xattn_Wq': 64.0,
     'L1_xattn_Wk': 64.0,
     'L1_xattn_Wv': 23.741,
     'L1_attn_qw': 8.0,
     'L1_attn_kw': 8.0,
     'L1_attn_vw': 8.0,
     'L1_attn_ow': 8.0,
     'L1_ffn_bias': 22.478}
    for name, (base, spread) in spreads.items():
        noise = np.random.default_rng([zlib.crc32(name.encode()), seed]).standard_normal(out[name].shape)
        drawn = base * np.exp(spread * noise) if base else spread * noise
        out[name] = jnp.asarray(drawn.astype(out[name].dtype))
    for name, factor in factors.items():
        out[name] = (out[name] * factor).astype(out[name].dtype)
    return out
```

```python
import numpy as np
from contextlib import ExitStack

import concourse.bass as bass
from concourse import mybir

B, T, D = 32, 32, 512
S = 257
P = 128
NT = B * T // P
NB = P // T
H, DH = 16, 32
HG, HQ = 4, 4
KD = D // P
SC = 86
SJ = 3
SL = S - 2 * SC
E, F = 32, 2048
CAP = 77
FT = F // P
F2 = 2 * D
FT2 = F2 // P
BIGROW = 4096.0
LN_EPS, RMS_EPS, GN_EPS = 1e-5, 1e-6, 1e-5
SS_SCALE = 2.0 ** 30

fp32 = mybir.dt.float32
u32 = mybir.dt.uint32
ALU = mybir.AluOpType
ACT = mybir.ActivationFunctionType
AX = mybir.AxisListType


class Steps:

    def __init__(self, eng, sem):
        self.eng, self.sem, self.base, self.per, self.i, self.k = eng, sem, 0, 0, None, 0

    def loop(self, i, per):
        self.base += self.k
        self.i, self.per, self.k = i, per, 0

    def leave(self, turns):
        assert self.k == self.per, f"the loop's turn has {self.k} steps, not {self.per}"
        self.base += turns * self.per
        self.i, self.k = None, 0

    def step(self, ins):
        ins.then_inc(self.sem, 1)
        self.k += 1
        at = self.base + self.k
        self.eng.wait_ge(self.sem, at if self.i is None else self.i * self.per + at)


def perceiver_kernel(nc, x, ctx, ctxT, wqkv0T, wproj0T, qkw, qkw_sw, cosT, sinS, gate_w, gate_b,
                     w1, b1, w2, b2, WqT, bq, WkT, bk, WvT, bv, WoT, bo,
                     gng, gnb, wqkv1T, owT, ob, fng, fnb, fw1T, fb1, fw2T, fb2,
                     Wr, Wi, fbias, dftC, dftS, dftN, ident, tri, ones, gones, causal,
                     decay, iotad, out, xe_dram, y_dram):
    with ExitStack() as st:
        def sem(name):
            return st.enter_context(nc.semaphore(name))

        WORDS = 53000
        arena = st.enter_context(nc.sbuf_tensor("arena", [P, WORDS], fp32))
        ps = st.enter_context(nc.psum_tensor("ps", [P, 8, 512], fp32))
        uidx = st.enter_context(nc.sbuf_tensor("uidx", [P, 2, 2, NT], u32))

        def view(off, *dims):
            n = int(np.prod(dims))
            assert off + n <= WORDS, (off, dims)
            a = arena[:, off:off + n]
            if len(dims) == 2:
                a = a.rearrange("p (a b) -> p a b", a=dims[0])
            if len(dims) == 3:
                a = a.rearrange("p (a b c) -> p a b c", a=dims[0], b=dims[1])
            if len(dims) == 4:
                a = a.rearrange("p (a b c d) -> p a b c d", a=dims[0], b=dims[1], c=dims[2])
            return a

        class Region:
            def __init__(self, off, size):
                self.at, self.end = off, off + size

            def take(self, *dims):
                n = int(np.prod(dims))
                assert self.at + n <= self.end, (dims, self.at + n - self.end)
                self.at += n
                return view(self.at - n, *dims)

        keep = Region(0, WORDS)
        x_sb = keep.take(NT, D)
        xhat = keep.take(NT, D)
        M_sb = keep.take(KD, D)
        id_sb, tri_sb, ones_sb, gones_sb = (keep.take(P) for _ in range(4))
        causal_sb, iotad_sb = keep.take(T), keep.take(E)
        gw_sb, gb_sb = keep.take(KD, E), keep.take(E)
        lg = keep.take(NT, E)
        wts = keep.take(2, NT)
        b1_sb = keep.take(E, FT)
        mv, stats, rstd, lnv = keep.take(2), keep.take(6), keep.take(1), keep.take(1)
        xn, xnT = keep.take(D), keep.take(KD, P)
        RW = KD * F
        ring_off = [[keep.at + (2 * a + b) * RW for b in range(2)] for a in range(2)]
        w1_sb = [view(ring_off[s][0], KD, F) for s in range(2)]
        w2_sb = [view(ring_off[s][1], FT, D) for s in range(2)]
        work_off = keep.at + 4 * RW
        work_size = WORDS - work_off

        rM = Region(ring_off[0][0], 2 * RW)
        C_sb, S_sb, N_sb, Wr_sb, Wi_sb, ATr, ATi = (rM.take(KD, D) for _ in range(7))

        rA = Region(ring_off[1][0], RW)
        wqkv0_sb, wproj0_sb = rA.take(KD, 3 * D), rA.take(KD, D)
        rA = Region(ring_off[1][1], RW)
        ctx_sb = rA.take(NB, SJ, D)
        CW, SW = rA.take(2, DH), rA.take(2, DH)
        cos_sb, sin_sb, qkw_sb, qkws_sb = rA.take(DH), rA.take(DH), rA.take(2, DH), rA.take(2, DH)
        W = Region(work_off, work_size)
        ctxT_sb = W.take(NB, KD, SC * SJ)
        rA = Region(ring_off[0][0], 2 * RW)
        g_sb, hTA = rA.take(NB, SJ * T), rA.take(NB, SJ, T)
        qkn, ropeA, ropeB, qkr, sq = (rA.take(2 * H, DH) for _ in range(5))
        ms, lnms, rs = rA.take(2 * H), rA.take(2 * H), rA.take(2 * H)
        qkT = rA.take(2, KD, P)
        vA = rA.take(D)
        sA, pA, pT = rA.take(H, T), rA.take(H, T), rA.take(H, T)
        mxA, sumA, rsA = rA.take(H), rA.take(H), rA.take(H)
        PTb = rA.take(H, P)
        oTA = rA.take(KD, P)

        W = Region(work_off, work_size)
        prob, t_a, t_b, oh1, oh2, cnt = (W.take(NT, E) for _ in range(6))
        off_sb = W.take(NT, E)
        pm1, pm2, rv1, rv2, rv3 = (W.take(NT) for _ in range(5))
        kk, pos, val, gidx, sidx = (W.take(2, NT) for _ in range(5))

        W = Region(work_off, work_size)
        hT = [W.take(FT, CAP) for _ in range(2)]
        xeT = [W.take(KD, CAP) for _ in range(2)]
        y_sb = [W.take(D) for _ in range(2)]
        b2_sb = [W.take(D) for _ in range(2)]
        xe_sb = [W.take(D) for _ in range(2)]
        zeros = view(ring_off[1][0], 4, D)
        yg = view(ring_off[1][1], 2 * NT, D)

        rC = Region(ring_off[0][0], RW)
        WkT_sb, WvT_sb, WqT_sb, WoT_sb = (rC.take(KD, D) for _ in range(4))
        rC = Region(ring_off[0][1], RW)
        wqkv1_sb, ow_sb = rC.take(KD, 3 * D), rC.take(KD, D)
        rC = Region(ring_off[1][0], RW)
        fw1_sb, fw2_sb = rC.take(KD, F2), rC.take(FT2, D)
        W = Region(work_off, work_size)
        ctxT_c = W.take(2, KD, SC * SJ)
        PTd = W.take(H, P)
        bv_sb, bo_sb, ob_sb, fb2_sb, fbias_sb = (W.take(D) for _ in range(5))
        decay_sb = W.take(H, T)
        bq_sb, bk_sb, gng_sb, gnb_sb, fng_sb, fnb_sb = (W.take(KD) for _ in range(6))
        fb1_sb = W.take(FT2)
        rC = Region(ring_off[1][1], RW)
        qTs = rC.take(KD, P)
        Qbd = rC.take(NB, HG, P)
        v_c, P_c, PT_c = rC.take(SJ, D), rC.take(HG, S), rC.take(SJ, HG * P)
        mxc, nmx, smc, rsc = (rC.take(HG) for _ in range(4))
        qk1 = rC.take(2, D)
        rC = Region(NT * D, NT * D)
        kT_c = rC.take(KD, S)
        oTc, r1, t1, t2, x2 = (rC.take(D) for _ in range(5))
        gs, gvar = rC.take(2 * H), rC.take(H)
        gm, g2, glr, grs = (rC.take(H) for _ in range(4))
        ssq, ssl, nrm = rC.take(2), rC.take(2), rC.take(2)
        rC = Region(ring_off[1][1] + D + NB * HG * P, SJ * D + HG * S + SJ * HG * P)
        qkT1, v1 = rC.take(2, KD, P), rC.take(D)
        hT2 = rC.take(FT2, P)

        consts_in, x_in, dft_in, wA_in, wC_in, b1_in = (sem(n) for n in (
            "consts_in", "x_in", "dft_in", "wA_in", "wC_in", "b1_in"))
        pads_zero, zeros_set, xe_zeroed = sem("pads_zero"), sem("zeros_set"), sem("xe_zeroed")
        dve_step, act_step = sem("dve_step"), sem("act_step")
        at_ps, at_sb, m_ps, m_sb = sem("at_ps"), sem("at_sb"), sem("m_ps"), sem("m_sb")
        ln_stats, ln_rstd = sem("ln_stats"), sem("ln_rstd")
        xn_rdy, xT_ps, xT_rdy = sem("xn_rdy"), sem("xT_ps"), sem("xT_rdy")
        ctx_in = [sem(f"ctx_in{b}") for b in range(NB)]
        x1_ps, g_rdy, hTA_rdy, gated_ps = sem("x1_ps"), sem("g_rdy"), sem("hTA_rdy"), sem("gated_ps")
        qkv_ps, sq_rdy, vA_rdy, ms_rdy, rs_rdy, qkr_rdy = (sem(n) for n in (
            "qkv_ps", "sq_rdy", "vA_rdy", "ms_rdy", "rs_rdy", "qkr_rdy"))
        qkT_ps, qkT_rdy, s_ps, sA_rdy, pA_rdy, PTb_rdy, oTA_ps, oTA_rdy, proj_ps, gate_ps = (sem(n) for n in (
            "qkT_ps", "qkT_rdy", "s_ps", "sA_rdy", "pA_rdy", "PTb_rdy", "oTA_ps", "oTA_rdy", "proj_ps", "gate_ps"))
        pr_sub, pr_exp, oh_rdy, cnt_ps, idx_rdy, scattered = (sem(n) for n in (
            "pr_sub", "pr_exp", "oh_rdy", "cnt_ps", "idx_rdy", "scattered"))
        w1_in, w2_in, xe_in, b2_in, y_stored = ([sem(f"{n}{s}") for s in range(2)] for n in (
            "w1_in", "w2_in", "xe_in", "b2_in", "y_stored"))
        xeT_ps, xeT_rdy, h_ps, hb_rdy, hT_rdy, y_ps, y_rdy = (sem(n) for n in (
            "xeT_ps", "xeT_rdy", "h_ps", "hb_rdy", "hT_rdy", "y_ps", "y_rdy"))
        gathered, moe_added = sem("gathered"), sem("moe_added")
        ctxc_in = [sem(f"ctxc_in{s}") for s in range(2)]
        q_ps, Qbd_rdy, k_ps, k_ev, sc_ps, nmx_rdy, exp_c, pn_rdy, v_ps, v_ev, pt_ps, pt_ev, pv_ps, oT_c = (
            sem(n) for n in ("q_ps", "Qbd_rdy", "k_ps", "k_ev", "sc_ps", "nmx_rdy", "exp_c", "pn_rdy",
                             "v_ps", "v_ev", "pt_ps", "pt_ev", "pv_ps", "oT_c"))
        wo_ps, gs_rdy, gst_ps, gv_rdy, grs_rdy = (sem(n) for n in (
            "wo_ps", "gs_rdy", "gst_ps", "gv_rdy", "grs_rdy"))
        qkv1_ps, ssq_rdy, ssc_rdy, nrm_rdy, v1_rdy, qk1_rdy, qkT1_ps, qkT1_rdy, st_ps, PTd_rdy = (
            sem(n) for n in ("qkv1_ps", "ssq_rdy", "ssc_rdy", "nrm_rdy", "v1_rdy", "qk1_rdy",
                             "qkT1_ps", "qkT1_rdy", "st_ps", "PTd_rdy"))
        oT1_ps, oT1_rdy, ow_ps, f1_ps, f1_rdy, f2_ps, spec_ps, out_rdy, stored = (sem(n) for n in (
            "oT1_ps", "oT1_rdy", "ow_ps", "f1_ps", "f1_rdy", "f2_ps", "spec_ps", "out_rdy", "stored"))

        SCALE = DH ** -0.5
        N_CONST = 8
        WA, WC = 6, 20
        q4 = [slice(32 * q, 32 * q + 32) for q in range(4)]
        HGROUPS = [(0, 6), (6, 12), (12, 16)]

        def rows(ap):
            return ap.rearrange("(k p) n -> p k n", p=P)

        def wait(eng, s, value):
            if not (isinstance(value, int) and value <= 0):
                eng.wait_ge(s, value)

        block = st.enter_context(nc.Block())

        @block.sync
        def _(sp):
            for dst, src in ((C_sb, dftC), (Wr_sb, Wr), (S_sb, dftS), (Wi_sb, Wi), (N_sb, dftN)):
                sp.dma_start(dst, rows(src)).then_inc(dft_in, 16)
            for dst, src in ((id_sb, ident), (tri_sb, tri), (ones_sb, ones), (gones_sb, gones),
                             (causal_sb, causal), (iotad_sb, iotad), (gw_sb, rows(gate_w)),
                             (gb_sb, gate_b.partition_broadcast(P))):
                sp.dma_start(dst, src).then_inc(consts_in, 16)
            sp.dma_start(x_sb, x.rearrange("(i p) d -> p i d", p=P)).then_inc(x_in, 16)
            sp.wait_ge(zeros_set, 1)
            for e in range(0, E, 4):
                sp.dma_start(xe_dram[e * CAP:(e + 4) * CAP, :].rearrange("(e c) d -> c e d", c=CAP),
                             zeros[0:CAP, :, :]).then_inc(xe_zeroed, 16)
            sp.wait_ge(xe_zeroed, 16 * (E // 4))
            sp.dma_start(wqkv0_sb, rows(wqkv0T)).then_inc(wA_in, 16)
            sp.dma_start(wproj0_sb, rows(wproj0T)).then_inc(wA_in, 16)
            for dst, src in ((cos_sb, cosT), (sin_sb, sinS), (qkw_sb, qkw.partition_broadcast(P)),
                             (qkws_sb, qkw_sw.partition_broadcast(P))):
                sp.dma_start(dst, src).then_inc(wA_in, 16)
            sp.dma_start(b1_sb, b1).then_inc(b1_in, 16)
            sp.wait_ge(pads_zero, 2)

            def load_ctx(i, b):
                sp.dma_start(ctxT_sb[:, b, :, 0:S],
                             ctxT[NB * i + b].rearrange("k p s -> p k s")).then_inc(ctx_in[b], 16)
                sp.dma_start(ctx_sb[0:SC, b, 0:2, :],
                             ctx[NB * i + b, 0:2 * SC, :].rearrange("(j p) d -> p j d", p=SC)
                             ).then_inc(ctx_in[b], 16)
                sp.dma_start(ctx_sb[0:SL, b, 2, :], ctx[NB * i + b, 2 * SC:S, :]).then_inc(ctx_in[b], 16)

            for b in range(NB):
                load_ctx(0, b)
            with sp.Fori(1, NT) as i:
                for b in range(NB):
                    sp.wait_ge(gated_ps, NB * i + (b - NB + 1))
                    load_ctx(i, b)

            def load_expert(e, s, i):
                def after(sm, value):
                    wait(sp, sm, value)
                after(h_ps, 3 * (e - 1))
                sp.dma_start(w1_sb[s], rows(w1[e])).then_inc(w1_in[s], 16)
                after(y_ps, e - 1)
                sp.dma_start(w2_sb[s], rows(w2[e])).then_inc(w2_in[s], 16)

            def load_rows(e, s):
                wait(sp, xeT_ps, e - 1)
                sp.dma_start(xe_sb[s][0:CAP, :], xe_dram[bass.ts(e, CAP), :]).then_inc(xe_in[s], 16)
                wait(sp, y_rdy, e - 1)
                sp.dma_start(b2_sb[s][0:CAP, :],
                             b2[bass.ts(e, 1), :].rearrange("a d -> (a d)").partition_broadcast(CAP)
                             ).then_inc(b2_in[s], 16)

            sp.wait_ge(gate_ps, NT)
            sp.wait_ge(oTA_rdy, NT)
            for s in range(2):
                load_expert(s, s, 0)
            sp.wait_ge(scattered, 16 * 2 * NT)
            for s in range(2):
                load_rows(s, s)
            with sp.Fori(1, E // 2) as i:
                for s in range(2):
                    load_rows(2 * i + s, s)
                    load_expert(2 * i + s, s, i)

            sp.wait_ge(h_ps, 3 * E)
            sp.wait_ge(y_ps, E)
            for s in range(2):
                sp.wait_ge(y_stored[s], 16 * (E // 2))
            for dst, src in ((WkT_sb, rows(WkT)), (WvT_sb, rows(WvT)), (WqT_sb, rows(WqT)),
                             (bq_sb, bq), (bk_sb, bk), (bv_sb, bv.partition_broadcast(P)),
                             (WoT_sb, rows(WoT)), (bo_sb, bo.partition_broadcast(P)),
                             (wqkv1_sb, rows(wqkv1T)), (gng_sb, gng), (gnb_sb, gnb),
                             (decay_sb, decay), (ow_sb, rows(owT)), (ob_sb, ob.partition_broadcast(P)),
                             (fng_sb, fng), (fnb_sb, fnb), (fb1_sb, fb1),
                             (fw1_sb, rows(fw1T)), (fw2_sb, rows(fw2T)),
                             (fb2_sb, fb2.partition_broadcast(P)),
                             (fbias_sb, fbias.partition_broadcast(P))):
                sp.dma_start(dst, src).then_inc(wC_in, 16)

            def load_ctxc(bb, s):
                sp.dma_start(ctxT_c[:, s, :, 0:S], ctxT[bb].rearrange("k p s -> p k s")).then_inc(ctxc_in[s], 16)

            for s in range(2):
                load_ctxc(s, s)
            def tile_c(i, more):
                for b in range(2, NB):
                    sp.wait_ge(v_ps, SJ * (NB * i + (b - 1)))
                    load_ctxc(NB * i + b, b % 2)
                if more:
                    for b in range(2):
                        sp.wait_ge(v_ps, SJ * (NB * i + (b + 3)))
                        load_ctxc(NB * i + (NB + b), b)
                sp.wait_ge(out_rdy, i + 1)
                sp.dma_start(out[bass.ts(i, P), :], x_sb[:, bass.ds(i, 1), :].rearrange("p a d -> p (a d)")
                             ).then_inc(stored, 16)

            with sp.Fori(0, NT - 1) as i:
                tile_c(i, True)
            tile_c(NT - 1, False)
            sp.wait_ge(stored, 16 * NT)

        @block.gpsimd
        def _(pool):
            pool.memset(zeros, 0.0).then_inc(zeros_set, 1)
            pool.memset(ctx_sb, 0.0).then_inc(pads_zero, 1)
            pool.memset(ctxT_sb, 0.0).then_inc(pads_zero, 1)
            pool.wait_ge(idx_rdy, 2)
            for i in range(NT):
                for k in range(2):
                    pool.indirect_dma_start(
                        out=xe_dram, out_offset=bass.IndirectOffsetOnAxis(ap=uidx[:, 0, k, i:i + 1], axis=0),
                        in_=xhat[:, i, :], in_offset=None, bounds_check=E * CAP - 1, oob_is_err=False
                    ).then_inc(scattered, 16)

            def store_y(e, s):
                pool.wait_ge(y_rdy, e + 1)
                pool.dma_start(y_dram[bass.ts(e, CAP), :], y_sb[s][0:CAP, :]).then_inc(y_stored[s], 16)

            with pool.Fori(0, E // 2) as i:
                for s in range(2):
                    store_y(2 * i + s, s)
            for s in range(2):
                pool.wait_ge(y_stored[s], 16 * (E // 2))
            for i in range(NT):
                for k in range(2):
                    pool.indirect_dma_start(
                        out=yg[:, 2 * i + k, :], out_offset=None, in_=y_dram,
                        in_offset=bass.IndirectOffsetOnAxis(ap=uidx[:, 1, k, i:i + 1], axis=0)
                    ).then_inc(gathered, 16)

        @block.scalar
        def _(act):
            my = Steps(act, act_step)

            def rsqrt(n):
                act.wait_ge(ln_stats, n + 1)
                my.step(act.activation(lnv, mv[:, 1:2], ACT.Ln, bias=LN_EPS, scale=1.0))
                act.activation(rstd, lnv, ACT.Exp, scale=-0.5).then_inc(ln_rstd, 1)

            def xT_out(n, gain=None, shift=None):
                act.wait_ge(xT_ps, n + 1)
                if gain is None:
                    act.activation(xnT, ps[:, 0, :].rearrange("p (k t) -> p k t", k=KD), ACT.Copy
                                   ).then_inc(xT_rdy, 1)
                    return
                for k in range(KD):
                    ins = act.activation(xnT[:, k, :], ps[:, 0, k * P:(k + 1) * P], ACT.Identity,
                                         bias=shift[:, k:k + 1], scale=gain[:, k:k + 1])
                    if k == KD - 1:
                        ins.then_inc(xT_rdy, 1)
                    else:
                        my.step(ins)

            for m in range(KD):
                act.wait_ge(at_ps, m + 1)
                act.activation(ATr[:, m, :], ps[:, m, :], ACT.Copy).then_inc(at_sb, 1)
            for m in range(KD):
                act.wait_ge(m_ps, m + 1)
                act.activation(M_sb[:, m, :], ps[:, m, :], ACT.Copy, scale=1.0 / D).then_inc(m_sb, 1)

            with act.Fori(0, NT) as i:
                my.loop(i, 3 + 1)
                rsqrt(3 * i)
                xT_out(3 * i)
                act.wait_ge(x1_ps, i + 1)
                act.activation(g_sb[0:SC, :, :], ps[0:SC, 1, 0:NB * SJ * T].rearrange("p (b f) -> p b f", b=NB),
                               ACT.Gelu_apprx_tanh).then_inc(g_rdy, 1)
                rsqrt(3 * i + 1)
                xT_out(3 * i + 1)
                act.wait_ge(qkv_ps, i + 1)
                act.activation(sq, ps[:, 3:5, :].rearrange("p a (h d) -> p (a h) d", h=H), ACT.Square
                               ).then_inc(sq_rdy, 1)
                act.activation(vA, ps[:, 5, :], ACT.Copy).then_inc(vA_rdy, 1)
                act.wait_ge(ms_rdy, i + 1)
                my.step(act.activation(lnms, ms, ACT.Ln, bias=RMS_EPS, scale=1.0 / DH))
                act.activation(rs, lnms, ACT.Exp, scale=-0.5).then_inc(rs_rdy, 1)
                act.wait_ge(qkT_ps, i + 1)
                act.activation(qkT, ps[:, 6:8, :].rearrange("p a (k t) -> p a k t", k=KD), ACT.Copy
                               ).then_inc(qkT_rdy, 1)
                act.wait_ge(sA_rdy, i + 1)
                act.activation(pA, sA, ACT.Exp).then_inc(pA_rdy, 1)
                act.wait_ge(oTA_ps, i + 1)
                act.activation(oTA, ps[:, 7, :].rearrange("p (k t) -> p k t", k=KD), ACT.Copy).then_inc(oTA_rdy, 1)
                rsqrt(3 * i + 2)
                xT_out(3 * i + 2)
            my.leave(NT)

            act.wait_ge(pr_sub, 1)
            act.activation(prob, t_a, ACT.Exp).then_inc(pr_exp, 1)

            def expert(e, s):
                act.wait_ge(xeT_ps, e + 1)
                act.activation(xeT[s], ps[:, 7, 0:KD * CAP].rearrange("p (k c) -> p k c", k=KD), ACT.Copy
                               ).then_inc(xeT_rdy, 1)
                for g, (a, z) in enumerate(HGROUPS):
                    act.wait_ge(hb_rdy, 3 * e + g + 1)
                    act.activation(hT[s][:, a:z, :], hT[s][:, a:z, :], ACT.Gelu).then_inc(hT_rdy, 1)

            with act.Fori(0, E // 2) as i:
                for s in range(2):
                    expert(2 * i + s, s)

            with act.Fori(0, NT) as i:
                my.loop(i, 21)
                rsqrt(3 * i + 3 * NT)
                xT_out(4 * i + 3 * NT)
                for b in range(NB):
                    bb = NB * i + b
                    for m in range(KD):
                        act.wait_ge(k_ps, KD * bb + (m + 1))
                        act.activation(kT_c[:, m, :], ps[:, 2 + m % 2, 0:S], ACT.Identity,
                                       bias=bk_sb[:, m:m + 1], scale=1.0).then_inc(k_ev, 1)
                    for g in range(HG):
                        act.wait_ge(nmx_rdy, HG * bb + (g + 1))
                        act.activation(P_c[:, g, :], ps[:, 4 + g % 2, 0:S], ACT.Exp, bias=nmx[:, g:g + 1],
                                       scale=SCALE, accum_out=smc[:, g:g + 1]).then_inc(exp_c, 1)
                    for j in range(SJ):
                        r = SC if j < 2 else SL
                        act.wait_ge(pt_ps, SJ * bb + (j + 1))
                        act.activation(PT_c[0:r, j, :], ps[0:r, j % 2, :], ACT.Copy).then_inc(pt_ev, 1)
                rsqrt(3 * i + (3 * NT + 1))

                def group_rstd(j):
                    act.wait_ge(gv_rdy, 2 * i + (j + 1))
                    my.step(act.activation(glr, gvar, ACT.Ln, bias=LN_EPS, scale=1.0))
                    act.activation(grs, glr, ACT.Exp, scale=-0.5).then_inc(grs_rdy, 1)

                group_rstd(0)
                xT_out(4 * i + (3 * NT + 1), gng_sb, gnb_sb)
                act.wait_ge(qkv1_ps, i + 1)
                for a in range(2):
                    act.activation(t2, ps[:, 2 + a, :], ACT.Square, accum_out=ssq[:, a:a + 1]
                                   ).then_inc(ssq_rdy, 1)
                    act.wait_ge(ssq_rdy, 2 * i + (a + 1))
                act.activation(v1, ps[:, 4, :], ACT.Copy).then_inc(v1_rdy, 1)
                act.wait_ge(ssc_rdy, i + 1)
                my.step(act.activation(ssl, ssl, ACT.Ln))
                my.step(act.activation(nrm, ssl, ACT.Exp, scale=-0.5))
                my.step(act.activation(nrm, nrm, ACT.Copy, scale=float(SS_SCALE ** 0.5)))
                act.activation(qk1[:, 0, :], ps[:, 2, :], ACT.Copy, scale=nrm[:, 0:1]).then_inc(nrm_rdy, 1)
                act.wait_ge(qkT1_ps, i + 1)
                act.activation(qkT1, ps[:, 5:7, :].rearrange("p a (k t) -> p a k t", k=KD), ACT.Copy
                               ).then_inc(qkT1_rdy, 1)
                act.wait_ge(oT1_ps, i + 1)
                act.activation(oTc, ps[:, 6, :], ACT.Copy).then_inc(oT1_rdy, 1)
                group_rstd(1)
                xT_out(4 * i + (3 * NT + 2), fng_sb, fnb_sb)
                act.wait_ge(f1_ps, i + 1)
                for f in range(FT2):
                    ins = act.activation(hT2[:, f, :], ps[:, 2 + f // 4, (f % 4) * P:(f % 4 + 1) * P],
                                         ACT.Silu, bias=fb1_sb[:, f:f + 1], scale=1.0)
                    if f == FT2 - 1:
                        ins.then_inc(f1_rdy, 1)
                    else:
                        my.step(ins)
                rsqrt(3 * i + (3 * NT + 2))
                xT_out(4 * i + (3 * NT + 3))
            my.leave(NT)

        @block.vector
        def _(dve):
            my = Steps(dve, dve_step)
            TT, TS, STT = dve.tensor_tensor, dve.tensor_scalar, dve.scalar_tensor_tensor

            def bc(ap, *shape):
                return ap.broadcast_to(list(shape))

            def layer_norm(src, dst, n, done=None):
                dve.drain()
                dve.bn_stats(stats, src)
                dve.drain()
                dve.bn_aggr(mv, stats).then_inc(ln_stats, 1)
                dve.wait_ge(ln_rstd, n + 1)
                dve.wait_ge(ln_stats, n + 1)
                ins = TS(dst, src, mv[:, 0:1], rstd, ALU.subtract, ALU.mult)
                if done is None:
                    my.step(ins)
                else:
                    ins.then_inc(done, 1)

            for m in range(KD):
                dve.wait_ge(at_ps, KD + m + 1)
                dve.tensor_copy(ATi[:, m, :], ps[:, 4 + m, :]).then_inc(at_sb, 1)
            dve.wait_ge(wA_in, 16 * WA)
            cs, sn = (bc(a.unsqueeze(1), P, 2, DH) for a in (cos_sb, sin_sb))
            my.step(TT(CW, qkw_sb, cs, ALU.mult))
            my.step(TT(SW, qkws_sb, sn, ALU.mult))
            dve.wait_ge(m_ps, KD)
            my.step(dve.memset(PTb, 0.0))
            dve.wait_ge(consts_in, 16 * N_CONST)
            dve.wait_ge(x_in, 16)

            with dve.Fori(0, NT) as i:
                my.loop(i, 15)
                xt = x_sb[:, bass.ds(i, 1), :].rearrange("p a d -> p (a d)")
                layer_norm(xt, xn, 3 * i, xn_rdy)
                dve.wait_ge(g_rdy, i + 1)
                TT(hTA[0:SC], g_sb[0:SC].rearrange("p b (j t) -> p b j t", j=SJ),
                   ps[0:SC, 1, 0:NB * SJ * T].rearrange("p (b j t) -> p b j t", b=NB, j=SJ), ALU.mult
                   ).then_inc(hTA_rdy, 1)
                dve.wait_ge(gated_ps, NB * i + NB)
                TT(xt, xt, ps[:, 2, :], ALU.add)
                layer_norm(xt, xn, 3 * i + 1, xn_rdy)
                dve.wait_ge(sq_rdy, i + 1)
                dve.reduce_sum(ms, sq, AX.X).then_inc(ms_rdy, 1)
                dve.wait_ge(rs_rdy, i + 1)
                my.step(TT(qkn, ps[:, 3:5, :].rearrange("p a (h d) -> p (a h) d", h=H),
                           bc(rs.unsqueeze(2), P, 2 * H, DH), ALU.mult))
                v4 = "p (a h) d -> p a h d"
                qn4, A4, B4 = (a.rearrange(v4, a=2) for a in (qkn, ropeA, ropeB))
                my.step(TT(A4, qn4, bc(CW.unsqueeze(2), P, 2, H, DH), ALU.mult))
                hd = DH // 2
                my.step(TT(B4[:, :, :, 0:hd], qn4[:, :, :, hd:DH],
                           bc(SW[:, :, 0:hd].unsqueeze(2), P, 2, H, hd), ALU.mult))
                my.step(TT(B4[:, :, :, hd:DH], qn4[:, :, :, 0:hd],
                           bc(SW[:, :, hd:DH].unsqueeze(2), P, 2, H, hd), ALU.mult))
                TT(qkr, ropeA, ropeB, ALU.add).then_inc(qkr_rdy, 1)
                dve.wait_ge(s_ps, i + 1)
                sc = ps[:, 3:7, :].rearrange("p a (g t) -> p (a g) t", g=HG)
                for q in range(NB):
                    my.step(STT(sA[q4[q]], sc[q4[q], :, q4[q]], SCALE,
                                bc(causal_sb[q4[q]].unsqueeze(1), T, H, T), ALU.mult, ALU.add))
                my.step(dve.reduce_max(mxA, sA, AX.X))
                TT(sA, sA, bc(mxA.unsqueeze(2), P, H, T), ALU.subtract).then_inc(sA_rdy, 1)
                dve.wait_ge(pA_rdy, i + 1)
                my.step(dve.reduce_sum(sumA, pA, AX.X))
                my.step(dve.reciprocal(rsA, sumA))
                my.step(TT(pA, pA, bc(rsA.unsqueeze(2), P, H, T), ALU.mult))
                my.step(dve.transpose(pT.rearrange("p h t -> p (h t)"), pA.rearrange("p h t -> p (h t)")))
                for q in range(NB):
                    dve.tensor_copy(PTb[q4[q], :, q4[q]], pT[q4[q]]).then_inc(PTb_rdy, 1)
                dve.wait_ge(proj_ps, i + 1)
                TT(xt, xt, ps[:, 2, :], ALU.add)
                layer_norm(xt, xn, 3 * i + 2, xn_rdy)
                my.step(TS(xhat[:, bass.ds(i, 1), :].rearrange("p a d -> p (a d)"), xt, mv[:, 0:1], rstd,
                           ALU.subtract, ALU.mult))
                dve.wait_ge(gate_ps, i + 1)
                my.step(TT(lg[:, bass.ds(i, 1), :].rearrange("p a d -> p (a d)"), ps[:, 1, 0:E], gb_sb, ALU.add))
            my.leave(NT)

            step = my.step

            def over_e(v):
                return bc(v.unsqueeze(2), P, NT, E)

            iota3 = bc(iotad_sb.unsqueeze(1), P, NT, E)
            step(dve.reduce_max(rv1, lg, AX.X))
            TT(t_a, lg, over_e(rv1), ALU.subtract).then_inc(pr_sub, 1)
            dve.wait_ge(pr_exp, 1)
            step(dve.reduce_sum(rv1, prob, AX.X))
            step(dve.reciprocal(rv2, rv1))
            step(TT(prob, prob, over_e(rv2), ALU.mult))
            for k, (oh, pm) in enumerate(((oh1, pm1), (oh2, pm2))):
                step(dve.reduce_max(pm, prob, AX.X))
                step(TT(t_a, prob, over_e(pm), ALU.is_ge))
                step(TT(t_a, t_a, iota3, ALU.mult))
                step(dve.reduce_max(kk[:, k, :], t_a, AX.X))
                step(TT(oh, iota3, over_e(kk[:, k, :]), ALU.is_equal))
                if k == 0:
                    step(TS(t_b, oh, -4.0, None, ALU.mult))
                    step(TT(prob, prob, t_b, ALU.add))
            TT(t_a, oh1, oh2, ALU.add).then_inc(oh_rdy, 1)
            step(TT(rv1, pm1, pm2, ALU.add))
            step(dve.reciprocal(rv2, rv1))
            step(TT(wts[:, 0, :], pm1, rv2, ALU.mult))
            step(TT(wts[:, 1, :], pm2, rv2, ALU.mult))
            step(dve.memset(off_sb[:, 0, :], 0.0))
            dve.wait_ge(cnt_ps, 2)
            tot = ps[:, 1, 0:NT * E].rearrange("p (i e) -> p i e", e=E)
            for i in range(1, NT):
                step(TT(off_sb[:, i, :], off_sb[:, i - 1, :], tot[:, i - 1, :], ALU.add))
            step(TT(cnt, off_sb, ps[:, 0, 0:NT * E].rearrange("p (i e) -> p i e", e=E), ALU.add))
            for k, oh in enumerate((oh1, oh2)):
                step(TT(t_b, oh, cnt, ALU.mult))
                step(dve.reduce_sum(pos[:, k, :], t_b, AX.X))
            step(TS(val, pos, float(CAP), None, ALU.is_lt))
            step(TT(wts, wts, val, ALU.mult))
            step(TS(kk, kk, -float(CAP), float(E * CAP), ALU.mult, ALU.add))
            step(TS(gidx, pos, float(CAP - 1), None, ALU.min))
            step(TT(gidx, gidx, kk, ALU.add))
            step(TS(val, val, -BIGROW, BIGROW, ALU.mult, ALU.add))
            step(TT(sidx, gidx, val, ALU.add))
            dve.tensor_copy(uidx[:, 0, :, :], sidx).then_inc(idx_rdy, 1)
            dve.tensor_copy(uidx[:, 1, :, :], gidx).then_inc(idx_rdy, 1)
            dve.wait_ge(idx_rdy, 2)

            dve.wait_ge(b1_in, 16)

            def expert(e, s, i):
                for g, (a, z) in enumerate(HGROUPS):
                    dve.wait_ge(h_ps, 3 * e + g + 1)
                    TT(hT[s][:, a:z, :], ps[:, 3 * s + g, 0:(z - a) * CAP].rearrange("p (f c) -> p f c", c=CAP),
                       bc(b1_of(e)[:, a:z].unsqueeze(2), P, z - a, CAP), ALU.add).then_inc(hb_rdy, 1)
                dve.wait_ge(y_ps, e + 1)
                dve.wait_ge(b2_in[s], 16 * i + 16)
                wait(dve, y_stored[s], 16 * i)
                TT(y_sb[s][0:CAP, :], ps[0:CAP, 6, :], b2_sb[s][0:CAP, :], ALU.add).then_inc(y_rdy, 1)

            def b1_of(e):
                if isinstance(e, int):
                    return b1_sb[:, e, :]
                return b1_sb[:, bass.ds(e, 1), :].rearrange("p a f -> p (a f)")

            for s in range(2):
                expert(s, s, 0)
            with dve.Fori(1, E // 2) as i:
                for s in range(2):
                    expert(2 * i + s, s, i)

            dve.wait_ge(gathered, 16 * 2 * NT)
            for i in range(NT):
                for k in range(2):
                    step(STT(x_sb[:, i, :], yg[:, 2 * i + k, :], wts[:, k, i:i + 1], x_sb[:, i, :],
                             ALU.mult, ALU.add))
            step(dve.memset(PTd, 0.0))
            step(dve.memset(Qbd, 0.0))
            dve.wait_ge(wC_in, 16 * 21)

            def group_norm(src, i, j, n):
                step(TT(t1, src, src, ALU.mult))
                step(dve.reduce_sum(gs[:, 0:H], src.rearrange("p (g c) -> p g c", g=H), AX.X))
                dve.reduce_sum(gs[:, H:2 * H], t1.rearrange("p (g c) -> p g c", g=H), AX.X).then_inc(gs_rdy, 1)
                dve.wait_ge(gst_ps, 2 * i + (j + 1))
                step(dve.tensor_copy(gm, ps[:, 0, 0:H]))
                step(TT(g2, gm, gm, ALU.mult))
                step(TT(gvar, ps[:, 0, H:2 * H], g2, ALU.subtract))
                TS(gvar, gvar, 0.0, None, ALU.max).then_inc(gv_rdy, 1)
                step(TT(t1.rearrange("p (g c) -> p g c", g=H), src.rearrange("p (g c) -> p g c", g=H),
                        bc(gm.unsqueeze(2), P, H, DH), ALU.subtract))
                dve.wait_ge(grs_rdy, 2 * i + (j + 1))
                TT(xn.rearrange("p (g c) -> p g c", g=H), t1.rearrange("p (g c) -> p g c", g=H),
                   bc(grs.unsqueeze(2), P, H, DH), ALU.mult).then_inc(xn_rdy, 1)

            with dve.Fori(0, NT) as i:
                my.loop(i, 40)
                xt = x_sb[:, bass.ds(i, 1), :].rearrange("p a d -> p (a d)")
                layer_norm(xt, xn, 3 * i + 3 * NT, xn_rdy)
                dve.wait_ge(q_ps, i + 1)
                step(TT(qTs, ps[:, 1, :].rearrange("p (k t) -> p k t", k=KD), bc(bq_sb.unsqueeze(2), P, KD, P), ALU.add))
                for q in range(HQ):
                    dve.tensor_copy(Qbd[q4[q], :, :, q4[q]],
                                    qTs[q4[q]].rearrange("p g (b t) -> p b g t", b=NB)).then_inc(Qbd_rdy, 1)
                for b in range(NB):
                    bb = NB * i + b
                    for g in range(HG):
                        dve.wait_ge(sc_ps, HG * bb + (g + 1))
                        step(dve.reduce_max(mxc[:, g:g + 1], ps[:, 4 + g % 2, 0:S], AX.X))
                        TS(nmx[:, g:g + 1], mxc[:, g:g + 1], -SCALE, None, ALU.mult).then_inc(nmx_rdy, 1)
                    dve.wait_ge(exp_c, HG * bb + HG)
                    step(dve.reciprocal(rsc, smc))
                    for g in range(HG):
                        TS(P_c[:, g, :], P_c[:, g, :], rsc[:, g:g + 1], None, ALU.mult).then_inc(pn_rdy, 1)
                    for j in range(SJ):
                        r = SC if j < 2 else SL
                        dve.wait_ge(v_ps, SJ * bb + (j + 1))
                        TT(v_c[0:r, j, :], ps[0:r, 6 + j % 2, :], bv_sb[0:r, :], ALU.add).then_inc(v_ev, 1)
                    dve.wait_ge(pv_ps, bb + 1)
                    pv = ps[:, 1, :].rearrange("p (g t) -> p g t", g=HG)
                    o3 = oTc.rearrange("p (g t) -> p g t", g=HG)
                    for q in range(HQ):
                        dve.tensor_copy(o3[q4[q], :, q4[b]], pv[q4[q], :, q4[q]]).then_inc(oT_c, 1)
                dve.wait_ge(wo_ps, i + 1)
                step(TT(t1, ps[:, 1, :], bo_sb, ALU.add))
                TT(xt, xt, t1, ALU.add)
                layer_norm(xt, r1, 3 * i + (3 * NT + 1))
                group_norm(r1, i, 0, 0)
                dve.wait_ge(ssq_rdy, 2 * i + 2)
                TS(ssl, ssq, 1e-24, SS_SCALE, ALU.max, ALU.mult).then_inc(ssc_rdy, 1)
                dve.wait_ge(nrm_rdy, i + 1)
                TS(qk1[:, 1, :], ps[:, 3, :], nrm[:, 1:2], None, ALU.mult).then_inc(qk1_rdy, 1)
                dve.wait_ge(st_ps, i + 1)
                sc = ps[:, 2:6, :].rearrange("p a (g t) -> p (a g) t", g=HG)
                for q in range(NB):
                    STT(PTd[q4[q], :, q4[q]], sc[q4[q], :, q4[q]], SCALE, decay_sb[q4[q]], ALU.mult, ALU.mult
                        ).then_inc(PTd_rdy, 1)
                dve.wait_ge(ow_ps, i + 1)
                step(TT(t1, ps[:, 7, :], ob_sb, ALU.add))
                step(TT(x2, r1, t1, ALU.add))
                group_norm(x2, i, 1, 1)
                dve.wait_ge(f2_ps, i + 1)
                step(TT(t1, ps[:, 4, :], fb2_sb, ALU.add))
                step(TT(t1, t1, x2, ALU.add))
                TT(xt, xt, t1, ALU.add)
                layer_norm(xt, xn, 3 * i + (3 * NT + 2), xn_rdy)
                dve.wait_ge(spec_ps, i + 1)
                step(TT(t1, ps[:, 5, :], fbias_sb, ALU.add))
                TT(xt, xt, t1, ALU.add).then_inc(out_rdy, 1)
            my.leave(NT)

        @block.tensor
        def _(pe):
            def group(dst, pairs, last=None):
                for n, (lhsT, rhs) in enumerate(pairs):
                    ins = pe.matmul(dst, lhsT, rhs, start=(n == 0), stop=(n == len(pairs) - 1))
                if last is not None:
                    ins.then_inc(last, 1)

            def chunk(k):
                return slice(k * P, (k + 1) * P)

            def transposes(src, n):
                pe.wait_ge(xn_rdy, n + 1)
                for k in range(KD):
                    ins = pe.transpose(ps[:, 0, chunk(k)], src[:, chunk(k)], id_sb)
                ins.then_inc(xT_ps, 1)

            pe.wait_ge(dft_in, 16 * 5)
            for m in range(KD):
                group(ps[:, m, :], [(a[:, k, chunk(m)], f[:, k, :]) for a, f in ((Wr_sb, C_sb), (Wi_sb, S_sb))
                                    for k in range(KD)], at_ps)
            for m in range(KD):
                group(ps[:, 4 + m, :], [(a[:, k, chunk(m)], f[:, k, :]) for a, f in ((Wr_sb, S_sb), (Wi_sb, N_sb))
                                        for k in range(KD)], at_ps)
            pe.wait_ge(at_sb, 2 * KD)
            for m in range(KD):
                group(ps[:, m, :], [(a[:, k, chunk(m)], f[:, k, :]) for a, f in ((ATr, C_sb), (ATi, S_sb))
                                    for k in range(KD)], m_ps)
            pe.wait_ge(m_sb, KD)

            pe.wait_ge(consts_in, 16 * N_CONST)
            pe.wait_ge(wA_in, 16 * WA)
            with pe.Fori(0, NT) as i:
                transposes(xn, 3 * i)
                pe.wait_ge(xT_rdy, 3 * i + 1)
                for b in range(NB):
                    pe.wait_ge(ctx_in[b], 48 * i + 48)
                    for j in range(SJ):
                        at = (b * SJ + j) * T
                        group(ps[0:SC, 1, at:at + T],
                              [(ctxT_sb[:, b, k, j * SC:(j + 1) * SC], xnT[:, k, q4[b]]) for k in range(KD)],
                              x1_ps if b == NB - 1 and j == SJ - 1 else None)
                pe.wait_ge(hTA_rdy, i + 1)
                for b in range(NB):
                    group(ps[q4[b], 2, :], [(hTA[0:SC, b, j, :], ctx_sb[0:SC, b, j, :]) for j in range(SJ)], gated_ps)
                transposes(xn, 3 * i + 1)
                pe.wait_ge(xT_rdy, 3 * i + 2)
                for a in range(3):
                    group(ps[:, 3 + a, :], [(xnT[:, k, :], wqkv0_sb[:, k, a * D:(a + 1) * D]) for k in range(KD)],
                          qkv_ps if a == 2 else None)
                pe.wait_ge(qkr_rdy, i + 1)
                rot = qkr.rearrange("p h d -> p (h d)")
                for a in range(2):
                    for k in range(KD):
                        ins = pe.transpose(ps[:, 6 + a, chunk(k)], rot[:, a * D + k * P:a * D + (k + 1) * P], id_sb)
                ins.then_inc(qkT_ps, 1)
                pe.wait_ge(qkT_rdy, i + 1)
                for g in range(HG):
                    for q in range(HQ):
                        ins = pe.matmul(ps[:, 3 + q, chunk(g)], qkT[q4[q], 0, g, :], qkT[q4[q], 1, g, :],
                                        start=True, stop=True)
                ins.then_inc(s_ps, 1)
                pe.wait_ge(PTb_rdy, NB * i + NB)
                pe.wait_ge(vA_rdy, i + 1)
                for g in range(HG):
                    for q in range(HQ):
                        h = HQ * g + q
                        ins = pe.matmul(ps[q4[q], 7, chunk(g)], vA[:, h * DH:(h + 1) * DH], PTb[:, q * HG + g, :],
                                        start=True, stop=True)
                ins.then_inc(oTA_ps, 1)
                pe.wait_ge(oTA_rdy, i + 1)
                group(ps[:, 2, :], [(oTA[:, k, :], wproj0_sb[:, k, :]) for k in range(KD)], proj_ps)
                transposes(xn, 3 * i + 2)
                pe.wait_ge(xT_rdy, 3 * i + 3)
                group(ps[:, 1, 0:E], [(xnT[:, k, :], gw_sb[:, k, :]) for k in range(KD)], gate_ps)

            pe.wait_ge(oh_rdy, 1)
            ohs = t_a.rearrange("p i e -> p (i e)")
            for n, m in enumerate((tri_sb, ones_sb)):
                pe.matmul(ps[:, n, 0:NT * E], m, ohs, start=True, stop=True).then_inc(cnt_ps, 1)

            def expert(e, s, i):
                pe.wait_ge(xe_in[s], 16 * i + 16)
                for k in range(KD):
                    ins = pe.transpose(ps[:, 7, k * CAP:(k + 1) * CAP], xe_sb[s][0:CAP, chunk(k)],
                                       id_sb[0:CAP, 0:CAP])
                ins.then_inc(xeT_ps, 1)
                pe.wait_ge(xeT_rdy, e + 1)
                pe.wait_ge(w1_in[s], 16 * i + 16)
                for g, (a, z) in enumerate(HGROUPS):
                    for f in range(a, z):
                        group(ps[:, 3 * s + g, (f - a) * CAP:(f - a + 1) * CAP],
                              [(w1_sb[s][:, k, chunk(f)], xeT[s][:, k, :]) for k in range(KD)],
                              h_ps if f == z - 1 else None)
                pe.wait_ge(w2_in[s], 16 * i + 16)
                wait(pe, y_rdy, e)
                for g, (a, z) in enumerate(HGROUPS):
                    pe.wait_ge(hT_rdy, 3 * e + g + 1)
                    for f in range(a, z):
                        ins = pe.matmul(ps[0:CAP, 6, :], hT[s][:, f, :], w2_sb[s][:, f, :],
                                        start=(f == 0), stop=(f == FT - 1))
                ins.then_inc(y_ps, 1)

            for s in range(2):
                expert(s, s, 0)
            with pe.Fori(1, E // 2) as i:
                for s in range(2):
                    expert(2 * i + s, s, i)

            pe.wait_ge(wC_in, 16 * 21)
            with pe.Fori(0, NT) as i:
                transposes(xn, 4 * i + 3 * NT)
                pe.wait_ge(xT_rdy, 4 * i + (3 * NT + 1))
                for m in range(KD):
                    group(ps[:, 1, chunk(m)], [(WqT_sb[:, k, chunk(m)], xnT[:, k, :]) for k in range(KD)],
                          q_ps if m == KD - 1 else None)

                def keys(b):
                    bb = NB * i + b
                    s = b % 2
                    pe.wait_ge(ctxc_in[s], 32 * i + 16 * (b // 2 + 1))
                    for m in range(KD):
                        if m >= 2:
                            pe.wait_ge(k_ev, KD * bb + (m - 1))
                        group(ps[:, 2 + m % 2, 0:S],
                              [(WkT_sb[:, k, chunk(m)], ctxT_c[:, s, k, 0:S]) for k in range(KD)], k_ps)

                keys(0)
                pe.wait_ge(Qbd_rdy, HQ * i + HQ)
                for b in range(NB):
                    bb = NB * i + b
                    s = b % 2
                    for g in range(HG):
                        pe.wait_ge(k_ev, KD * bb + (g + 1))
                        if g >= 2:
                            pe.wait_ge(exp_c, HG * bb + (g - 1))
                        pe.matmul(ps[:, 4 + g % 2, 0:S], Qbd[:, b, g, :], kT_c[:, g, :],
                                  start=True, stop=True).then_inc(sc_ps, 1)
                    for j in range(SJ):
                        r = SC if j < 2 else SL
                        if j == 2:
                            pe.wait_ge(v_ev, SJ * bb + 1)
                        group(ps[0:r, 6 + j % 2, :],
                              [(ctxT_c[:, s, k, j * SC:j * SC + r], WvT_sb[:, k, :]) for k in range(KD)], v_ps)
                    pe.wait_ge(pn_rdy, HG * bb + HG)
                    for j in range(SJ):
                        r = SC if j < 2 else SL
                        if j == 2:
                            pe.wait_ge(pt_ev, SJ * bb + 1)
                        for g in range(HG):
                            ins = pe.transpose(ps[0:r, j % 2, chunk(g)], P_c[:, g, j * SC:j * SC + r], id_sb)
                        ins.then_inc(pt_ps, 1)
                    if b < NB - 1:
                        keys(b + 1)
                    pe.wait_ge(pt_ev, SJ * bb + SJ)
                    pe.wait_ge(v_ev, SJ * bb + SJ)
                    for g in range(HG):
                        group(ps[:, 1, chunk(g)],
                              [(v_c[0:r, j, chunk(g)], PT_c[0:r, j, chunk(g)]) for j, r in enumerate((SC, SC, SL))],
                              pv_ps if g == HG - 1 else None)
                pe.wait_ge(oT_c, NB * HQ * i + NB * HQ)
                group(ps[:, 1, :], [(oTc[:, chunk(k)], WoT_sb[:, k, :]) for k in range(KD)], wo_ps)

                def group_sums(j):
                    pe.wait_ge(gs_rdy, 2 * i + (j + 1))
                    pe.matmul(ps[:, 0, 0:2 * H], gones_sb, gs, start=True, stop=True).then_inc(gst_ps, 1)

                group_sums(0)
                transposes(xn, 4 * i + (3 * NT + 1))
                pe.wait_ge(xT_rdy, 4 * i + (3 * NT + 2))
                for a in range(3):
                    group(ps[:, 2 + a, :], [(xnT[:, k, :], wqkv1_sb[:, k, a * D:(a + 1) * D]) for k in range(KD)],
                          qkv1_ps if a == 2 else None)
                pe.wait_ge(nrm_rdy, i + 1)
                pe.wait_ge(qk1_rdy, i + 1)
                for a in range(2):
                    for k in range(KD):
                        ins = pe.transpose(ps[:, 5 + a, chunk(k)], qk1[:, a, chunk(k)], id_sb)
                ins.then_inc(qkT1_ps, 1)
                pe.wait_ge(qkT1_rdy, i + 1)
                for g in range(HG):
                    for q in range(HQ):
                        ins = pe.matmul(ps[:, 2 + q, chunk(g)], qkT1[q4[q], 1, g, :], qkT1[q4[q], 0, g, :],
                                        start=True, stop=True)
                ins.then_inc(st_ps, 1)
                pe.wait_ge(PTd_rdy, NB * i + NB)
                for g in range(HG):
                    for q in range(HQ):
                        h = HQ * g + q
                        ins = pe.matmul(ps[q4[q], 6, chunk(g)], v1[:, h * DH:(h + 1) * DH], PTd[:, q * HG + g, :],
                                        start=True, stop=True)
                ins.then_inc(oT1_ps, 1)
                pe.wait_ge(oT1_rdy, i + 1)
                group(ps[:, 7, :], [(oTc[:, chunk(k)], ow_sb[:, k, :]) for k in range(KD)], ow_ps)
                group_sums(1)
                transposes(xn, 4 * i + (3 * NT + 2))
                pe.wait_ge(xT_rdy, 4 * i + (3 * NT + 3))
                for f in range(FT2):
                    group(ps[:, 2 + f // 4, chunk(f % 4)],
                          [(fw1_sb[:, k, chunk(f)], xnT[:, k, :]) for k in range(KD)],
                          f1_ps if f == FT2 - 1 else None)
                pe.wait_ge(f1_rdy, i + 1)
                group(ps[:, 4, :], [(hT2[:, f, :], fw2_sb[:, f, :]) for f in range(FT2)], f2_ps)
                transposes(xn, 4 * i + (3 * NT + 3))
                pe.wait_ge(xT_rdy, 4 * i + (3 * NT + 4))
                group(ps[:, 5, :], [(xnT[:, k, :], M_sb[:, k, :]) for k in range(KD)], spec_ps)



def constants():
    c = {}
    n = np.arange(D)
    ang = 2.0 * np.pi * ((n[:, None] * n[None, :]) % D) / D
    c["dftC"] = np.cos(ang).astype(np.float32)
    c["dftS"] = np.sin(ang).astype(np.float32)
    c["dftN"] = -c["dftC"]
    c["ident"] = np.eye(P, dtype=np.float32)
    p = np.arange(P)
    c["tri"] = (p[:, None] < p[None, :]).astype(np.float32)
    c["ones"] = np.ones((P, P), np.float32)
    c["gones"] = ((p[:, None] // T == p[None, :] // T) / float(T * D // H)).astype(np.float32)
    t = np.arange(T)
    c["causal"] = np.tile(np.where(t[None, :] <= t[:, None], 0.0, -1e30).astype(np.float32), (NB, 1))
    c["iotad"] = np.tile((E - np.arange(E)).astype(np.float32), (P, 1))
    freqs = (np.float32(32.0) ** (-np.arange(0, DH, 2, dtype=np.float32) / DH)).astype(np.float32)
    rot = (t.astype(np.float32)[:, None] * freqs[None, :]).astype(np.float32)
    cos, sin = np.cos(rot).astype(np.float32), np.sin(rot).astype(np.float32)
    c["cosT"] = np.tile(np.concatenate([cos, cos], 1), (NB, 1))
    c["sinS"] = np.tile(np.concatenate([-sin, sin], 1), (NB, 1))
    gam = (1.0 - np.exp(np.linspace(np.log(1.0 / 32.0), np.log(1.0 / 512.0), H))).astype(np.float32)
    dec = np.zeros((T, H, T), np.float32)
    for q in range(HQ):
        for g in range(HG):
            d = t[None, :] - t[:, None]
            dec[:, q * HG + g, :] = np.where(d >= 0, gam[HQ * g + q].astype(np.float64) ** np.maximum(d, 0), 0.0)
    c["decay"] = np.tile(dec, (NB, 1, 1))
    return c


def columns(v):
    return v.reshape(-1, P).T


def kernel(**inputs):
    import concourse.bacc as _bacc
    from concourse.bass_utils import run_bass_kernel_spmd as _run

    a = {k: np.asarray(v) for k, v in inputs.items()}
    hd = DH // 2
    qkw = np.stack([a["L0_attn_q_norm_w"], a["L0_attn_k_norm_w"]])
    ctx = a["ctx_1024"]
    laid = {
        "x": a["x"].reshape(B * T, D),
        "ctx": ctx,
        "ctxT": ctx.transpose(0, 2, 1).reshape(B, KD, P, S),
        "wqkv0T": a["L0_attn_w_qkv"].T, "wproj0T": a["L0_attn_w_proj"].T,
        "qkw": qkw, "qkw_sw": np.concatenate([qkw[:, hd:], qkw[:, :hd]], 1),
        "gate_w": a["L0_ffn_gate_w"], "gate_b": a["L0_ffn_gate_b"],
        "w1": a["L0_ffn_w1"], "b1": a["L0_ffn_b1"].reshape(E, FT, P).transpose(2, 0, 1),
        "w2": a["L0_ffn_w2"], "b2": a["L0_ffn_b2"],
        "WqT": a["L1_xattn_Wq"].T, "bq": columns(a["L1_xattn_bq"]), "WkT": a["L1_xattn_Wk"].T, "bk": columns(a["L1_xattn_bk"]),
        "WvT": a["L1_xattn_Wv"].T, "bv": a["L1_xattn_bv"], "WoT": a["L1_xattn_Wo"].T, "bo": a["L1_xattn_bo"],
        "gng": columns(a["L1_attn_norm_g"]), "gnb": columns(a["L1_attn_norm_b"]),
        "wqkv1T": np.concatenate([a["L1_attn_qw"].T, a["L1_attn_kw"].T, a["L1_attn_vw"].T], 1),
        "owT": a["L1_attn_ow"].T, "ob": a["L1_attn_ob"],
        "fng": columns(a["L1_attn_ffn_norm_g"]), "fnb": columns(a["L1_attn_ffn_norm_b"]),
        "fw1T": a["L1_attn_w1"].T, "fb1": columns(a["L1_attn_b1"]), "fw2T": a["L1_attn_w2"].T, "fb2": a["L1_attn_b2"],
        "Wr": a["L1_ffn_w_freq_real"], "Wi": a["L1_ffn_w_freq_imag"], "fbias": a["L1_ffn_bias"],
        **constants(),
    }
    nc = _bacc.Bacc("TRN2", target_bir_lowering=False, num_devices=1)
    arrays, aps = {}, {}
    for name, v in laid.items():
        v = np.ascontiguousarray(v)
        arrays[f"in_{name}"] = v
        aps[name] = nc.dram_tensor(f"in_{name}", v.shape, mybir.dt.from_np(v.dtype), kind="ExternalInput").ap()
    aps["out"] = nc.dram_tensor("out_0", (B * T, D), fp32, kind="ExternalOutput").ap()
    aps["xe_dram"] = nc.dram_tensor("xe_rows", (E * CAP, D), fp32).ap()
    aps["y_dram"] = nc.dram_tensor("y_rows", (E * CAP, D), fp32).ap()
    perceiver_kernel(nc, **aps)
    r = _run(nc, [arrays], core_ids=[0])
    return np.asarray(r.results[0]["out_0"]).reshape(B, T, D)
```

```python
import numpy as np
from contextlib import ExitStack

import concourse.bass as bass
from concourse import mybir

B, T, D = 32, 32, 512
S = 257
P = 128
NT = B * T // P
NB = P // T
H, DH = 16, 32
HG, HQ = 4, 4
KD = D // P
SC = 86
SJ = 3
SL = S - 2 * SC
E, F = 32, 2048
CAP = 77
CAPP = 96
FT = F // P
F2 = 2 * D
FT2 = F2 // P
BIGROW = 4096.0
LN_EPS, RMS_EPS, GN_EPS = 1e-5, 1e-6, 1e-5

fp32 = mybir.dt.float32
u32 = mybir.dt.uint32
ALU = mybir.AluOpType
ACT = mybir.ActivationFunctionType
AX = mybir.AxisListType


class Steps:

    def __init__(self, eng, sem):
        self.eng, self.sem, self.base, self.per, self.i, self.k = eng, sem, 0, 0, None, 0

    def loop(self, i, per, first):
        self.base += self.k - first * per
        self.i, self.per, self.k = i, per, 0

    def leave(self, end):
        assert self.k == self.per, f"the loop's turn has {self.k} steps, not {self.per}"
        self.base += end * self.per
        self.i, self.k = None, 0

    def step(self, ins):
        ins.then_inc(self.sem, 1)
        self.k += 1
        at = self.base + self.k
        self.eng.wait_ge(self.sem, at if self.i is None else self.i * self.per + at)


def weave(main, side, after):
    left = list(after)
    for n, _ in enumerate(main):
        while left and left[0] == n:
            left.pop(0)
            next(side, None)
    assert not left, left
    for _ in side:
        raise AssertionError("a piece is left")


def run(stage):
    for _ in stage:
        pass


def perceiver_kernel(nc, x, ctx, ctxT, wqkv0T, wproj0T, qkw, qkw_sw, cosT, sinS, gate_w, gate_b,
                     w1, b1, w2, b2, WqT, bq, WkT, bk, WvT, bv, WoT, bo,
                     gng, gnb, wqkv1T, owT, ob, fng, fnb, fw1T, fb1, fw2T, fb2,
                     Wr, Wi, fbias, dftC, dftS, dftN, ident, tri, ones, gones, causal,
                     decay, iotad, out, xe_dram, y_dram):
    with ExitStack() as st:
        def sem(name):
            return st.enter_context(nc.semaphore(name))

        WORDS = 53160
        arena = st.enter_context(nc.sbuf_tensor("arena", [P, WORDS], fp32))
        ps = st.enter_context(nc.psum_tensor("ps", [P, 8, 512], fp32))
        uidx = st.enter_context(nc.sbuf_tensor("uidx", [P, 2, 2, NT], u32))

        def view(off, *dims):
            n = int(np.prod(dims))
            assert off + n <= WORDS, (off, dims)
            a = arena[:, off:off + n]
            if len(dims) == 2:
                a = a.rearrange("p (a b) -> p a b", a=dims[0])
            if len(dims) == 3:
                a = a.rearrange("p (a b c) -> p a b c", a=dims[0], b=dims[1])
            if len(dims) == 4:
                a = a.rearrange("p (a b c d) -> p a b c d", a=dims[0], b=dims[1], c=dims[2])
            return a

        class Region:
            def __init__(self, off, size):
                self.at, self.end = off, off + size

            def take(self, *dims):
                n = int(np.prod(dims))
                assert self.at + n <= self.end, (dims, self.at + n - self.end)
                self.at += n
                return view(self.at - n, *dims)

        keep = Region(0, WORDS)
        x_sb = keep.take(NT, D)
        xhat = keep.take(NT, D)
        M_sb = keep.take(KD, D)
        id_sb, tri_sb, ones_sb, gones_sb = (keep.take(P) for _ in range(4))
        causal_sb, iotad_sb = keep.take(T), keep.take(E)
        gw_sb, gb_sb = keep.take(KD, E), keep.take(E)
        lg = keep.take(NT, E)
        wts = keep.take(2, NT)
        b1_sb = keep.take(E, FT)
        mv, stats, rstd, veps = keep.take(2), keep.take(6), keep.take(1), keep.take(1)
        half_sb = keep.take(2 * H)
        xn, xnT = keep.take(D), keep.take(KD, P)
        RW = KD * F
        ring_off = [[keep.at + (2 * a + b) * RW for b in range(2)] for a in range(2)]
        w1_sb = [view(ring_off[s][0], KD, F) for s in range(2)]
        w2_sb = [view(ring_off[s][1], FT, D) for s in range(2)]
        work_off = keep.at + 4 * RW
        work_size = WORDS - work_off

        rM = Region(ring_off[0][0], 2 * RW)
        C_sb, S_sb, N_sb, Wr_sb, Wi_sb, ATr, ATi = (rM.take(KD, D) for _ in range(7))

        rA = Region(ring_off[1][0], RW)
        wqkv0_sb, wproj0_sb = rA.take(KD, 3 * D), rA.take(KD, D)
        rA = Region(ring_off[1][1], RW)
        ctx_sb = rA.take(NB, SJ, D)
        CW, SW = rA.take(2, DH), rA.take(2, DH)
        cos_sb, sin_sb, qkw_sb, qkws_sb = rA.take(DH), rA.take(DH), rA.take(2, DH), rA.take(2, DH)
        W = Region(work_off, work_size)
        ctxT_sb = W.take(NB, KD, SC * SJ)
        rA = Region(ring_off[0][0], 2 * RW)
        g_sb, hTA = rA.take(NB, SJ * T), rA.take(NB, SJ, T)
        qkn, ropeA, ropeB, qkr, sq = (rA.take(2 * H, DH) for _ in range(5))
        ms, rs = rA.take(2 * H), rA.take(2 * H)
        xn0, xnT0 = rA.take(D), rA.take(KD, P)
        qkT = rA.take(2, KD, P)
        vA = rA.take(D)
        sA, pA, pT = rA.take(H, T), rA.take(H, T), rA.take(H, T)
        mxA, sumA, rsA = rA.take(H), rA.take(H), rA.take(H)
        PTb = rA.take(H, P)
        oTA = rA.take(KD, P)

        W = Region(work_off, work_size)
        prob, t_a, t_b, oh1, oh2, cnt = (W.take(NT, E) for _ in range(6))
        off_sb = W.take(NT, E)
        pm1, pm2, rv1, rv2, rv3 = (W.take(NT) for _ in range(5))
        kk, pos, val, gidx, sidx = (W.take(2, NT) for _ in range(5))

        W = Region(work_off, work_size)
        hT = [W.take(FT, CAP) for _ in range(2)]
        xeT = [W.take(KD, CAPP) for _ in range(2)]
        y_sb = [W.take(D) for _ in range(2)]
        b2_sb = [W.take(D) for _ in range(2)]
        xe_sb = [W.take(D) for _ in range(2)]
        zeros = view(ring_off[1][0], 4, D)
        yg = view(ring_off[1][1], 2 * NT, D)

        rC = Region(ring_off[0][0], RW)
        WkT_sb, WvT_sb, WqT_sb, WoT_sb = (rC.take(KD, D) for _ in range(4))
        rC = Region(ring_off[0][1], RW)
        wqkv1_sb, ow_sb = rC.take(KD, 3 * D), rC.take(KD, D)
        rC = Region(ring_off[1][0], RW)
        fw1_sb, fw2_sb = rC.take(KD, F2), rC.take(FT2, D)
        W = Region(work_off, work_size)
        ctxT_c = W.take(2, KD, SC * SJ)
        PTd = W.take(H, P)
        bv_sb, bo_sb, ob_sb, fb2_sb, fbias_sb = (W.take(D) for _ in range(5))
        decay_sb = W.take(H, T)
        bq_sb, bk_sb, gng_sb, gnb_sb, fng_sb, fnb_sb = (W.take(KD) for _ in range(6))
        fb1_sb = W.take(FT2)
        gs, gvar = W.take(2 * H), W.take(H)
        gm, g2, grs = (W.take(H) for _ in range(3))
        ssq, nrm = W.take(2), W.take(2)
        rC = Region(ring_off[1][1], RW)
        Qbd = rC.take(NB, HG, P)
        v_c, P_c, PT_c, kT_c = rC.take(SJ, D), rC.take(HG, S), rC.take(SJ, HG * P), rC.take(KD, S)
        mxc, nmx, smc, rsc = (rC.take(HG) for _ in range(4))
        oTc = rC.take(D)
        rC = Region(NT * D, NT * D)
        r1, t1, x2 = (rC.take(D) for _ in range(3))
        qTs = t1.rearrange("p (k t) -> p k t", k=KD)
        qk1 = rC.take(2, D)
        hT2 = qk1.rearrange("p a (f t) -> p (a f) t", t=P)
        qkT1, v1 = rC.take(2, KD, P), rC.take(D)
        oT1 = v1

        consts_in, x_in, dft_in, wA_in, wC_in, b1_in = (sem(n) for n in (
            "consts_in", "x_in", "dft_in", "wA_in", "wC_in", "b1_in"))
        pads_zero, zeros_set, xe_zeroed, half_set = (sem(n) for n in ("pads_zero", "zeros_set", "xe_zeroed", "half_set"))
        dve_step, act_step = sem("dve_step"), sem("act_step")
        at_ps, at_sb, m_ps, m_sb = sem("at_ps"), sem("at_sb"), sem("m_ps"), sem("m_sb")
        ln_stats, ln_rstd, xn_rdy, xT_ps, xT_rdy = ([sem(f"{n}{a}") for a in range(2)] for n in (
            "ln_stats", "ln_rstd", "xn_rdy", "xT_ps", "xT_rdy"))
        ctx_in = [sem(f"ctx_in{b}") for b in range(NB)]
        x1_ps, g_rdy, hTA_rdy, gated_ps = sem("x1_ps"), sem("g_rdy"), sem("hTA_rdy"), sem("gated_ps")
        qkv_ps, sq_rdy, vA_rdy, ms_rdy, rs_rdy, qkr_rdy = (sem(n) for n in (
            "qkv_ps", "sq_rdy", "vA_rdy", "ms_rdy", "rs_rdy", "qkr_rdy"))
        qkT_ps, qkT_rdy, s_ps, sA_rdy, pA_rdy, PTb_rdy, oTA_ps, oTA_rdy, proj_ps, gate_ps = (sem(n) for n in (
            "qkT_ps", "qkT_rdy", "s_ps", "sA_rdy", "pA_rdy", "PTb_rdy", "oTA_ps", "oTA_rdy", "proj_ps", "gate_ps"))
        pr_sub, pr_exp, oh_rdy, cnt_ps, idx_rdy, scattered = (sem(n) for n in (
            "pr_sub", "pr_exp", "oh_rdy", "cnt_ps", "idx_rdy", "scattered"))
        w1_in, w2_in, b2_in, xe_in, y_stored = ([sem(f"{n}{s}") for s in range(2)] for n in (
            "w1_in", "w2_in", "b2_in", "xe_in", "y_stored"))
        xeT_ps, xeT_rdy, h_ps, hb_rdy, hT_rdy, y_ps, y_rdy = (sem(n) for n in (
            "xeT_ps", "xeT_rdy", "h_ps", "hb_rdy", "hT_rdy", "y_ps", "y_rdy"))
        gathered, moe_added = sem("gathered"), sem("moe_added")
        ctxc_in = [sem(f"ctxc_in{s}") for s in range(2)]
        q_ps, Qbd_rdy, k_ps, k_ev, sc_ps, nmx_rdy, exp_c, pn_rdy, v_ps, v_ev, pt_ps, pt_ev, pv_ps, oT_c = (
            sem(n) for n in ("q_ps", "Qbd_rdy", "k_ps", "k_ev", "sc_ps", "nmx_rdy", "exp_c", "pn_rdy",
                             "v_ps", "v_ev", "pt_ps", "pt_ev", "pv_ps", "oT_c"))
        wo_ps, gs_rdy, gst_ps, gv_rdy, grs_rdy = (sem(n) for n in (
            "wo_ps", "gs_rdy", "gst_ps", "gv_rdy", "grs_rdy"))
        qkv1_ps, ssq_rdy, ssc_rdy, nrm_rdy, v1_rdy, q1_rdy, k1_rdy, qkT1_ps, qkT1_rdy, st_ps, PTd_rdy = (
            sem(n) for n in ("qkv1_ps", "ssq_rdy", "ssc_rdy", "nrm_rdy", "v1_rdy", "q1_rdy", "k1_rdy",
                             "qkT1_ps", "qkT1_rdy", "st_ps", "PTd_rdy"))
        oT1_ps, oT1_rdy, ow_ps, f1_ps, f1_rdy, f2_ps, spec_ps, out_rdy, stored = (sem(n) for n in (
            "oT1_ps", "oT1_rdy", "ow_ps", "f1_ps", "f1_rdy", "f2_ps", "spec_ps", "out_rdy", "stored"))

        SCALE = DH ** -0.5
        N_CONST = 8
        WA, WC = 6, 20
        q4 = [slice(32 * q, 32 * q + 32) for q in range(4)]
        HB = 4
        NHB = FT // HB

        PLAN_A = [0, 1, 2, 3, 4]
        PLAN_C = [0, 2, 4, 5, 8, 10, 11, 13, 15, 17, 19, 20, 21, 23, 25, 26, 27, 29]
        N_TAIL = 15

        def bS(g): return g
        def bV(j): return (4, 0, 1)[j]
        def bT(j): return (2, 3, 4)[j]
        def bK(m): return m
        bPV = 4

        def rows(ap):
            return ap.rearrange("(k p) n -> p k n", p=P)

        def wait(eng, s, value):
            if not (isinstance(value, int) and value <= 0):
                eng.wait_ge(s, value)

        def chain(*stages):
            for stage in stages:
                yield from stage

        def phase_c(eng, head, cross, tail, my, per, keys0=None):
            run(head(0))
            if keys0 is not None:
                keys0()
            weave(cross(0, True), head(1), PLAN_C[N_TAIL:])
            with eng.Fori(1, NT - 1) as i:
                if my is not None:
                    my.loop(i, per, 1)
                weave(cross(i, True), chain(tail(i - 1), head(i + 1)), PLAN_C)
            if my is not None:
                my.leave(NT - 1)
            weave(cross(NT - 1, False), tail(NT - 2), PLAN_C[:N_TAIL])
            run(tail(NT - 1))

        block = st.enter_context(nc.Block())

        @block.sync
        def _(sp):
            for dst, src in ((C_sb, dftC), (Wr_sb, Wr), (S_sb, dftS), (Wi_sb, Wi), (N_sb, dftN)):
                sp.dma_start(dst, rows(src)).then_inc(dft_in, 16)
            for dst, src in ((id_sb, ident), (tri_sb, tri), (ones_sb, ones), (gones_sb, gones),
                             (causal_sb, causal), (iotad_sb, iotad), (gw_sb, rows(gate_w)),
                             (gb_sb, gate_b.partition_broadcast(P))):
                sp.dma_start(dst, src).then_inc(consts_in, 16)
            sp.dma_start(x_sb, x.rearrange("(i p) d -> p i d", p=P)).then_inc(x_in, 16)
            sp.wait_ge(zeros_set, 1)
            for e in range(0, E, 4):
                sp.dma_start(xe_dram[e * CAP:(e + 4) * CAP, :].rearrange("(e c) d -> c e d", c=CAP),
                             zeros[0:CAP, :, :]).then_inc(xe_zeroed, 16)
            sp.wait_ge(xe_zeroed, 16 * (E // 4))
            sp.dma_start(wqkv0_sb, rows(wqkv0T)).then_inc(wA_in, 16)
            sp.dma_start(wproj0_sb, rows(wproj0T)).then_inc(wA_in, 16)
            for dst, src in ((cos_sb, cosT), (sin_sb, sinS), (qkw_sb, qkw.partition_broadcast(P)),
                             (qkws_sb, qkw_sw.partition_broadcast(P))):
                sp.dma_start(dst, src).then_inc(wA_in, 16)
            sp.dma_start(b1_sb, b1).then_inc(b1_in, 16)
            sp.wait_ge(pads_zero, 2)

            def load_ctx(i, b):
                sp.dma_start(ctxT_sb[:, b, :, 0:S],
                             ctxT[NB * i + b].rearrange("k p s -> p k s")).then_inc(ctx_in[b], 16)
                sp.dma_start(ctx_sb[0:SC, b, 0:2, :],
                             ctx[NB * i + b, 0:2 * SC, :].rearrange("(j p) d -> p j d", p=SC)
                             ).then_inc(ctx_in[b], 16)
                sp.dma_start(ctx_sb[0:SL, b, 2, :], ctx[NB * i + b, 2 * SC:S, :]).then_inc(ctx_in[b], 16)

            for b in range(NB):
                load_ctx(0, b)
            with sp.Fori(1, NT) as i:
                for b in range(NB):
                    sp.wait_ge(gated_ps, NB * i + (b - NB + 1))
                    load_ctx(i, b)

            def load_expert(e, s, i):
                def after(sm, value):
                    wait(sp, sm, value)
                after(h_ps, NHB * (e - 1))
                sp.dma_start(w1_sb[s], rows(w1[e])).then_inc(w1_in[s], 16)
                after(y_ps, e - 1)
                sp.dma_start(w2_sb[s], rows(w2[e])).then_inc(w2_in[s], 16)

            def load_rows(e, s):
                wait(sp, xeT_ps, e - 1)
                sp.dma_start(xe_sb[s][0:CAP, :], xe_dram[bass.ts(e, CAP), :]).then_inc(xe_in[s], 16)
                wait(sp, y_rdy, e - 1)
                sp.dma_start(b2_sb[s][0:CAP, :],
                             b2[bass.ts(e, 1), :].rearrange("a d -> (a d)").partition_broadcast(CAP)
                             ).then_inc(b2_in[s], 16)

            sp.wait_ge(gate_ps, NT)
            for s in range(2):
                load_expert(s, s, 0)
            sp.wait_ge(scattered, 16 * 2 * NT)
            for s in range(2):
                load_rows(s, s)
            with sp.Fori(1, E // 2) as i:
                for s in range(2):
                    load_expert(2 * i + s, s, i)
                    load_rows(2 * i + s, s)

            sp.wait_ge(h_ps, NHB * E)
            sp.wait_ge(y_ps, E)
            for s in range(2):
                sp.wait_ge(y_stored[s], 16 * (E // 2))
            for dst, src in ((WkT_sb, rows(WkT)), (WvT_sb, rows(WvT)), (WqT_sb, rows(WqT)),
                             (bq_sb, bq), (bk_sb, bk), (bv_sb, bv.partition_broadcast(P)),
                             (WoT_sb, rows(WoT)), (bo_sb, bo.partition_broadcast(P)),
                             (wqkv1_sb, rows(wqkv1T)), (gng_sb, gng), (gnb_sb, gnb),
                             (decay_sb, decay), (ow_sb, rows(owT)), (ob_sb, ob.partition_broadcast(P)),
                             (fng_sb, fng), (fnb_sb, fnb), (fb1_sb, fb1),
                             (fw1_sb, rows(fw1T)), (fw2_sb, rows(fw2T)),
                             (fb2_sb, fb2.partition_broadcast(P)),
                             (fbias_sb, fbias.partition_broadcast(P))):
                sp.dma_start(dst, src).then_inc(wC_in, 16)

            def load_ctxc(bb, s):
                sp.dma_start(ctxT_c[:, s, :, 0:S], ctxT[bb].rearrange("k p s -> p k s")).then_inc(ctxc_in[s], 16)

            for s in range(2):
                load_ctxc(s, s)
            def tile_c(i, more):
                for b in range(2, NB):
                    sp.wait_ge(v_ps, SJ * (NB * i + (b - 1)))
                    load_ctxc(NB * i + b, b % 2)
                if more:
                    for b in range(2):
                        sp.wait_ge(v_ps, SJ * (NB * i + (b + 3)))
                        load_ctxc(NB * i + (NB + b), b)

            def store(i):
                sp.wait_ge(out_rdy, i + 1)
                sp.dma_start(out[bass.ts(i, P), :], x_sb[:, bass.ds(i, 1), :].rearrange("p a d -> p (a d)")
                             ).then_inc(stored, 16)

            tile_c(0, True)
            with sp.Fori(1, NT - 1) as i:
                tile_c(i, True)
                store(i - 1)
            tile_c(NT - 1, False)
            store(NT - 2)
            store(NT - 1)
            sp.wait_ge(stored, 16 * NT)

        @block.gpsimd
        def _(pool):
            pool.memset(zeros, 0.0).then_inc(zeros_set, 1)
            pool.memset(ctx_sb, 0.0).then_inc(pads_zero, 1)
            pool.memset(ctxT_sb, 0.0).then_inc(pads_zero, 1)
            pool.memset(half_sb, -0.5).then_inc(half_set, 1)
            pool.wait_ge(half_set, 1)

            def root(src, dst, ready, value, done):
                pool.wait_ge(ready, value)
                pool.tensor_tensor(dst, src, half_sb[:, 0:src.shape[-1]], ALU.pow).then_inc(done, 1)

            def norm_root(a, n):
                root(veps, rstd, ln_stats[a], n + 1, ln_rstd[a])

            def gated(i):
                norm_root(0, i)
                yield
                for _ in range(4):
                    yield

            def attention(i):
                norm_root(1, 2 * i)
                yield
                yield
                root(ms, rs, ms_rdy, i + 1, rs_rdy)
                yield
                for _ in range(3):
                    yield
                norm_root(1, 2 * i + 1)
                yield
                yield
                yield

            run(gated(0))
            with pool.Fori(1, NT) as i:
                weave(attention(i - 1), gated(i), PLAN_A)
            run(attention(NT - 1))

            pool.wait_ge(idx_rdy, 2)
            for i in range(NT):
                for k in range(2):
                    pool.indirect_dma_start(
                        out=xe_dram, out_offset=bass.IndirectOffsetOnAxis(ap=uidx[:, 0, k, i:i + 1], axis=0),
                        in_=xhat[:, i, :], in_offset=None, bounds_check=E * CAP - 1, oob_is_err=False
                    ).then_inc(scattered, 16)

            def store_y(e, s):
                pool.wait_ge(y_rdy, e + 1)
                pool.dma_start(y_dram[bass.ts(e, CAP), :], y_sb[s][0:CAP, :]).then_inc(y_stored[s], 16)

            with pool.Fori(0, E // 2) as i:
                for s in range(2):
                    store_y(2 * i + s, s)
            for s in range(2):
                pool.wait_ge(y_stored[s], 16 * (E // 2))
            for i in range(NT):
                for k in range(2):
                    pool.indirect_dma_start(
                        out=yg[:, 2 * i + k, :], out_offset=None, in_=y_dram,
                        in_offset=bass.IndirectOffsetOnAxis(ap=uidx[:, 1, k, i:i + 1], axis=0)
                    ).then_inc(gathered, 16)

            def head(i):
                norm_root(0, NT + i)
                yield
                yield
                yield

            def cross(i, more):
                for _ in range(8 * NB):
                    yield

            def tail(i):
                norm_root(1, 2 * i + 2 * NT)
                yield
                root(gvar, grs, gv_rdy, 2 * i + 1, grs_rdy)
                yield
                yield
                root(ssq, nrm, ssc_rdy, i + 1, nrm_rdy)
                yield
                for _ in range(5):
                    yield
                root(gvar, grs, gv_rdy, 2 * i + 2, grs_rdy)
                yield
                yield
                yield
                norm_root(1, 2 * i + (2 * NT + 1))
                yield
                yield
                yield

            phase_c(pool, head, cross, tail, None, None)

        @block.scalar
        def _(act):
            my = Steps(act, act_step)

            def xT_out(a, n, bank, gain=None, shift=None, dst=xnT):
                act.wait_ge(xT_ps[a], n + 1)
                if gain is None:
                    act.activation(dst, ps[:, bank, :].rearrange("p (k t) -> p k t", k=KD), ACT.Copy
                                   ).then_inc(xT_rdy[a], 1)
                    return
                for k in range(KD):
                    ins = act.activation(dst[:, k, :], ps[:, bank, k * P:(k + 1) * P], ACT.Identity,
                                         bias=shift[:, k:k + 1], scale=gain[:, k:k + 1])
                    if k == KD - 1:
                        ins.then_inc(xT_rdy[a], 1)
                    else:
                        my.step(ins)

            for m in range(KD):
                act.wait_ge(at_ps, m + 1)
                act.activation(ATr[:, m, :], ps[:, m, :], ACT.Copy).then_inc(at_sb, 1)
            for m in range(KD):
                act.wait_ge(m_ps, m + 1)
                act.activation(M_sb[:, m, :], ps[:, m, :], ACT.Copy, scale=1.0 / D).then_inc(m_sb, 1)

            def gated(i):
                yield
                xT_out(0, i, 0, dst=xnT0)
                yield
                act.wait_ge(x1_ps, i + 1)
                act.activation(g_sb[0:SC, :, :], ps[0:SC, 1, 0:NB * SJ * T].rearrange("p (b f) -> p b f", b=NB),
                               ACT.Gelu_apprx_tanh).then_inc(g_rdy, 1)
                yield
                yield
                yield

            def attention(i):
                yield
                xT_out(1, 2 * i, 3)
                yield
                act.wait_ge(qkv_ps, i + 1)
                act.activation(sq, ps[:, 4:6, :].rearrange("p a (h d) -> p (a h) d", h=H), ACT.Square
                               ).then_inc(sq_rdy, 1)
                act.activation(vA, ps[:, 6, :], ACT.Copy).then_inc(vA_rdy, 1)
                yield
                act.wait_ge(qkT_ps, 2 * i + 1)
                act.activation(qkT[:, 0], ps[:, 3, :].rearrange("p (k t) -> p k t", k=KD), ACT.Copy
                               ).then_inc(qkT_rdy, 1)
                act.wait_ge(qkT_ps, 2 * i + 2)
                act.activation(qkT[:, 1], ps[:, 7, :].rearrange("p (k t) -> p k t", k=KD), ACT.Copy
                               ).then_inc(qkT_rdy, 1)
                yield
                act.wait_ge(sA_rdy, i + 1)
                act.activation(pA, sA, ACT.Exp).then_inc(pA_rdy, 1)
                yield
                act.wait_ge(oTA_ps, i + 1)
                act.activation(oTA, ps[:, 7, :].rearrange("p (k t) -> p k t", k=KD), ACT.Copy).then_inc(oTA_rdy, 1)
                yield
                yield
                xT_out(1, 2 * i + 1, 4)
                yield
                yield

            run(gated(0))
            with act.Fori(1, NT) as i:
                weave(attention(i - 1), gated(i), PLAN_A)
            run(attention(NT - 1))

            act.wait_ge(pr_sub, 1)
            act.activation(prob, t_a, ACT.Exp).then_inc(pr_exp, 1)

            act.wait_ge(pads_zero, 3)

            def rows_out(e, s):
                act.wait_ge(xeT_ps, e + 1)
                act.activation(xeT[s][:, :, 0:CAP], ps[:, 6 + s, 0:KD * CAP].rearrange("p (k c) -> p k c", k=KD),
                               ACT.Copy).then_inc(xeT_rdy, 1)

            def hidden_out(e, s):
                for g in range(NHB):
                    act.wait_ge(hb_rdy, NHB * e + (g + 1))
                    hg = hT[s][:, g * HB:(g + 1) * HB, :]
                    act.activation(hg, hg, ACT.Gelu).then_inc(hT_rdy, 1)

            rows_out(0, 0)
            with act.Fori(0, E // 2 - 1) as i:
                for s in range(2):
                    hidden_out(2 * i + s, s)
                    rows_out(2 * i + (s + 1), 1 - s)
            hidden_out(E - 2, 0)
            rows_out(E - 1, 1)
            hidden_out(E - 1, 1)

            def head(i):
                yield
                xT_out(0, NT + i, 5)
                yield
                yield

            def keys_out(bb):
                for m in range(KD):
                    act.wait_ge(k_ps, KD * bb + (m + 1))
                    act.activation(kT_c[:, m, :], ps[:, bK(m), 0:S], ACT.Identity,
                                   bias=bk_sb[:, m:m + 1], scale=1.0).then_inc(k_ev, 1)
                    if m == 1:
                        yield

            def cross(i, more):
                for b in range(NB):
                    bb = NB * i + b
                    for g in range(HG):
                        act.wait_ge(nmx_rdy, HG * bb + (g + 1))
                        act.activation(P_c[:, g, :], ps[:, bS(g), 0:S], ACT.Exp, bias=nmx[:, g:g + 1],
                                       scale=SCALE, accum_out=smc[:, g:g + 1]).then_inc(exp_c, 1)
                    yield
                    yield
                    yield
                    yield
                    for j in range(SJ):
                        r = SC if j < 2 else SL
                        act.wait_ge(pt_ps, SJ * bb + (j + 1))
                        act.activation(PT_c[0:r, j, :], ps[0:r, bT(j), :], ACT.Copy).then_inc(pt_ev, 1)
                    yield
                    if b < NB - 1 or more:
                        yield from keys_out(bb + 1)
                    else:
                        yield
                    yield
                    yield

            def tail(i):
                yield
                yield
                xT_out(1, 3 * i + 2 * NT, 5, gng_sb, gnb_sb)
                yield
                act.wait_ge(qkv1_ps, i + 1)
                for a in range(2):
                    act.activation(qk1[:, a, :], ps[:, 6 + a, :], ACT.Square, accum_out=ssq[:, a:a + 1]
                                   ).then_inc(ssq_rdy, 1)
                act.activation(v1, ps[:, 5, :], ACT.Copy).then_inc(v1_rdy, 1)
                act.wait_ge(nrm_rdy, i + 1)
                act.activation(qk1[:, 0, :], ps[:, 6, :], ACT.Copy, scale=nrm[:, 0:1]).then_inc(q1_rdy, 1)
                yield
                act.wait_ge(qkT1_ps, i + 1)
                act.activation(qkT1, ps[:, 6:8, :].rearrange("p a (k t) -> p a k t", k=KD), ACT.Copy
                               ).then_inc(qkT1_rdy, 1)
                yield
                yield
                yield
                act.wait_ge(oT1_ps, i + 1)
                act.activation(oT1, ps[:, 7, :], ACT.Copy).then_inc(oT1_rdy, 1)
                yield
                yield
                yield
                xT_out(1, 3 * i + (2 * NT + 1), 7, fng_sb, fnb_sb)
                yield
                act.wait_ge(f1_ps, i + 1)
                for f in range(FT2):
                    ins = act.activation(hT2[:, f, :], ps[:, 5 + f // 4, (f % 4) * P:(f % 4 + 1) * P],
                                         ACT.Silu, bias=fb1_sb[:, f:f + 1], scale=1.0)
                    if f == FT2 - 1:
                        ins.then_inc(f1_rdy, 1)
                    else:
                        my.step(ins)
                yield
                yield
                xT_out(1, 3 * i + (2 * NT + 2), 5)
                yield
                yield

            phase_c(act, head, cross, tail, my, 13, lambda: run(keys_out(0)))

        @block.vector
        def _(dve):
            my = Steps(dve, dve_step)
            TT, TS, STT = dve.tensor_tensor, dve.tensor_scalar, dve.scalar_tensor_tensor

            def bc(ap, *shape):
                return ap.broadcast_to(list(shape))

            def layer_norm(a, src, dst, n, done=None):
                dve.drain()
                dve.bn_stats(stats, src)
                dve.drain()
                my.step(dve.bn_aggr(mv, stats))
                TS(veps, mv[:, 1:2], LN_EPS, None, ALU.add).then_inc(ln_stats[a], 1)
                dve.wait_ge(ln_rstd[a], n + 1)
                ins = TS(dst, src, mv[:, 0:1], rstd, ALU.subtract, ALU.mult)
                if done is None:
                    my.step(ins)
                else:
                    ins.then_inc(done, 1)

            for m in range(KD):
                dve.wait_ge(at_ps, KD + m + 1)
                dve.tensor_copy(ATi[:, m, :], ps[:, 4 + m, :]).then_inc(at_sb, 1)
            dve.wait_ge(wA_in, 16 * WA)
            cs, sn = (bc(a.unsqueeze(1), P, 2, DH) for a in (cos_sb, sin_sb))
            my.step(TT(CW, qkw_sb, cs, ALU.mult))
            my.step(TT(SW, qkws_sb, sn, ALU.mult))
            dve.wait_ge(m_ps, KD)
            my.step(dve.memset(PTb, 0.0))
            dve.wait_ge(consts_in, 16 * N_CONST)
            dve.wait_ge(x_in, 16)

            def tile_of(a, i):
                if isinstance(i, int):
                    return a[:, i, :]
                return a[:, bass.ds(i, 1), :].rearrange("p a d -> p (a d)")

            def gated(i):
                xt = tile_of(x_sb, i)
                layer_norm(0, xt, xn0, i, xn_rdy[0])
                yield
                yield
                dve.wait_ge(g_rdy, i + 1)
                TT(hTA[0:SC], g_sb[0:SC].rearrange("p b (j t) -> p b j t", j=SJ),
                   ps[0:SC, 1, 0:NB * SJ * T].rearrange("p (b j t) -> p b j t", b=NB, j=SJ), ALU.mult
                   ).then_inc(hTA_rdy, 1)
                yield
                yield
                dve.wait_ge(gated_ps, NB * i + NB)
                my.step(TT(xt, xt, ps[:, 2, :], ALU.add))
                yield

            def attention(i):
                xt = tile_of(x_sb, i)
                layer_norm(1, xt, xn, 2 * i, xn_rdy[1])
                yield
                yield
                dve.wait_ge(sq_rdy, i + 1)
                my.step(dve.reduce_sum(ms, sq, AX.X))
                TS(ms, ms, 1.0 / DH, RMS_EPS, ALU.mult, ALU.add).then_inc(ms_rdy, 1)
                dve.wait_ge(rs_rdy, i + 1)
                my.step(TT(qkn, ps[:, 4:6, :].rearrange("p a (h d) -> p (a h) d", h=H),
                           bc(rs.unsqueeze(2), P, 2 * H, DH), ALU.mult))
                v4 = "p (a h) d -> p a h d"
                qn4, A4, B4 = (a.rearrange(v4, a=2) for a in (qkn, ropeA, ropeB))
                my.step(TT(A4, qn4, bc(CW.unsqueeze(2), P, 2, H, DH), ALU.mult))
                hd = DH // 2
                my.step(TT(B4[:, :, :, 0:hd], qn4[:, :, :, hd:DH],
                           bc(SW[:, :, 0:hd].unsqueeze(2), P, 2, H, hd), ALU.mult))
                my.step(TT(B4[:, :, :, hd:DH], qn4[:, :, :, 0:hd],
                           bc(SW[:, :, hd:DH].unsqueeze(2), P, 2, H, hd), ALU.mult))
                TT(qkr, ropeA, ropeB, ALU.add).then_inc(qkr_rdy, 1)
                yield
                yield
                dve.wait_ge(s_ps, i + 1)
                sc = ps[:, 3:7, :].rearrange("p a (g t) -> p (a g) t", g=HG)
                for q in range(NB):
                    my.step(STT(sA[q4[q]], sc[q4[q], :, q4[q]], SCALE,
                                bc(causal_sb[q4[q]].unsqueeze(1), T, H, T), ALU.mult, ALU.add))
                my.step(dve.reduce_max(mxA, sA, AX.X))
                TT(sA, sA, bc(mxA.unsqueeze(2), P, H, T), ALU.subtract).then_inc(sA_rdy, 1)
                dve.wait_ge(pA_rdy, i + 1)
                my.step(dve.reduce_sum(sumA, pA, AX.X))
                my.step(dve.reciprocal(rsA, sumA))
                my.step(TT(pA, pA, bc(rsA.unsqueeze(2), P, H, T), ALU.mult))
                my.step(dve.transpose(pT.rearrange("p h t -> p (h t)"), pA.rearrange("p h t -> p (h t)")))
                for q in range(NB):
                    dve.tensor_copy(PTb[q4[q], :, q4[q]], pT[q4[q]]).then_inc(PTb_rdy, 1)
                yield
                yield
                dve.wait_ge(proj_ps, i + 1)
                TT(xt, xt, ps[:, 3, :], ALU.add)
                layer_norm(1, xt, xn, 2 * i + 1, xn_rdy[1])
                my.step(TS(tile_of(xhat, i), xt, mv[:, 0:1], rstd, ALU.subtract, ALU.mult))
                yield
                yield
                dve.wait_ge(gate_ps, i + 1)
                my.step(TT(tile_of(lg, i), ps[:, 5, 0:E], gb_sb, ALU.add))
                yield

            run(gated(0))
            with dve.Fori(1, NT) as i:
                my.loop(i, 20, 1)
                weave(attention(i - 1), gated(i), PLAN_A)
            my.leave(NT)
            run(attention(NT - 1))

            step = my.step

            def over_e(v):
                return bc(v.unsqueeze(2), P, NT, E)

            iota3 = bc(iotad_sb.unsqueeze(1), P, NT, E)
            step(dve.reduce_max(rv1, lg, AX.X))
            TT(t_a, lg, over_e(rv1), ALU.subtract).then_inc(pr_sub, 1)
            dve.wait_ge(pr_exp, 1)
            step(dve.reduce_sum(rv1, prob, AX.X))
            step(dve.reciprocal(rv2, rv1))
            step(TT(prob, prob, over_e(rv2), ALU.mult))
            for k, (oh, pm) in enumerate(((oh1, pm1), (oh2, pm2))):
                step(dve.reduce_max(pm, prob, AX.X))
                step(TT(t_a, prob, over_e(pm), ALU.is_ge))
                step(TT(t_a, t_a, iota3, ALU.mult))
                step(dve.reduce_max(kk[:, k, :], t_a, AX.X))
                step(TT(oh, iota3, over_e(kk[:, k, :]), ALU.is_equal))
                if k == 0:
                    step(TS(t_b, oh, -4.0, None, ALU.mult))
                    step(TT(prob, prob, t_b, ALU.add))
            TT(t_a, oh1, oh2, ALU.add).then_inc(oh_rdy, 1)
            step(TT(rv1, pm1, pm2, ALU.add))
            step(dve.reciprocal(rv2, rv1))
            step(TT(wts[:, 0, :], pm1, rv2, ALU.mult))
            step(TT(wts[:, 1, :], pm2, rv2, ALU.mult))
            step(dve.memset(off_sb[:, 0, :], 0.0))
            for s in range(2):
                ins = dve.memset(xeT[s], 0.0)
            ins.then_inc(pads_zero, 1)
            dve.wait_ge(cnt_ps, 2)
            tot = ps[:, 1, 0:NT * E].rearrange("p (i e) -> p i e", e=E)
            for i in range(1, NT):
                step(TT(off_sb[:, i, :], off_sb[:, i - 1, :], tot[:, i - 1, :], ALU.add))
            step(TT(cnt, off_sb, ps[:, 0, 0:NT * E].rearrange("p (i e) -> p i e", e=E), ALU.add))
            for k, oh in enumerate((oh1, oh2)):
                step(TT(t_b, oh, cnt, ALU.mult))
                step(dve.reduce_sum(pos[:, k, :], t_b, AX.X))
            step(TS(val, pos, float(CAP), None, ALU.is_lt))
            step(TT(wts, wts, val, ALU.mult))
            step(TS(kk, kk, -float(CAP), float(E * CAP), ALU.mult, ALU.add))
            step(TS(gidx, pos, float(CAP - 1), None, ALU.min))
            step(TT(gidx, gidx, kk, ALU.add))
            step(TS(val, val, -BIGROW, BIGROW, ALU.mult, ALU.add))
            step(TT(sidx, gidx, val, ALU.add))
            dve.tensor_copy(uidx[:, 0, :, :], sidx).then_inc(idx_rdy, 1)
            dve.tensor_copy(uidx[:, 1, :, :], gidx).then_inc(idx_rdy, 1)
            dve.wait_ge(idx_rdy, 2)

            dve.wait_ge(b1_in, 16)

            def expert(e, s, i):
                for g in range(NHB):
                    dve.wait_ge(h_ps, NHB * e + (g + 1))
                    fs = slice(g * HB, (g + 1) * HB)
                    TT(hT[s][:, fs, :], ps[:, g, 0:HB * CAPP].rearrange("p (f c) -> p f c", c=CAPP)[:, :, 0:CAP],
                       bc(tile_of(b1_sb, e)[:, fs].unsqueeze(2), P, HB, CAP), ALU.add).then_inc(hb_rdy, 1)
                dve.wait_ge(b2_in[s], 16 * i + 16)
                dve.wait_ge(y_ps, e + 1)
                wait(dve, y_stored[s], 16 * i)
                TT(y_sb[s][0:CAP, :], ps[0:CAP, 4 + s, :], b2_sb[s][0:CAP, :], ALU.add).then_inc(y_rdy, 1)

            for s in range(2):
                expert(s, s, 0)
            with dve.Fori(1, E // 2) as i:
                for s in range(2):
                    expert(2 * i + s, s, i)

            dve.wait_ge(gathered, 16 * 2 * NT)
            for i in range(NT):
                for k in range(2):
                    step(STT(x_sb[:, i, :], yg[:, 2 * i + k, :], wts[:, k, i:i + 1], x_sb[:, i, :],
                             ALU.mult, ALU.add))
            step(dve.memset(PTd, 0.0))
            step(dve.memset(Qbd, 0.0))
            dve.wait_ge(wC_in, 16 * 21)

            def group_sums(src):
                step(TT(t1, src, src, ALU.mult))
                step(dve.reduce_sum(gs[:, 0:H], src.rearrange("p (g c) -> p g c", g=H), AX.X))
                dve.reduce_sum(gs[:, H:2 * H], t1.rearrange("p (g c) -> p g c", g=H), AX.X).then_inc(gs_rdy, 1)

            def group_norm(src, n, bank):
                dve.wait_ge(gst_ps, n + 1)
                step(dve.tensor_copy(gm, ps[:, bank, 0:H]))
                step(TT(g2, gm, gm, ALU.mult))
                step(TT(gvar, ps[:, bank, H:2 * H], g2, ALU.subtract))
                TS(gvar, gvar, 0.0, GN_EPS, ALU.max, ALU.add).then_inc(gv_rdy, 1)
                step(TT(t1.rearrange("p (g c) -> p g c", g=H), src.rearrange("p (g c) -> p g c", g=H),
                        bc(gm.unsqueeze(2), P, H, DH), ALU.subtract))
                dve.wait_ge(grs_rdy, n + 1)
                TT(xn.rearrange("p (g c) -> p g c", g=H), t1.rearrange("p (g c) -> p g c", g=H),
                   bc(grs.unsqueeze(2), P, H, DH), ALU.mult).then_inc(xn_rdy[1], 1)

            def head(i):
                layer_norm(0, tile_of(x_sb, i), xn, NT + i, xn_rdy[0])
                yield
                yield
                dve.wait_ge(q_ps, i + 1)
                step(TT(qTs, ps[:, 7, :].rearrange("p (k t) -> p k t", k=KD), bc(bq_sb.unsqueeze(2), P, KD, P), ALU.add))
                for q in range(HQ):
                    dve.tensor_copy(Qbd[q4[q], :, :, q4[q]],
                                    qTs[q4[q]].rearrange("p g (b t) -> p b g t", b=NB)).then_inc(Qbd_rdy, 1)
                yield

            def cross(i, more):
                for b in range(NB):
                    bb = NB * i + b
                    for g in range(HG):
                        dve.wait_ge(sc_ps, HG * bb + (g + 1))
                        step(dve.reduce_max(mxc[:, g:g + 1], ps[:, bS(g), 0:S], AX.X))
                        TS(nmx[:, g:g + 1], mxc[:, g:g + 1], -SCALE, None, ALU.mult).then_inc(nmx_rdy, 1)
                    yield
                    dve.wait_ge(exp_c, HG * bb + HG)
                    step(dve.reciprocal(rsc, smc))
                    for g in range(HG):
                        TS(P_c[:, g, :], P_c[:, g, :], rsc[:, g:g + 1], None, ALU.mult).then_inc(pn_rdy, 1)
                    for j in range(SJ):
                        r = SC if j < 2 else SL
                        dve.wait_ge(v_ps, SJ * bb + (j + 1))
                        TT(v_c[0:r, j, :], ps[0:r, bV(j), :], bv_sb[0:r, :], ALU.add).then_inc(v_ev, 1)
                        yield
                    yield
                    yield
                    yield
                    dve.wait_ge(pv_ps, bb + 1)
                    pv = ps[:, bPV, :].rearrange("p (g t) -> p g t", g=HG)
                    o3 = oTc.rearrange("p (g t) -> p g t", g=HG)
                    for q in range(HQ):
                        dve.tensor_copy(o3[q4[q], :, q4[b]], pv[q4[q], :, q4[q]]).then_inc(oT_c, 1)
                    yield

            def decayed(i, a):
                dve.wait_ge(st_ps, 2 * i + (a + 1))
                sc = ps[:, 5:7, :].rearrange("p a (g t) -> p (a g) t", g=HG)
                h2 = slice(2 * HG * a, 2 * HG * (a + 1))
                for q in range(NB):
                    STT(PTd[q4[q], h2, q4[q]], sc[q4[q], :, q4[q]], SCALE, decay_sb[q4[q], h2, :],
                        ALU.mult, ALU.mult).then_inc(PTd_rdy, 1)

            def tail(i):
                xt = tile_of(x_sb, i)
                dve.wait_ge(wo_ps, i + 1)
                step(TT(t1, ps[:, 6, :], bo_sb, ALU.add))
                TT(xt, xt, t1, ALU.add)
                layer_norm(1, xt, r1, 2 * i + 2 * NT)
                group_sums(r1)
                yield
                group_norm(r1, 2 * i, 7)
                yield
                yield
                dve.wait_ge(ssq_rdy, 2 * i + 2)
                TS(ssq, ssq, 1e-24, None, ALU.max).then_inc(ssc_rdy, 1)
                dve.wait_ge(nrm_rdy, i + 1)
                TS(qk1[:, 1, :], ps[:, 7, :], nrm[:, 1:2], None, ALU.mult).then_inc(k1_rdy, 1)
                yield
                yield
                decayed(i, 0)
                yield
                decayed(i, 1)
                yield
                yield
                dve.wait_ge(ow_ps, i + 1)
                step(TT(t1, ps[:, 5, :], ob_sb, ALU.add))
                step(TT(x2, r1, t1, ALU.add))
                group_sums(x2)
                yield
                group_norm(x2, 2 * i + 1, 6)
                yield
                yield
                yield
                dve.wait_ge(f2_ps, i + 1)
                step(TT(t1, ps[:, 7, :], fb2_sb, ALU.add))
                step(TT(t1, t1, x2, ALU.add))
                TT(xt, xt, t1, ALU.add)
                layer_norm(1, xt, xn, 2 * i + (2 * NT + 1), xn_rdy[1])
                yield
                yield
                dve.wait_ge(spec_ps, i + 1)
                step(TT(t1, ps[:, 6, :], fbias_sb, ALU.add))
                TT(xt, xt, t1, ALU.add).then_inc(out_rdy, 1)
                yield

            phase_c(dve, head, cross, tail, my, 43)

        @block.tensor
        def _(pe):
            def group(dst, pairs, last=None):
                for n, (lhsT, rhs) in enumerate(pairs):
                    ins = pe.matmul(dst, lhsT, rhs, start=(n == 0), stop=(n == len(pairs) - 1))
                if last is not None:
                    ins.then_inc(last, 1)

            def chunk(k):
                return slice(k * P, (k + 1) * P)

            def transposes(a, src, n, bank):
                pe.wait_ge(xn_rdy[a], n + 1)
                for k in range(KD):
                    ins = pe.transpose(ps[:, bank, chunk(k)], src[:, chunk(k)], id_sb)
                ins.then_inc(xT_ps[a], 1)

            pe.wait_ge(dft_in, 16 * 5)
            for m in range(KD):
                group(ps[:, m, :], [(a[:, k, chunk(m)], f[:, k, :]) for a, f in ((Wr_sb, C_sb), (Wi_sb, S_sb))
                                    for k in range(KD)], at_ps)
            for m in range(KD):
                group(ps[:, 4 + m, :], [(a[:, k, chunk(m)], f[:, k, :]) for a, f in ((Wr_sb, S_sb), (Wi_sb, N_sb))
                                        for k in range(KD)], at_ps)
            pe.wait_ge(at_sb, 2 * KD)
            for m in range(KD):
                group(ps[:, m, :], [(a[:, k, chunk(m)], f[:, k, :]) for a, f in ((ATr, C_sb), (ATi, S_sb))
                                    for k in range(KD)], m_ps)
            pe.wait_ge(m_sb, KD)

            pe.wait_ge(consts_in, 16 * N_CONST)
            pe.wait_ge(wA_in, 16 * WA)

            def gated(i):
                yield
                transposes(0, xn0, i, 0)
                yield
                pe.wait_ge(xT_rdy[0], i + 1)
                for b in range(NB):
                    pe.wait_ge(ctx_in[b], 48 * i + 48)
                    for j in range(SJ):
                        at = (b * SJ + j) * T
                        group(ps[0:SC, 1, at:at + T],
                              [(ctxT_sb[:, b, k, j * SC:(j + 1) * SC], xnT0[:, k, q4[b]]) for k in range(KD)],
                              x1_ps if b == NB - 1 and j == SJ - 1 else None)
                yield
                pe.wait_ge(hTA_rdy, i + 1)
                for b in range(NB):
                    group(ps[q4[b], 2, :], [(hTA[0:SC, b, j, :], ctx_sb[0:SC, b, j, :]) for j in range(SJ)], gated_ps)
                    if b == 1:
                        yield
                yield

            def attention(i):
                yield
                transposes(1, xn, 2 * i, 3)
                yield
                pe.wait_ge(xT_rdy[1], 2 * i + 1)
                for a in range(3):
                    group(ps[:, 4 + a, :], [(xnT[:, k, :], wqkv0_sb[:, k, a * D:(a + 1) * D]) for k in range(KD)],
                          qkv_ps if a == 2 else None)
                yield
                pe.wait_ge(qkr_rdy, i + 1)
                rot = qkr.rearrange("p h d -> p (h d)")
                for a in range(2):
                    for k in range(KD):
                        ins = pe.transpose(ps[:, (3, 7)[a], chunk(k)], rot[:, a * D + k * P:a * D + (k + 1) * P], id_sb)
                    ins.then_inc(qkT_ps, 1)
                yield
                pe.wait_ge(qkT_rdy, 2 * i + 2)
                for g in range(HG):
                    for q in range(HQ):
                        ins = pe.matmul(ps[:, 3 + q, chunk(g)], qkT[q4[q], 0, g, :], qkT[q4[q], 1, g, :],
                                        start=True, stop=True)
                ins.then_inc(s_ps, 1)
                yield
                pe.wait_ge(PTb_rdy, NB * i + NB)
                pe.wait_ge(vA_rdy, i + 1)
                for g in range(HG):
                    for q in range(HQ):
                        h = HQ * g + q
                        ins = pe.matmul(ps[q4[q], 7, chunk(g)], vA[:, h * DH:(h + 1) * DH], PTb[:, q * HG + g, :],
                                        start=True, stop=True)
                ins.then_inc(oTA_ps, 1)
                yield
                pe.wait_ge(oTA_rdy, i + 1)
                group(ps[:, 3, :], [(oTA[:, k, :], wproj0_sb[:, k, :]) for k in range(KD)], proj_ps)
                yield
                transposes(1, xn, 2 * i + 1, 4)
                yield
                pe.wait_ge(xT_rdy[1], 2 * i + 2)
                group(ps[:, 5, 0:E], [(xnT[:, k, :], gw_sb[:, k, :]) for k in range(KD)], gate_ps)
                yield

            run(gated(0))
            with pe.Fori(1, NT) as i:
                weave(attention(i - 1), gated(i), PLAN_A)
            run(attention(NT - 1))

            pe.wait_ge(oh_rdy, 1)
            ohs = t_a.rearrange("p i e -> p (i e)")
            for n, m in enumerate((tri_sb, ones_sb)):
                pe.matmul(ps[:, n, 0:NT * E], m, ohs, start=True, stop=True).then_inc(cnt_ps, 1)

            def rows_in(e, s, i):
                pe.wait_ge(xe_in[s], 16 * i + 16)
                for k in range(KD):
                    ins = pe.transpose(ps[:, 6 + s, k * CAP:(k + 1) * CAP], xe_sb[s][0:CAP, chunk(k)],
                                       id_sb[0:CAP, 0:CAP])
                ins.then_inc(xeT_ps, 1)

            def hidden(e, s, i):
                pe.wait_ge(xeT_rdy, e + 1)
                pe.wait_ge(w1_in[s], 16 * i + 16)
                for f in range(FT):
                    g, c = f // HB, f % HB
                    group(ps[:, g, c * CAPP:(c + 1) * CAPP],
                          [(w1_sb[s][:, k, chunk(f)], xeT[s][:, k, :]) for k in range(KD)],
                          h_ps if c == HB - 1 else None)

            def result(e, s, i):
                pe.wait_ge(w2_in[s], 16 * i + 16)
                wait(pe, y_rdy, e - 1)
                for f in range(FT):
                    if f % HB == 0:
                        pe.wait_ge(hT_rdy, NHB * e + (f // HB + 1))
                    ins = pe.matmul(ps[0:CAP, 4 + s, :], hT[s][:, f, :], w2_sb[s][:, f, :],
                                    start=(f == 0), stop=(f == FT - 1))
                ins.then_inc(y_ps, 1)

            def pair(i, last=False):
                for s in range(2):
                    hidden(2 * i + s, s, i)
                    if s == 0:
                        rows_in(2 * i + 1, 1, i)
                    elif not last:
                        rows_in(2 * i + 2, 0, i + 1)
                    result(2 * i + s, s, i)

            rows_in(0, 0, 0)
            pair(0)
            with pe.Fori(1, E // 2 - 1) as i:
                pair(i)
            pair(E // 2 - 1, True)

            pe.wait_ge(wC_in, 16 * 21)

            def head(i):
                yield
                transposes(0, xn, NT + i, 5)
                yield
                pe.wait_ge(xT_rdy[0], NT + i + 1)
                for m in range(KD):
                    group(ps[:, 7, chunk(m)], [(WqT_sb[:, k, chunk(m)], xnT[:, k, :]) for k in range(KD)],
                          q_ps if m == KD - 1 else None)
                yield

            def keys(i, b, before):
                bb = NB * i + b
                pe.wait_ge(ctxc_in[b % 2], 32 * i + 16 * (b // 2 + 1))
                for m in range(KD):
                    if before is not None:
                        pe.wait_ge((v_ev, v_ev, pt_ev, pt_ev)[m], SJ * before + (2, 3, 1, 2)[m])
                    group(ps[:, bK(m), 0:S],
                          [(WkT_sb[:, k, chunk(m)], ctxT_c[:, b % 2, k, 0:S]) for k in range(KD)], k_ps)
                    if m == 1:
                        yield

            def cross(i, more):
                pe.wait_ge(Qbd_rdy, HQ * i + HQ)
                for b in range(NB):
                    bb = NB * i + b
                    s = b % 2
                    for g in range(HG):
                        pe.wait_ge(k_ev, KD * bb + (g + 1))
                        pe.matmul(ps[:, bS(g), 0:S], Qbd[:, b, g, :], kT_c[:, g, :],
                                  start=True, stop=True).then_inc(sc_ps, 1)
                    yield
                    for j in range(SJ):
                        r = SC if j < 2 else SL
                        if j == 0:
                            wait(pe, oT_c, HQ * bb)
                        else:
                            pe.wait_ge(exp_c, HG * bb + j)
                        group(ps[0:r, bV(j), :],
                              [(ctxT_c[:, s, k, j * SC:j * SC + r], WvT_sb[:, k, :]) for k in range(KD)], v_ps)
                        yield
                    pe.wait_ge(pn_rdy, HG * bb + HG)
                    for j in range(SJ):
                        r = SC if j < 2 else SL
                        if j == 2:
                            pe.wait_ge(v_ev, SJ * bb + 1)
                        for g in range(HG):
                            ins = pe.transpose(ps[0:r, bT(j), chunk(g)], P_c[:, g, j * SC:j * SC + r], id_sb)
                        ins.then_inc(pt_ps, 1)
                    yield
                    if b < NB - 1:
                        yield from keys(i, b + 1, bb)
                    elif more:
                        yield from keys(i + 1, 0, bb)
                    else:
                        yield
                    yield
                    pe.wait_ge(pt_ev, SJ * bb + SJ)
                    pe.wait_ge(v_ev, SJ * bb + SJ)
                    for g in range(HG):
                        group(ps[:, bPV, chunk(g)],
                              [(v_c[0:r, j, chunk(g)], PT_c[0:r, j, chunk(g)]) for j, r in enumerate((SC, SC, SL))],
                              pv_ps if g == HG - 1 else None)
                    yield

            def group_sums(n, bank):
                pe.wait_ge(gs_rdy, n + 1)
                pe.matmul(ps[:, bank, 0:2 * H], gones_sb, gs, start=True, stop=True).then_inc(gst_ps, 1)

            def tail(i):
                pe.wait_ge(oT_c, NB * HQ * i + NB * HQ)
                group(ps[:, 6, :], [(oTc[:, chunk(k)], WoT_sb[:, k, :]) for k in range(KD)], wo_ps)
                yield
                group_sums(2 * i, 7)
                yield
                transposes(1, xn, 3 * i + 2 * NT, 5)
                yield
                pe.wait_ge(xT_rdy[1], 3 * i + (2 * NT + 1))
                for a in range(3):
                    group(ps[:, (6, 7, 5)[a], :],
                          [(xnT[:, k, :], wqkv1_sb[:, k, a * D:(a + 1) * D]) for k in range(KD)],
                          qkv1_ps if a == 2 else None)
                yield
                pe.wait_ge(q1_rdy, i + 1)
                pe.wait_ge(k1_rdy, i + 1)
                for a in range(2):
                    for k in range(KD):
                        ins = pe.transpose(ps[:, 6 + a, chunk(k)], qk1[:, a, chunk(k)], id_sb)
                ins.then_inc(qkT1_ps, 1)
                yield
                pe.wait_ge(qkT1_rdy, i + 1)
                for a in range(2):
                    if a:
                        pe.wait_ge(PTd_rdy, 2 * NB * i + NB)
                    for g in range(HG):
                        for q in range(2 * a, 2 * a + 2):
                            ins = pe.matmul(ps[:, 5 + q % 2, chunk(g)], qkT1[q4[q], 1, g, :], qkT1[q4[q], 0, g, :],
                                            start=True, stop=True)
                    ins.then_inc(st_ps, 1)
                    yield
                pe.wait_ge(PTd_rdy, 2 * NB * i + 2 * NB)
                for g in range(HG):
                    for q in range(HQ):
                        h = HQ * g + q
                        ins = pe.matmul(ps[q4[q], 7, chunk(g)], v1[:, h * DH:(h + 1) * DH], PTd[:, q * HG + g, :],
                                        start=True, stop=True)
                ins.then_inc(oT1_ps, 1)
                yield
                pe.wait_ge(oT1_rdy, i + 1)
                group(ps[:, 5, :], [(oT1[:, chunk(k)], ow_sb[:, k, :]) for k in range(KD)], ow_ps)
                yield
                group_sums(2 * i + 1, 6)
                yield
                transposes(1, xn, 3 * i + (2 * NT + 1), 7)
                yield
                pe.wait_ge(xT_rdy[1], 3 * i + (2 * NT + 2))
                for f in range(FT2):
                    group(ps[:, 5 + f // 4, chunk(f % 4)],
                          [(fw1_sb[:, k, chunk(f)], xnT[:, k, :]) for k in range(KD)],
                          f1_ps if f == FT2 - 1 else None)
                yield
                pe.wait_ge(f1_rdy, i + 1)
                group(ps[:, 7, :], [(hT2[:, f, :], fw2_sb[:, f, :]) for f in range(FT2)], f2_ps)
                yield
                transposes(1, xn, 3 * i + (2 * NT + 2), 5)
                yield
                pe.wait_ge(xT_rdy[1], 3 * i + (2 * NT + 3))
                group(ps[:, 6, :], [(xnT[:, k, :], M_sb[:, k, :]) for k in range(KD)], spec_ps)
                yield

            phase_c(pe, head, cross, tail, None, None, lambda: run(keys(0, 0, None)))



def constants():
    c = {}
    n = np.arange(D)
    ang = 2.0 * np.pi * ((n[:, None] * n[None, :]) % D) / D
    c["dftC"] = np.cos(ang).astype(np.float32)
    c["dftS"] = np.sin(ang).astype(np.float32)
    c["dftN"] = -c["dftC"]
    c["ident"] = np.eye(P, dtype=np.float32)
    p = np.arange(P)
    c["tri"] = (p[:, None] < p[None, :]).astype(np.float32)
    c["ones"] = np.ones((P, P), np.float32)
    c["gones"] = ((p[:, None] // T == p[None, :] // T) / float(T * D // H)).astype(np.float32)
    t = np.arange(T)
    c["causal"] = np.tile(np.where(t[None, :] <= t[:, None], 0.0, -1e30).astype(np.float32), (NB, 1))
    c["iotad"] = np.tile((E - np.arange(E)).astype(np.float32), (P, 1))
    freqs = (np.float32(32.0) ** (-np.arange(0, DH, 2, dtype=np.float32) / DH)).astype(np.float32)
    rot = (t.astype(np.float32)[:, None] * freqs[None, :]).astype(np.float32)
    cos, sin = np.cos(rot).astype(np.float32), np.sin(rot).astype(np.float32)
    c["cosT"] = np.tile(np.concatenate([cos, cos], 1), (NB, 1))
    c["sinS"] = np.tile(np.concatenate([-sin, sin], 1), (NB, 1))
    gam = (1.0 - np.exp(np.linspace(np.log(1.0 / 32.0), np.log(1.0 / 512.0), H))).astype(np.float32)
    dec = np.zeros((T, H, T), np.float32)
    for q in range(HQ):
        for g in range(HG):
            d = t[None, :] - t[:, None]
            dec[:, q * HG + g, :] = np.where(d >= 0, gam[HQ * g + q].astype(np.float64) ** np.maximum(d, 0), 0.0)
    c["decay"] = np.tile(dec, (NB, 1, 1))
    return c


def columns(v):
    return v.reshape(-1, P).T


def kernel(**inputs):
    import concourse.bacc as _bacc
    from concourse.bass_utils import run_bass_kernel_spmd as _run

    a = {k: np.asarray(v) for k, v in inputs.items()}
    hd = DH // 2
    qkw = np.stack([a["L0_attn_q_norm_w"], a["L0_attn_k_norm_w"]])
    ctx = a["ctx_1024"]
    laid = {
        "x": a["x"].reshape(B * T, D),
        "ctx": ctx,
        "ctxT": ctx.transpose(0, 2, 1).reshape(B, KD, P, S),
        "wqkv0T": a["L0_attn_w_qkv"].T, "wproj0T": a["L0_attn_w_proj"].T,
        "qkw": qkw, "qkw_sw": np.concatenate([qkw[:, hd:], qkw[:, :hd]], 1),
        "gate_w": a["L0_ffn_gate_w"], "gate_b": a["L0_ffn_gate_b"],
        "w1": a["L0_ffn_w1"], "b1": a["L0_ffn_b1"].reshape(E, FT, P).transpose(2, 0, 1),
        "w2": a["L0_ffn_w2"], "b2": a["L0_ffn_b2"],
        "WqT": a["L1_xattn_Wq"].T, "bq": columns(a["L1_xattn_bq"]), "WkT": a["L1_xattn_Wk"].T, "bk": columns(a["L1_xattn_bk"]),
        "WvT": a["L1_xattn_Wv"].T, "bv": a["L1_xattn_bv"], "WoT": a["L1_xattn_Wo"].T, "bo": a["L1_xattn_bo"],
        "gng": columns(a["L1_attn_norm_g"]), "gnb": columns(a["L1_attn_norm_b"]),
        "wqkv1T": np.concatenate([a["L1_attn_qw"].T, a["L1_attn_kw"].T, a["L1_attn_vw"].T], 1),
        "owT": a["L1_attn_ow"].T, "ob": a["L1_attn_ob"],
        "fng": columns(a["L1_attn_ffn_norm_g"]), "fnb": columns(a["L1_attn_ffn_norm_b"]),
        "fw1T": a["L1_attn_w1"].T, "fb1": columns(a["L1_attn_b1"]), "fw2T": a["L1_attn_w2"].T, "fb2": a["L1_attn_b2"],
        "Wr": a["L1_ffn_w_freq_real"], "Wi": a["L1_ffn_w_freq_imag"], "fbias": a["L1_ffn_bias"],
        **constants(),
    }
    nc = _bacc.Bacc("TRN2", target_bir_lowering=False, num_devices=1)
    arrays, aps = {}, {}
    for name, v in laid.items():
        v = np.ascontiguousarray(v)
        arrays[f"in_{name}"] = v
        aps[name] = nc.dram_tensor(f"in_{name}", v.shape, mybir.dt.from_np(v.dtype), kind="ExternalInput").ap()
    aps["out"] = nc.dram_tensor("out_0", (B * T, D), fp32, kind="ExternalOutput").ap()
    aps["xe_dram"] = nc.dram_tensor("xe_rows", (E * CAP, D), fp32).ap()
    aps["y_dram"] = nc.dram_tensor("y_rows", (E * CAP, D), fp32).ap()
    perceiver_kernel(nc, **aps)
    r = _run(nc, [arrays], core_ids=[0])
    return np.asarray(r.results[0]["out_0"]).reshape(B, T, D)
```

```python
import numpy as np
from contextlib import ExitStack

import concourse.bass as bass
from concourse import mybir

B, T, D = 32, 32, 512
S = 257
P = 128
NT = B * T // P
HD = D // 2 + 1
NB = P // T
H, DH = 16, 32
HG, HQ = 4, 4
KD = D // P
SC = 86
SJ = 3
SL = S - 2 * SC
E, F = 32, 2048
CAP = 77
CAPP = 96
FT = F // P
F2 = 2 * D
FT2 = F2 // P
BIGROW = 4096.0
LN_EPS, RMS_EPS, GN_EPS = 1e-5, 1e-6, 1e-5

fp32 = mybir.dt.float32
u32 = mybir.dt.uint32
ALU = mybir.AluOpType
ACT = mybir.ActivationFunctionType
AX = mybir.AxisListType


class Steps:

    def __init__(self, eng, sem):
        self.eng, self.sem, self.base, self.per, self.i, self.k = eng, sem, 0, 0, None, 0

    def loop(self, i, per, first):
        self.base += self.k - first * per
        self.i, self.per, self.k = i, per, 0

    def leave(self, end):
        assert self.k == self.per, f"the loop's turn has {self.k} steps, not {self.per}"
        self.base += end * self.per
        self.i, self.k = None, 0

    def step(self, ins):
        ins.then_inc(self.sem, 1)
        self.k += 1
        at = self.base + self.k
        self.eng.wait_ge(self.sem, at if self.i is None else self.i * self.per + at)


def weave(main, side, after):
    left = list(after)
    for n, _ in enumerate(main):
        while left and left[0] == n:
            left.pop(0)
            next(side, None)
    assert not left, left
    for _ in side:
        raise AssertionError("a piece is left")


def run(stage):
    for _ in stage:
        pass


def interleave(order, **stages):
    for key in order:
        if key in stages:
            next(stages[key], None)
    for key, stage in stages.items():
        for _ in stage:
            raise AssertionError(f"a piece of {key} is left")


def perceiver_kernel(nc, x, ctx, ctxT, wqkv0T, wproj0T, qkw, qkw_sw, cosT, sinS, gate_w, gate_b,
                     w1, b1, w2, b2, WqT, bq, WkT, bk, WvT, bv, WoT, bo,
                     gng, gnb, wqkv1T, owT, ob, fng, fnb, fw1T, fb1, fw2T, fb2,
                     Wr, Wi, fbias, dftC, dftS, ident, tri, ones, gones, causal,
                     decay, iotad, out, xe_dram, y_dram):
    with ExitStack() as st:
        def sem(name):
            return st.enter_context(nc.semaphore(name))

        WORDS = 53160
        arena = st.enter_context(nc.sbuf_tensor("arena", [P, WORDS], fp32))
        ps = st.enter_context(nc.psum_tensor("ps", [P, 8, 512], fp32))
        uidx = st.enter_context(nc.sbuf_tensor("uidx", [P, 2, 2, NT], u32))

        def view(off, *dims):
            n = int(np.prod(dims))
            assert off + n <= WORDS, (off, dims)
            a = arena[:, off:off + n]
            if len(dims) == 2:
                a = a.rearrange("p (a b) -> p a b", a=dims[0])
            if len(dims) == 3:
                a = a.rearrange("p (a b c) -> p a b c", a=dims[0], b=dims[1])
            if len(dims) == 4:
                a = a.rearrange("p (a b c d) -> p a b c d", a=dims[0], b=dims[1], c=dims[2])
            return a

        class Region:
            def __init__(self, off, size):
                self.at, self.end = off, off + size

            def take(self, *dims):
                n = int(np.prod(dims))
                assert self.at + n <= self.end, (dims, self.at + n - self.end)
                self.at += n
                return view(self.at - n, *dims)

        keep = Region(0, WORDS)
        x_sb = keep.take(NT, D)
        xhat = keep.take(NT, D)
        M_sb = keep.take(KD, D)
        id_sb, tri_sb, ones_sb, gones_sb = (keep.take(P) for _ in range(4))
        causal_sb, iotad_sb = keep.take(T), keep.take(E)
        gw_sb, gb_sb = keep.take(KD, E), keep.take(E)
        lg = keep.take(NT, E)
        wts = keep.take(2, NT)
        b1_sb = keep.take(E, FT)
        bq_sb, bk_sb = keep.take(KD), keep.take(KD)
        mv, stats, rstd, veps = keep.take(2), keep.take(6), keep.take(1), keep.take(1)
        half_sb = keep.take(2 * H)
        xn, xnT = keep.take(D), keep.take(KD, P)
        RW = KD * F
        ring_off = [[keep.at + (2 * a + b) * RW for b in range(2)] for a in range(2)]
        w1_sb = [view(ring_off[s][0], KD, F) for s in range(2)]
        w2_sb = [view(ring_off[s][1], FT, D) for s in range(2)]
        work_off = keep.at + 4 * RW
        work_size = WORDS - work_off

        rA = Region(ring_off[1][0], RW)
        wqkv0_sb, wproj0_sb = rA.take(KD, 3 * D), rA.take(KD, D)
        rA = Region(ring_off[1][1], RW)
        ctx_sb = rA.take(NB, SJ, D)
        rA.take(2 * DH)
        CW, SW = rA.take(2, DH), rA.take(2, DH)
        cos_sb, sin_sb, qkw_sb, qkws_sb = rA.take(DH), rA.take(DH), rA.take(2, DH), rA.take(2, DH)
        W = Region(work_off, work_size)
        ctxT_sb = W.take(NB, KD, S)
        zeros = W.take(4, D)
        rA = Region(ring_off[0][0], 2 * RW)
        g_sb, hA, hTA = rA.take(S), rA.take(S), rA.take(SJ, P)
        qkn, ropeA, ropeB, qkr, sq = (rA.take(2 * H, DH) for _ in range(5))
        ms, rs = rA.take(2 * H), rA.take(2 * H)
        xn0, xnT0, xn1 = rA.take(D), rA.take(KD, P), rA.take(D)
        qT = rA.take(HG, P)
        Kbd = rA.take(NB, HG, P)
        vA = rA.take(D)
        sA, pA, pT = rA.take(H, T), rA.take(H, T), rA.take(H, T)
        mxA, sumA, rsA = rA.take(H), rA.take(H), rA.take(H)
        PTb = rA.take(H, P)
        oTA = rA.take(KD, P)

        rM = Region(ring_off[1][1], RW)
        Wr_sb, Wi_sb = rM.take(KD, D), rM.take(KD, D)
        C_sb, S_sb = rM.take(KD, HD), rM.take(KD, HD)
        rM = Region(ring_off[1][0], RW)
        ATr, ATi, tmpM = rM.take(KD, D), rM.take(KD, D), rM.take(2, HD)

        W = Region(work_off, work_size)
        prob, t_a, t_b, oh1, oh2, cnt = (W.take(NT, E) for _ in range(6))
        off_sb = W.take(NT, E)
        pm1, pm2, rv1, rv2 = (W.take(NT) for _ in range(4))
        kk, pos, val, gidx, sidx = (W.take(2, NT) for _ in range(5))

        W = Region(work_off, work_size)
        hT, xe_sb, b2_sb, xeT, y_sb = [], [], [], [], []
        for _ in range(2):
            hT.append(W.take(FT, CAP))
            xe_sb.append(W.take(D))
            b2_sb.append(W.take(D))
            xeT.append(W.take(KD, CAPP))
            y_sb.append(W.take(D))
        yg = view(ring_off[1][0], 2 * NT, D)

        rC = Region(ring_off[0][0], RW)
        WkT_sb, WvT_sb, WqT_sb, WoT_sb = (rC.take(KD, D) for _ in range(4))
        rC = Region(ring_off[0][1], RW)
        wqkv1_sb, ow_sb = rC.take(KD, 3 * D), rC.take(KD, D)
        rC = Region(ring_off[1][0], RW)
        fw1_sb, fw2_sb = rC.take(KD, F2), rC.take(FT2, D)
        W = Region(work_off, work_size)
        ctxT_c = W.take(KD, 2 * S)
        PTd = W.take(H, P)
        Qbd1 = PTd.rearrange("p (b g) t -> p b g t", b=NB)
        bv_sb, bo_sb, ob_sb, fb2_sb, fbias_sb = (W.take(D) for _ in range(5))
        decay_sb = W.take(H, T)
        gng_sb, gnb_sb, fng_sb, fnb_sb = (W.take(KD) for _ in range(4))
        fb1_sb = W.take(FT2)
        gs, gvar = W.take(2 * H), W.take(H)
        gm, g2, grs = (W.take(H) for _ in range(3))
        ssq, nrm = W.take(2), W.take(2)
        rC = Region(ring_off[1][1], RW)
        Qbd = rC.take(NB, HG, P)
        v_c, P_c, PT_c, kT_c = rC.take(SJ, D), rC.take(HG, S + 1), rC.take(SJ, HG * P), rC.take(KD, S)
        mxc, nmx, smc, rsc = (rC.take(HG) for _ in range(4))
        oTc = rC.take(D)
        rC = Region(NT * D, NT * D)
        r1, t1, x2 = (rC.take(D) for _ in range(3))
        qTs = t1.rearrange("p (k t) -> p k t", k=KD)
        qk1 = rC.take(2, D)
        hT2 = qk1.rearrange("p a (f t) -> p (a f) t", t=P)
        kT1, v1 = rC.take(KD, P), rC.take(D)
        oT1 = v1

        consts_in, x_in, dft_in, wA_in, wC_in, b1_in = (sem(n) for n in (
            "consts_in", "x_in", "dft_in", "wA_in", "wC_in", "b1_in"))
        x0_in, id_in = sem("x0_in"), sem("id_in")
        pads_zero, zeros_set, xe_zeroed, half_set = (sem(n) for n in ("pads_zero", "zeros_set", "xe_zeroed", "half_set"))
        dve_step, act_step = sem("dve_step"), sem("act_step")
        at_ps, at_tmp, at_sb, m_ps, m_tmp, m_sb = (sem(n) for n in (
            "at_ps", "at_tmp", "at_sb", "m_ps", "m_tmp", "m_sb"))
        ln_stats, ln_rstd, xn_rdy, xT_ps, xT_rdy = ([sem(f"{n}{a}") for a in range(3)] for n in (
            "ln_stats", "ln_rstd", "xn_rdy", "xT_ps", "xT_rdy"))
        ctxT_in, ctx_in = sem("ctxT_in"), sem("ctx_in")
        x1_ps, g_rdy, hA_rdy, hTA_ps, hTA_rdy, gated_ps = (sem(n) for n in (
            "x1_ps", "g_rdy", "hA_rdy", "hTA_ps", "hTA_rdy", "gated_ps"))
        qkv_ps, sq_rdy, vA_rdy, ms_rdy, rs_rdy, qkr_rdy = (sem(n) for n in (
            "qkv_ps", "sq_rdy", "vA_rdy", "ms_rdy", "rs_rdy", "qkr_rdy"))
        qkT_ps, qkT_rdy, s_ps, sA_rdy, pA_rdy, PTb_rdy, oTA_ps, oTA_rdy, proj_ps, gate_ps, lg_rdy, bd_zero = (sem(n) for n in (
            "qkT_ps", "qkT_rdy", "s_ps", "sA_rdy", "pA_rdy", "PTb_rdy", "oTA_ps", "oTA_rdy", "proj_ps", "gate_ps", "lg_rdy", "bd_zero"))
        pr_sub, pr_exp, oh_rdy, cnt_ps, idx_rdy, scattered = (sem(n) for n in (
            "pr_sub", "pr_exp", "oh_rdy", "cnt_ps", "idx_rdy", "scattered"))
        w1_in, w2_in, b2_in, xe_in, y_stored = ([sem(f"{n}{s}") for s in range(2)] for n in (
            "w1_in", "w2_in", "b2_in", "xe_in", "y_stored"))
        xeT_ps, xeT_rdy, h_ps, hb_rdy, hT_rdy, y_ps, y_rdy = (sem(n) for n in (
            "xeT_ps", "xeT_rdy", "h_ps", "hb_rdy", "hT_rdy", "y_ps", "y_rdy"))
        gathered, gathered0, moe_added, wK_in, wF_in = (sem(n) for n in ("gathered", "gathered0", "moe_added", "wK_in", "wF_in"))
        ctxc_in = [sem(f"ctxc_in{s}") for s in range(2)]
        q_ps, Qbd_rdy, k_ps, k_ev, sc_ps, nmx_rdy, exp_c, pn_rdy, v_ps, v_ev, pt_ps, pt_ev, pv_ps, oT_c = (
            sem(n) for n in ("q_ps", "Qbd_rdy", "k_ps", "k_ev", "sc_ps", "nmx_rdy", "exp_c", "pn_rdy",
                             "v_ps", "v_ev", "pt_ps", "pt_ev", "pv_ps", "oT_c"))
        wo_ps, gs_rdy, gst_ps, gv_rdy, grs_rdy = (sem(n) for n in (
            "wo_ps", "gs_rdy", "gst_ps", "gv_rdy", "grs_rdy"))
        qkv1_ps, ssq_rdy, ssc_rdy, nrm_rdy, v1_rdy, q1_rdy, k1_rdy, qkT1_ps, qkT1_rdy, st_ps, PTd_rdy = (
            sem(n) for n in ("qkv1_ps", "ssq_rdy", "ssc_rdy", "nrm_rdy", "v1_rdy", "q1_rdy", "k1_rdy",
                             "qkT1_ps", "qkT1_rdy", "st_ps", "PTd_rdy"))
        oT1_ps, oT1_rdy, ow_ps, f1_ps, f1_rdy, f2_ps, spec_ps, out_rdy, stored = (sem(n) for n in (
            "oT1_ps", "oT1_rdy", "ow_ps", "f1_ps", "f1_rdy", "f2_ps", "spec_ps", "out_rdy", "stored"))

        SCALE = DH ** -0.5
        N_CONST = 7
        WA, WK, WC, WF = 6, 3, 16, 2
        q4 = [slice(32 * q, 32 * q + 32) for q in range(4)]
        HB = 4
        NHB = FT // HB

        PLAN_A = "gzawgawgzgagzaga"
        PLAN_C = [0, 2, 5, 6, 8, 9, 9, 10, 12, 14, 17, 18, 20, 22, 23, 23, 25, 26]
        N_TAIL = 15

        NV = 5

        def v_chunks(s): return ((0, 1, 2), (3, 4))[s]
        def v_rows(c): return min(P, 2 * S - P * c)
        def v_before(i, b): return 2 * NV * i + (NV * (b // 2) + 3 * (b % 2))
        def v_after(i, b): return 2 * NV * i + (0, 3, 5, 8, 10)[b + 1]
        def key_rows(s): return (P, P, 1 + s)

        def bS(g): return g
        def bV(n): return (4, 0, 1)[n]
        def bT(j): return (2, 3, 4)[j]
        def bK(m): return m
        bPV = 4

        def rows(ap):
            return ap.rearrange("(k p) n -> p k n", p=P)

        def wait(eng, s, value):
            if not (isinstance(value, int) and value <= 0):
                eng.wait_ge(s, value)

        def first_at(eng, i, tile, s, value):
            if isinstance(i, int) and i == tile:
                eng.wait_ge(s, value)

        def chain(*stages):
            for stage in stages:
                yield from stage

        def phase_a(eng, gated, scored, attended, routed, spectral, my, per):
            run(gated(0))
            interleave(PLAN_A, a=scored(0), g=gated(1))
            interleave(PLAN_A, a=scored(1), g=gated(2), z=attended(0))
            with eng.Fori(2, NT - 1) as i:
                if my is not None:
                    my.loop(i, per, 2)
                interleave(PLAN_A, a=scored(i), g=gated(i + 1), z=attended(i - 1), w=routed(i - 2))
            if my is not None:
                my.leave(NT - 1)
            interleave(PLAN_A, a=scored(NT - 1), z=attended(NT - 2), w=routed(NT - 3))
            interleave("zwwmzzm", z=attended(NT - 1), w=routed(NT - 2), m=spectral)
            run(routed(NT - 1))

        def phase_c(eng, head, cross, tail, my, per, after_head=None):
            run(head(0))
            if after_head is not None:
                after_head()
            weave(cross(0, True), head(1), PLAN_C[N_TAIL:])
            with eng.Fori(1, NT - 1) as i:
                if my is not None:
                    my.loop(i, per, 1)
                weave(cross(i, True), chain(tail(i - 1), head(i + 1)), PLAN_C)
            if my is not None:
                my.leave(NT - 1)
            weave(cross(NT - 1, False), tail(NT - 2), PLAN_C[:N_TAIL])
            run(tail(NT - 1))

        block = st.enter_context(nc.Block())

        @block.sync
        def _(sp):
            sp.dma_start(x_sb[:, 0, :], x[0:P, :]).then_inc(x0_in, 16)
            sp.dma_start(id_sb, ident).then_inc(id_in, 16)

            def load_ctxT(i):
                for b in range(NB):
                    sp.dma_start(ctxT_sb[:, b, :, 0:S],
                                 ctxT[NB * i + b].rearrange("k p s -> p k s")).then_inc(ctxT_in, 16)

            def load_ctx(i):
                for b in range(NB):
                    sp.dma_start(ctx_sb[0:SC, b, 0:2, :],
                                 ctx[NB * i + b, 0:2 * SC, :].rearrange("(j p) d -> p j d", p=SC)
                                 ).then_inc(ctx_in, 16)
                    sp.dma_start(ctx_sb[0:SL, b, 2, :], ctx[NB * i + b, 2 * SC:S, :]).then_inc(ctx_in, 16)

            load_ctxT(0)
            load_ctx(0)
            for dst, src in ((wqkv0_sb, rows(wqkv0T)), (cos_sb, cosT), (sin_sb, sinS),
                             (qkw_sb, qkw.partition_broadcast(P)), (qkws_sb, qkw_sw.partition_broadcast(P)),
                             (wproj0_sb, rows(wproj0T))):
                sp.dma_start(dst, src).then_inc(wA_in, 16)
            sp.dma_start(x_sb[:, 1:NT, :], x[P:, :].rearrange("(i p) d -> p i d", p=P)).then_inc(x_in, 16)

            def next_ctx(i):
                sp.wait_ge(x1_ps, i)
                load_ctxT(i)
                sp.wait_ge(gated_ps, i)
                load_ctx(i)

            next_ctx(1)
            for dst, src in ((causal_sb, causal), (gw_sb, rows(gate_w)), (gb_sb, gate_b.partition_broadcast(P)),
                             (tri_sb, tri), (ones_sb, ones), (gones_sb, gones), (iotad_sb, iotad)):
                sp.dma_start(dst, src).then_inc(consts_in, 16)
            sp.dma_start(b1_sb, b1).then_inc(b1_in, 16)
            sp.wait_ge(zeros_set, 1)
            for e in range(0, E, 4):
                sp.dma_start(xe_dram[e * CAP:(e + 4) * CAP, :].rearrange("(e c) d -> c e d", c=CAP),
                             zeros[0:CAP, :, :]).then_inc(xe_zeroed, 16)
            with sp.Fori(2, NT) as i:
                next_ctx(i)

            sp.wait_ge(gated_ps, NT)
            for dst, src in ((Wr_sb, Wr), (C_sb, dftC), (Wi_sb, Wi), (S_sb, dftS)):
                sp.dma_start(dst, rows(src)).then_inc(dft_in, 16)

            def load_w1(e, s):
                wait(sp, h_ps, NHB * (e - 1))
                sp.dma_start(w1_sb[s], rows(w1[e])).then_inc(w1_in[s], 16)

            def load_w2(e, s):
                wait(sp, y_ps, e - 1)
                sp.dma_start(w2_sb[s], rows(w2[e])).then_inc(w2_in[s], 16)

            def load_rows(e, s):
                wait(sp, xeT_ps, e - 1)
                sp.dma_start(xe_sb[s][0:CAP, :], xe_dram[bass.ts(e, CAP), :]).then_inc(xe_in[s], 16)

            def load_b2(e, s):
                wait(sp, y_rdy, e - 1)
                sp.dma_start(b2_sb[s][0:CAP, :],
                             b2[bass.ts(e, 1), :].rearrange("a d -> (a d)").partition_broadcast(CAP)
                             ).then_inc(b2_in[s], 16)

            sp.wait_ge(gate_ps, NT)
            load_w1(0, 0)
            load_w2(0, 0)
            sp.wait_ge(scattered, 16 * 2 * NT)
            for s in range(2):
                load_rows(s, s)
            for s in range(2):
                load_b2(s, s)
            sp.wait_ge(m_sb, 2 * KD)
            load_w1(1, 1)
            load_w2(1, 1)
            with sp.Fori(1, E // 2) as i:
                for s in range(2):
                    load_w1(2 * i + s, s)
                    load_rows(2 * i + s, s)
                    load_w2(2 * i + s, s)
                    load_b2(2 * i + s, s)

            def load_c(sm, *pairs):
                for dst, src in pairs:
                    sp.dma_start(dst, src).then_inc(sm, 16)

            sp.wait_ge(h_ps, NHB * (E - 1))
            load_c(wK_in, (WkT_sb, rows(WkT)), (bk_sb, bk), (bq_sb, bq))
            load_c(wC_in, (WvT_sb, rows(WvT)), (WqT_sb, rows(WqT)), (WoT_sb, rows(WoT)))
            sp.wait_ge(y_ps, E - 1)
            load_c(wC_in, (wqkv1_sb, rows(wqkv1T)), (ow_sb, rows(owT)))

            def load_ctxc(bb, s):
                sp.dma_start(ctxT_c[:, :, s * S:(s + 1) * S],
                             ctxT[bb].rearrange("k p s -> p k s")).then_inc(ctxc_in[s], 16)

            sp.wait_ge(y_rdy, E - 1)
            load_ctxc(0, 0)
            for s in range(2):
                sp.wait_ge(y_stored[s], 16 * (E // 2))
            load_ctxc(1, 1)
            load_c(wC_in, (bv_sb, bv.partition_broadcast(P)), (bo_sb, bo.partition_broadcast(P)),
                   (gng_sb, gng), (gnb_sb, gnb), (decay_sb, decay), (ob_sb, ob.partition_broadcast(P)),
                   (fng_sb, fng), (fnb_sb, fnb), (fb1_sb, fb1), (fb2_sb, fb2.partition_broadcast(P)),
                   (fbias_sb, fbias.partition_broadcast(P)))
            sp.wait_ge(moe_added, 2 * NT)
            load_c(wF_in, (fw1_sb, rows(fw1T)), (fw2_sb, rows(fw2T)))

            def tile_c(i, more):
                for b in range(2, NB):
                    sp.wait_ge(v_ps, v_after(i, b - 2))
                    load_ctxc(NB * i + b, b % 2)
                if more:
                    for b in range(2):
                        sp.wait_ge(v_ps, v_after(i, b + 2))
                        load_ctxc(NB * i + (NB + b), b)

            def store(i):
                sp.wait_ge(out_rdy, i + 1)
                sp.dma_start(out[bass.ts(i, P), :], x_sb[:, bass.ds(i, 1), :].rearrange("p a d -> p (a d)")
                             ).then_inc(stored, 16)

            tile_c(0, True)
            with sp.Fori(1, NT - 1) as i:
                tile_c(i, True)
                store(i - 1)
            tile_c(NT - 1, False)
            store(NT - 2)
            store(NT - 1)
            sp.wait_ge(stored, 16 * NT)

        @block.gpsimd
        def _(pool):
            pool.memset(zeros, 0.0).then_inc(zeros_set, 1)
            pool.memset(half_sb, -0.5).then_inc(half_set, 1)
            pool.wait_ge(half_set, 1)

            def root(src, dst, ready, value, done):
                pool.wait_ge(ready, value)
                pool.tensor_tensor(dst, src, half_sb[:, 0:src.shape[-1]], ALU.pow).then_inc(done, 1)

            def norm_root(a, n):
                root(veps, rstd, ln_stats[a], n + 1, ln_rstd[a])

            def gated(i):
                norm_root(0, i)
                yield
                yield
                yield
                yield
                norm_root(1, i)
                yield
                yield

            def scored(i):
                yield
                root(ms, rs, ms_rdy, i + 1, rs_rdy)
                yield
                yield
                yield
                yield

            def attended(i):
                yield
                yield
                norm_root(2, i)
                yield

            def routed(i):
                yield
                yield

            phase_a(pool, gated, scored, attended, routed, iter(()), None, None)

            pool.wait_ge(idx_rdy, 2)
            pool.wait_ge(xe_zeroed, 16 * (E // 4))
            for i in range(NT):
                for k in range(2):
                    pool.indirect_dma_start(
                        out=xe_dram, out_offset=bass.IndirectOffsetOnAxis(ap=uidx[:, 0, k, i:i + 1], axis=0),
                        in_=xhat[:, i, :], in_offset=None, bounds_check=E * CAP - 1, oob_is_err=False
                    ).then_inc(scattered, 16)

            def store_y(e, s):
                pool.wait_ge(y_rdy, e + 1)
                pool.dma_start(y_dram[bass.ts(e, CAP), :], y_sb[s][0:CAP, :]).then_inc(y_stored[s], 16)

            with pool.Fori(0, E // 2) as i:
                for s in range(2):
                    store_y(2 * i + s, s)
            for s in range(2):
                pool.wait_ge(y_stored[s], 16 * (E // 2))
            for i in range(NT):
                for k in range(2):
                    pool.indirect_dma_start(
                        out=yg[:, 2 * i + k, :], out_offset=None, in_=y_dram,
                        in_offset=bass.IndirectOffsetOnAxis(ap=uidx[:, 1, k, i:i + 1], axis=0)
                    ).then_inc(gathered if i else gathered0, 16)

            def head(i):
                norm_root(0, NT + i)
                yield
                yield
                yield

            def cross(i, more):
                for _ in range(8 * NB):
                    yield

            def tail(i):
                norm_root(1, 2 * i + NT)
                yield
                root(gvar, grs, gv_rdy, 2 * i + 1, grs_rdy)
                yield
                yield
                root(ssq, nrm, ssc_rdy, i + 1, nrm_rdy)
                yield
                for _ in range(5):
                    yield
                root(gvar, grs, gv_rdy, 2 * i + 2, grs_rdy)
                yield
                yield
                yield
                norm_root(1, 2 * i + (NT + 1))
                yield
                yield
                yield

            phase_c(pool, head, cross, tail, None, None)

        @block.scalar
        def _(act):
            my = Steps(act, act_step)

            def xT_out(a, n, bank, gain=None, shift=None, dst=xnT):
                act.wait_ge(xT_ps[a], n + 1)
                if gain is None:
                    act.activation(dst, ps[:, bank, :].rearrange("p (k t) -> p k t", k=KD), ACT.Copy
                                   ).then_inc(xT_rdy[a], 1)
                    return
                for k in range(KD):
                    ins = act.activation(dst[:, k, :], ps[:, bank, k * P:(k + 1) * P], ACT.Identity,
                                         bias=shift[:, k:k + 1], scale=gain[:, k:k + 1])
                    if k == KD - 1:
                        ins.then_inc(xT_rdy[a], 1)
                    else:
                        my.step(ins)

            def spectral_chunk(m):
                for half in range(2):
                    n = 2 * m + half
                    act.wait_ge(at_ps, n + 1)
                    if n >= 2:
                        act.wait_ge(at_sb, 2 * (n - 1))
                    act.activation(tmpM[:, half, :], ps[:, 2 * half + 1, 0:HD], ACT.Copy).then_inc(at_tmp, 1)

            def spectral():
                spectral_chunk(0)
                yield
                spectral_chunk(1)
                yield

            def gated(i):
                yield
                xT_out(0, i, 0, dst=xnT0)
                yield
                act.wait_ge(x1_ps, i + 1)
                act.activation(g_sb, ps[:, 1, 0:S], ACT.Gelu_apprx_tanh).then_inc(g_rdy, 1)
                yield
                act.wait_ge(hTA_ps, i + 1)
                act.activation(hTA[0:SC, 0:2, :], ps[0:SC, 0, 0:2 * P].rearrange("p (j t) -> p j t", j=2), ACT.Copy
                               ).then_inc(hTA_rdy, 1)
                act.activation(hTA[0:SL, 2, :], ps[0:SL, 0, 2 * P:3 * P], ACT.Copy).then_inc(hTA_rdy, 1)
                yield
                yield
                xT_out(1, i, 3)
                yield

            def scored(i):
                act.wait_ge(qkv_ps, i + 1)
                act.activation(sq, ps[:, 4:6, :].rearrange("p a (h d) -> p (a h) d", h=H), ACT.Square
                               ).then_inc(sq_rdy, 1)
                yield
                yield
                wait(act, oTA_ps, i)
                act.activation(vA, ps[:, 6, :], ACT.Copy).then_inc(vA_rdy, 1)
                yield
                act.wait_ge(qkT_ps, 2 * i + 1)
                act.activation(qT, ps[:, 3, :].rearrange("p (k t) -> p k t", k=KD), ACT.Copy
                               ).then_inc(qkT_rdy, 1)
                act.wait_ge(qkT_ps, 2 * i + 2)
                for q in range(HQ):
                    act.activation(Kbd[q4[q], :, :, q4[q]],
                                   ps[q4[q], 4, :].rearrange("p (g b t) -> p b g t", g=HG, b=NB), ACT.Copy
                                   ).then_inc(qkT_rdy, 1)
                yield
                yield

            def attended(i):
                act.wait_ge(sA_rdy, i + 1)
                act.activation(pA, sA, ACT.Exp).then_inc(pA_rdy, 1)
                yield
                act.wait_ge(oTA_ps, i + 1)
                act.activation(oTA, ps[:, 7, :].rearrange("p (k t) -> p k t", k=KD), ACT.Copy).then_inc(oTA_rdy, 1)
                yield
                yield

            def routed(i):
                xT_out(2, i, 7)
                yield
                yield

            act.wait_ge(bd_zero, 1)
            phase_a(act, gated, scored, attended, routed, spectral(), None, None)

            act.wait_ge(pr_sub, 1)
            act.activation(prob, t_a, ACT.Exp).then_inc(pr_exp, 1)

            spectral_chunk(2)
            spectral_chunk(3)
            for m in range(KD):
                act.wait_ge(m_ps, m + 1)
                if m == 0:
                    act.wait_ge(at_sb, 4 * KD)
                if m >= 2:
                    act.wait_ge(m_sb, 2 * (m - 1))
                act.activation(tmpM[:, m % 2, :], ps[:, 2 * (m % 2) + 1, 0:HD], ACT.Copy, scale=1.0 / D
                               ).then_inc(m_tmp, 1)

            act.wait_ge(pads_zero, 1)

            def rows_out(e, s):
                act.wait_ge(xeT_ps, e + 1)
                act.activation(xeT[s][:, :, 0:CAP], ps[:, 6 + s, 0:KD * CAP].rearrange("p (k c) -> p k c", k=KD),
                               ACT.Copy).then_inc(xeT_rdy, 1)

            def hidden_out(e, s):
                for g in range(NHB):
                    act.wait_ge(hb_rdy, NHB * e + (g + 1))
                    hg = hT[s][:, g * HB:(g + 1) * HB, :]
                    act.activation(hg, hg, ACT.Gelu).then_inc(hT_rdy, 1)

            rows_out(0, 0)
            with act.Fori(0, E // 2 - 1) as i:
                for s in range(2):
                    hidden_out(2 * i + s, s)
                    rows_out(2 * i + (s + 1), 1 - s)
            hidden_out(E - 2, 0)
            rows_out(E - 1, 1)
            hidden_out(E - 1, 1)

            def head(i):
                yield
                xT_out(0, NT + i, 5)
                yield
                yield

            def keys_out(bb):
                for m in range(KD):
                    act.wait_ge(k_ps, KD * bb + (m + 1))
                    act.activation(kT_c[:, m, :], ps[:, bK(m), 0:S], ACT.Identity,
                                   bias=bk_sb[:, m:m + 1], scale=1.0).then_inc(k_ev, 1)
                    if m == 1:
                        yield

            def cross(i, more):
                for b in range(NB):
                    bb = NB * i + b
                    for g in range(HG):
                        act.wait_ge(nmx_rdy, HG * bb + (g + 1))
                        act.activation(P_c[:, g, b % 2:b % 2 + S], ps[:, bS(g), 0:S], ACT.Exp, bias=nmx[:, g:g + 1],
                                       scale=SCALE, accum_out=smc[:, g:g + 1]).then_inc(exp_c, 1)
                    yield
                    yield
                    yield
                    yield
                    for j, r in enumerate(key_rows(b % 2)):
                        act.wait_ge(pt_ps, SJ * bb + (j + 1))
                        act.activation(PT_c[0:r, j, :], ps[0:r, bT(j), :], ACT.Copy).then_inc(pt_ev, 1)
                    yield
                    if b < NB - 1 or more:
                        yield from keys_out(bb + 1)
                    else:
                        yield
                    yield
                    yield

            def tail(i):
                yield
                yield
                xT_out(1, 3 * i + NT, 5, gng_sb, gnb_sb)
                yield
                act.wait_ge(qkv1_ps, i + 1)
                for a in range(2):
                    act.activation(qk1[:, a, :], ps[:, 6 + a, :], ACT.Square, accum_out=ssq[:, a:a + 1]
                                   ).then_inc(ssq_rdy, 1)
                act.activation(v1, ps[:, 5, :], ACT.Copy).then_inc(v1_rdy, 1)
                act.wait_ge(nrm_rdy, i + 1)
                act.activation(qk1[:, 0, :], ps[:, 6, :], ACT.Copy, scale=nrm[:, 0:1]).then_inc(q1_rdy, 1)
                yield
                act.wait_ge(qkT1_ps, i + 1)
                act.activation(kT1, ps[:, 7, :].rearrange("p (k t) -> p k t", k=KD), ACT.Copy
                               ).then_inc(qkT1_rdy, 1)
                for q in range(HQ):
                    act.activation(Qbd1[q4[q], :, :, q4[q]],
                                   ps[q4[q], 6, :].rearrange("p (g b t) -> p b g t", g=HG, b=NB), ACT.Copy
                                   ).then_inc(qkT1_rdy, 1)
                yield
                yield
                yield
                act.wait_ge(oT1_ps, i + 1)
                act.activation(oT1, ps[:, 7, :], ACT.Copy).then_inc(oT1_rdy, 1)
                yield
                yield
                yield
                xT_out(1, 3 * i + (NT + 1), 7, fng_sb, fnb_sb)
                yield
                act.wait_ge(f1_ps, i + 1)
                for f in range(FT2):
                    ins = act.activation(hT2[:, f, :], ps[:, 5 + f // 4, (f % 4) * P:(f % 4 + 1) * P],
                                         ACT.Silu, bias=fb1_sb[:, f:f + 1], scale=1.0)
                    if f == FT2 - 1:
                        ins.then_inc(f1_rdy, 1)
                    else:
                        my.step(ins)
                yield
                yield
                xT_out(1, 3 * i + (NT + 2), 5)
                yield
                yield

            act.wait_ge(wK_in, 16 * WK)
            act.wait_ge(y_ps, E)
            run(keys_out(0))
            act.wait_ge(wC_in, 16 * WC)
            phase_c(act, head, cross, tail, my, 13)

        @block.vector
        def _(dve):
            my = Steps(dve, dve_step)
            TT, TS, STT = dve.tensor_tensor, dve.tensor_scalar, dve.scalar_tensor_tensor

            def bc(ap, *shape):
                return ap.broadcast_to(list(shape))

            def layer_norm(a, src, dst, n, done=None):
                dve.drain()
                dve.bn_stats(stats, src)
                dve.drain()
                my.step(dve.bn_aggr(mv, stats))
                TS(veps, mv[:, 1:2], LN_EPS, None, ALU.add).then_inc(ln_stats[a], 1)
                dve.wait_ge(ln_rstd[a], n + 1)
                ins = TS(dst, src, mv[:, 0:1], rstd, ALU.subtract, ALU.mult)
                if done is None:
                    my.step(ins)
                else:
                    ins.then_inc(done, 1)

            my.step(dve.memset(PTb, 0.0))
            dve.memset(Kbd, 0.0).then_inc(bd_zero, 1)
            def tile_of(a, i):
                if isinstance(i, int):
                    return a[:, i, :]
                return a[:, bass.ds(i, 1), :].rearrange("p a d -> p (a d)")

            def gated(i):
                xt = tile_of(x_sb, i)
                first_at(dve, i, 1, x_in, 16)
                layer_norm(0, xt, xn0, i, xn_rdy[0])
                yield
                yield
                dve.wait_ge(g_rdy, i + 1)
                TT(hA, g_sb, ps[:, 1, 0:S], ALU.mult).then_inc(hA_rdy, 1)
                yield
                yield
                dve.wait_ge(gated_ps, i + 1)
                TT(xt, xt, ps[:, 2, :], ALU.add)
                layer_norm(1, xt, xn1, i, xn_rdy[1])
                yield
                yield

            def scored(i):
                first_at(dve, i, 0, wA_in, 16 * WA)
                if isinstance(i, int) and i == 0:
                    cs, sn = (bc(a.unsqueeze(1), P, 2, DH) for a in (cos_sb, sin_sb))
                    my.step(TT(CW, qkw_sb, cs, ALU.mult))
                    my.step(TT(SW, qkws_sb, sn, ALU.mult))
                yield
                dve.wait_ge(sq_rdy, i + 1)
                my.step(dve.reduce_sum(ms, sq, AX.X))
                TS(ms, ms, 1.0 / DH, RMS_EPS, ALU.mult, ALU.add).then_inc(ms_rdy, 1)
                yield
                dve.wait_ge(rs_rdy, i + 1)
                my.step(TT(qkn, ps[:, 4:6, :].rearrange("p a (h d) -> p (a h) d", h=H),
                           bc(rs.unsqueeze(2), P, 2 * H, DH), ALU.mult))
                v4 = "p (a h) d -> p a h d"
                qn4, A4, B4 = (a.rearrange(v4, a=2) for a in (qkn, ropeA, ropeB))
                my.step(TT(A4, qn4, bc(CW.unsqueeze(2), P, 2, H, DH), ALU.mult))
                hd = DH // 2
                my.step(TT(B4[:, :, :, 0:hd], qn4[:, :, :, hd:DH],
                           bc(SW[:, :, 0:hd].unsqueeze(2), P, 2, H, hd), ALU.mult))
                my.step(TT(B4[:, :, :, hd:DH], qn4[:, :, :, 0:hd],
                           bc(SW[:, :, hd:DH].unsqueeze(2), P, 2, H, hd), ALU.mult))
                TT(qkr, ropeA, ropeB, ALU.add).then_inc(qkr_rdy, 1)
                yield
                yield
                yield

            def attended(i):
                xt = tile_of(x_sb, i)
                first_at(dve, i, 0, consts_in, 16 * N_CONST)
                dve.wait_ge(s_ps, i + 1)
                my.step(STT(sA, ps[:, 6, :].rearrange("p (h t) -> p h t", h=H), SCALE,
                            bc(causal_sb.unsqueeze(1), P, H, T), ALU.mult, ALU.add))
                my.step(dve.reduce_max(mxA, sA, AX.X))
                TT(sA, sA, bc(mxA.unsqueeze(2), P, H, T), ALU.subtract).then_inc(sA_rdy, 1)
                dve.wait_ge(pA_rdy, i + 1)
                my.step(dve.reduce_sum(sumA, pA, AX.X))
                my.step(dve.reciprocal(rsA, sumA))
                my.step(TT(pA, pA, bc(rsA.unsqueeze(2), P, H, T), ALU.mult))
                my.step(dve.transpose(pT.rearrange("p h t -> p (h t)"), pA.rearrange("p h t -> p (h t)")))
                for b in range(NB):
                    dve.tensor_copy(PTb[q4[b], :, q4[b]], pT[q4[b]]).then_inc(PTb_rdy, 1)
                yield
                yield
                dve.wait_ge(proj_ps, i + 1)
                TT(xt, xt, ps[:, 7, :], ALU.add)
                layer_norm(2, xt, xn, i, xn_rdy[2])
                my.step(TS(tile_of(xhat, i), xt, mv[:, 0:1], rstd, ALU.subtract, ALU.mult))
                yield

            def routed(i):
                yield
                dve.wait_ge(gate_ps, i + 1)
                TT(tile_of(lg, i), ps[:, 7, 0:E], gb_sb, ALU.add).then_inc(lg_rdy, 1)
                yield

            def mirrored(dst, plain, other, done):
                scale = 1.0 if done is at_sb else 1.0 / D
                STT(dst[:, 0:HD], plain[:, 0:HD], scale, other[:, 0:HD], ALU.mult, ALU.add).then_inc(done, 1)
                STT(dst[:, HD:D], plain[:, HD - 2:0:-1], scale, other[:, HD - 2:0:-1],
                    ALU.mult, ALU.subtract).then_inc(done, 1)

            def spectral_chunk(m):
                dve.wait_ge(at_tmp, 2 * m + 1)
                mirrored(ATr[:, m, :], ps[:, 0, :], tmpM[:, 0, :], at_sb)
                dve.wait_ge(at_tmp, 2 * m + 2)
                STT(ATi[:, m, 0:HD], tmpM[:, 1, :], -1.0, ps[:, 2, 0:HD], ALU.mult, ALU.add).then_inc(at_sb, 1)
                STT(ATi[:, m, HD:D], tmpM[:, 1, HD - 2:0:-1], -1.0, ps[:, 2, HD - 2:0:-1],
                    ALU.mult, ALU.subtract).then_inc(at_sb, 1)

            def spectral():
                spectral_chunk(0)
                yield
                spectral_chunk(1)
                yield

            dve.wait_ge(x0_in, 16)
            phase_a(dve, gated, scored, attended, routed, spectral(), my, 15)
            dve.wait_ge(lg_rdy, NT)

            step = my.step

            def over_e(v):
                return bc(v.unsqueeze(2), P, NT, E)

            iota3 = bc(iotad_sb.unsqueeze(1), P, NT, E)
            step(dve.reduce_max(rv1, lg, AX.X))
            TT(t_a, lg, over_e(rv1), ALU.subtract).then_inc(pr_sub, 1)
            dve.wait_ge(pr_exp, 1)
            step(dve.reduce_sum(rv1, prob, AX.X))
            step(dve.reciprocal(rv2, rv1))
            step(TT(prob, prob, over_e(rv2), ALU.mult))
            for k, (oh, pm) in enumerate(((oh1, pm1), (oh2, pm2))):
                step(dve.reduce_max(pm, prob, AX.X))
                step(TT(t_a, prob, over_e(pm), ALU.is_ge))
                step(TT(t_a, t_a, iota3, ALU.mult))
                step(dve.reduce_max(kk[:, k, :], t_a, AX.X))
                step(TT(oh, iota3, over_e(kk[:, k, :]), ALU.is_equal))
                if k == 0:
                    step(TS(t_b, oh, -4.0, None, ALU.mult))
                    step(TT(prob, prob, t_b, ALU.add))
            TT(t_a, oh1, oh2, ALU.add).then_inc(oh_rdy, 1)
            spectral_chunk(2)
            step(TT(rv1, pm1, pm2, ALU.add))
            step(dve.reciprocal(rv2, rv1))
            step(TT(wts[:, 0, :], pm1, rv2, ALU.mult))
            step(TT(wts[:, 1, :], pm2, rv2, ALU.mult))
            step(dve.memset(off_sb[:, 0, :], 0.0))
            for s in range(2):
                ins = dve.memset(xeT[s], 0.0)
            ins.then_inc(pads_zero, 1)
            dve.wait_ge(cnt_ps, 2)
            tot = ps[:, 5, 0:NT * E].rearrange("p (i e) -> p i e", e=E)
            for i in range(1, NT):
                step(TT(off_sb[:, i, :], off_sb[:, i - 1, :], tot[:, i - 1, :], ALU.add))
            step(TT(cnt, off_sb, ps[:, 4, 0:NT * E].rearrange("p (i e) -> p i e", e=E), ALU.add))
            for k, oh in enumerate((oh1, oh2)):
                step(TT(t_b, oh, cnt, ALU.mult))
                step(dve.reduce_sum(pos[:, k, :], t_b, AX.X))
            step(TS(val, pos, float(CAP), None, ALU.is_lt))
            step(TT(wts, wts, val, ALU.mult))
            step(TS(kk, kk, -float(CAP), float(E * CAP), ALU.mult, ALU.add))
            step(TS(gidx, pos, float(CAP - 1), None, ALU.min))
            step(TT(gidx, gidx, kk, ALU.add))
            step(TS(val, val, -BIGROW, BIGROW, ALU.mult, ALU.add))
            step(TT(sidx, gidx, val, ALU.add))
            dve.tensor_copy(uidx[:, 0, :, :], sidx).then_inc(idx_rdy, 1)
            dve.tensor_copy(uidx[:, 1, :, :], gidx).then_inc(idx_rdy, 1)
            dve.wait_ge(idx_rdy, 2)

            spectral_chunk(3)
            for m in range(KD):
                dve.wait_ge(m_tmp, m + 1)
                mirrored(M_sb[:, m, :], ps[:, 2 * (m % 2), :], tmpM[:, m % 2, :], m_sb)

            dve.wait_ge(b1_in, 16)

            def expert(e, s, i):
                for g in range(NHB):
                    dve.wait_ge(h_ps, NHB * e + (g + 1))
                    fs = slice(g * HB, (g + 1) * HB)
                    TT(hT[s][:, fs, :], ps[:, g, 0:HB * CAPP].rearrange("p (f c) -> p f c", c=CAPP)[:, :, 0:CAP],
                       bc(tile_of(b1_sb, e)[:, fs].unsqueeze(2), P, HB, CAP), ALU.add).then_inc(hb_rdy, 1)
                dve.wait_ge(b2_in[s], 16 * i + 16)
                dve.wait_ge(y_ps, e + 1)
                wait(dve, y_stored[s], 16 * i)
                TT(y_sb[s][0:CAP, :], ps[0:CAP, 4 + s, :], b2_sb[s][0:CAP, :], ALU.add).then_inc(y_rdy, 1)

            for s in range(2):
                expert(s, s, 0)
            with dve.Fori(1, E // 2) as i:
                for s in range(2):
                    expert(2 * i + s, s, i)

            dve.wait_ge(y_ps, E)
            for s in range(2):
                dve.wait_ge(y_stored[s], 16 * (E // 2))
            step(dve.memset(PTd, 0.0))
            step(dve.memset(Qbd, 0.0))

            def add_experts(i):
                for k in range(2):
                    ins = STT(x_sb[:, i, :], yg[:, 2 * i + k, :], wts[:, k, i:i + 1], x_sb[:, i, :],
                              ALU.mult, ALU.add)
                    ins.then_inc(moe_added, 1)
                    dve.wait_ge(moe_added, 2 * i + k + 1)

            dve.wait_ge(gathered0, 32)
            add_experts(0)

            def group_sums(src):
                step(TT(t1, src, src, ALU.mult))
                step(dve.reduce_sum(gs[:, 0:H], src.rearrange("p (g c) -> p g c", g=H), AX.X))
                dve.reduce_sum(gs[:, H:2 * H], t1.rearrange("p (g c) -> p g c", g=H), AX.X).then_inc(gs_rdy, 1)

            def group_norm(src, n, bank):
                dve.wait_ge(gst_ps, n + 1)
                step(dve.tensor_copy(gm, ps[:, bank, 0:H]))
                step(TT(g2, gm, gm, ALU.mult))
                step(TT(gvar, ps[:, bank, H:2 * H], g2, ALU.subtract))
                TS(gvar, gvar, 0.0, GN_EPS, ALU.max, ALU.add).then_inc(gv_rdy, 1)
                step(TT(t1.rearrange("p (g c) -> p g c", g=H), src.rearrange("p (g c) -> p g c", g=H),
                        bc(gm.unsqueeze(2), P, H, DH), ALU.subtract))
                dve.wait_ge(grs_rdy, n + 1)
                TT(xn.rearrange("p (g c) -> p g c", g=H), t1.rearrange("p (g c) -> p g c", g=H),
                   bc(grs.unsqueeze(2), P, H, DH), ALU.mult).then_inc(xn_rdy[1], 1)

            def head(i):
                layer_norm(0, tile_of(x_sb, i), xn, NT + i, xn_rdy[0])
                yield
                yield
                dve.wait_ge(q_ps, i + 1)
                step(TT(qTs, ps[:, 7, :].rearrange("p (k t) -> p k t", k=KD), bc(bq_sb.unsqueeze(2), P, KD, P), ALU.add))
                for q in range(HQ):
                    dve.tensor_copy(Qbd[q4[q], :, :, q4[q]],
                                    qTs[q4[q]].rearrange("p g (b t) -> p b g t", b=NB)).then_inc(Qbd_rdy, 1)
                yield

            def cross(i, more):
                for b in range(NB):
                    bb = NB * i + b
                    s = b % 2
                    for g in range(HG):
                        dve.wait_ge(sc_ps, HG * bb + (g + 1))
                        step(dve.reduce_max(mxc[:, g:g + 1], ps[:, bS(g), 0:S], AX.X))
                        TS(nmx[:, g:g + 1], mxc[:, g:g + 1], -SCALE, None, ALU.mult).then_inc(nmx_rdy, 1)
                    if s == 1:
                        step(dve.memset(P_c[:, :, 0:1], 0.0))
                    yield
                    dve.wait_ge(exp_c, HG * bb + HG)
                    step(dve.reciprocal(rsc, smc))
                    for g in range(HG):
                        TS(P_c[:, g, s:s + S], P_c[:, g, s:s + S], rsc[:, g:g + 1], None, ALU.mult
                           ).then_inc(pn_rdy, 1)
                    for n, c in enumerate(v_chunks(s)):
                        r = v_rows(c)
                        dve.wait_ge(v_ps, v_before(i, b) + (n + 1))
                        TT(v_c[0:r, c % 3, :], ps[0:r, bV(n), :], bv_sb[0:r, :], ALU.add).then_inc(v_ev, 1)
                        yield
                    if s == 1:
                        yield
                    yield
                    yield
                    yield
                    dve.wait_ge(pv_ps, bb + 1)
                    pv = ps[:, bPV, :].rearrange("p (g t) -> p g t", g=HG)
                    o3 = oTc.rearrange("p (g t) -> p g t", g=HG)
                    for q in range(HQ):
                        dve.tensor_copy(o3[q4[q], :, q4[b]], pv[q4[q], :, q4[q]]).then_inc(oT_c, 1)
                    yield

            def decayed(i):
                dve.wait_ge(st_ps, i + 1)
                for b in range(NB):
                    STT(PTd[q4[b], :, q4[b]], ps[q4[b], 5, :].rearrange("p (h t) -> p h t", h=H), SCALE,
                        decay_sb[q4[b]], ALU.mult, ALU.mult).then_inc(PTd_rdy, 1)

            def tail(i):
                xt = tile_of(x_sb, i)
                dve.wait_ge(wo_ps, i + 1)
                step(TT(t1, ps[:, 6, :], bo_sb, ALU.add))
                TT(xt, xt, t1, ALU.add)
                layer_norm(1, xt, r1, 2 * i + NT)
                group_sums(r1)
                yield
                group_norm(r1, 2 * i, 7)
                yield
                yield
                dve.wait_ge(ssq_rdy, 2 * i + 2)
                TS(ssq, ssq, 1e-24, None, ALU.max).then_inc(ssc_rdy, 1)
                dve.wait_ge(nrm_rdy, i + 1)
                TS(qk1[:, 1, :], ps[:, 7, :], nrm[:, 1:2], None, ALU.mult).then_inc(k1_rdy, 1)
                yield
                yield
                decayed(i)
                yield
                yield
                yield
                dve.wait_ge(ow_ps, i + 1)
                step(TT(t1, ps[:, 5, :], ob_sb, ALU.add))
                step(TT(x2, r1, t1, ALU.add))
                group_sums(x2)
                yield
                group_norm(x2, 2 * i + 1, 6)
                yield
                yield
                yield
                dve.wait_ge(f2_ps, i + 1)
                step(TT(t1, ps[:, 7, :], fb2_sb, ALU.add))
                step(TT(t1, t1, x2, ALU.add))
                TT(xt, xt, t1, ALU.add)
                layer_norm(1, xt, xn, 2 * i + (NT + 1), xn_rdy[1])
                yield
                yield
                dve.wait_ge(spec_ps, i + 1)
                step(TT(t1, ps[:, 6, :], fbias_sb, ALU.add))
                TT(xt, xt, t1, ALU.add).then_inc(out_rdy, 1)
                yield

            def other_tiles():
                dve.wait_ge(gathered, 32 * (NT - 1))
                for i in range(1, NT):
                    add_experts(i)
                dve.wait_ge(wC_in, 16 * WC)

            dve.wait_ge(wK_in, 16 * WK)
            phase_c(dve, head, cross, tail, my, 45, other_tiles)

        @block.tensor
        def _(pe):
            def group(dst, pairs, last=None):
                for n, (lhsT, rhs) in enumerate(pairs):
                    ins = pe.matmul(dst, lhsT, rhs, start=(n == 0), stop=(n == len(pairs) - 1))
                if last is not None:
                    ins.then_inc(last, 1)

            def chunk(k):
                return slice(k * P, (k + 1) * P)

            def transposes(a, src, n, bank):
                pe.wait_ge(xn_rdy[a], n + 1)
                for k in range(KD):
                    ins = pe.transpose(ps[:, bank, chunk(k)], src[:, chunk(k)], id_sb)
                ins.then_inc(xT_ps[a], 1)

            def product(bank, pairs, last=None):
                group(ps[:, bank, 0:HD], [(a[:, k, cs], f[:, k, :]) for a, cs, f in pairs for k in range(KD)], last)

            def spectral_chunk(m):
                for half, (f0, f1) in enumerate(((C_sb, S_sb), (S_sb, C_sb))):
                    n = 2 * m + half
                    if n >= 2:
                        pe.wait_ge(at_sb, 2 * (n - 1))
                    product(2 * half, [(Wr_sb, chunk(m), f0)])
                    product(2 * half + 1, [(Wi_sb, chunk(m), f1)], at_ps)

            def spectral():
                pe.wait_ge(dft_in, 16 * 4)
                spectral_chunk(0)
                yield
                spectral_chunk(1)
                yield

            pe.wait_ge(id_in, 16)

            def gated(i):
                yield
                transposes(0, xn0, i, 0)
                yield
                pe.wait_ge(xT_rdy[0], i + 1)
                pe.wait_ge(ctxT_in, 64 * i + 64)
                for k in range(KD):
                    for b in range(NB):
                        ins = pe.matmul(ps[q4[b], 1, 0:S], xnT0[:, k, q4[b]], ctxT_sb[:, b, k, 0:S],
                                        start=(k == 0), stop=(k == KD - 1))
                ins.then_inc(x1_ps, 1)
                yield
                pe.wait_ge(hA_rdy, i + 1)
                for j in range(SJ):
                    r = SC if j < 2 else SL
                    ins = pe.transpose(ps[0:r, 0, chunk(j)], hA[:, j * SC:j * SC + r], id_sb)
                ins.then_inc(hTA_ps, 1)
                yield
                pe.wait_ge(hTA_rdy, 2 * i + 2)
                pe.wait_ge(ctx_in, 128 * i + 128)
                for j in range(SJ):
                    r = SC if j < 2 else SL
                    for b in range(NB):
                        ins = pe.matmul(ps[q4[b], 2, :], hTA[0:r, j, q4[b]], ctx_sb[0:r, b, j, :],
                                        start=(j == 0), stop=(j == SJ - 1))
                ins.then_inc(gated_ps, 1)
                yield
                wait(pe, qkT_rdy, 5 * i - 4)
                transposes(1, xn1, i, 3)
                yield

            def scored(i):
                pe.wait_ge(xT_rdy[1], i + 1)
                first_at(pe, i, 0, wA_in, 16 * WA)
                for a in range(3):
                    if a == 2:
                        wait(pe, sA_rdy, i)
                    group(ps[:, 4 + a, :], [(xnT[:, k, :], wqkv0_sb[:, k, a * D:(a + 1) * D]) for k in range(KD)],
                          qkv_ps if a == 2 else None)
                yield
                yield
                yield
                pe.wait_ge(qkr_rdy, i + 1)
                rot = qkr.rearrange("p h d -> p (h d)")
                for a in range(2):
                    for k in range(KD):
                        ins = pe.transpose(ps[:, 3 + a, chunk(k)], rot[:, a * D + k * P:a * D + (k + 1) * P], id_sb)
                    ins.then_inc(qkT_ps, 1)
                yield
                pe.wait_ge(qkT_rdy, 5 * i + 5)
                pe.wait_ge(vA_rdy, i + 1)
                for g in range(HG):
                    for b in range(NB):
                        ins = pe.matmul(ps[q4[b], 6, chunk(g)], qT[:, g, q4[b]], Kbd[:, b, g, :],
                                        start=True, stop=True)
                ins.then_inc(s_ps, 1)
                yield

            def attended(i):
                yield
                pe.wait_ge(PTb_rdy, NB * i + NB)
                pe.wait_ge(vA_rdy, i + 1)
                wait(pe, lg_rdy, i)
                for g in range(HG):
                    for q in range(HQ):
                        h = HQ * g + q
                        ins = pe.matmul(ps[q4[q], 7, chunk(g)], vA[:, h * DH:(h + 1) * DH], PTb[:, h, :],
                                        start=True, stop=True)
                ins.then_inc(oTA_ps, 1)
                yield
                pe.wait_ge(oTA_rdy, i + 1)
                group(ps[:, 7, :], [(oTA[:, k, :], wproj0_sb[:, k, :]) for k in range(KD)], proj_ps)
                yield

            def routed(i):
                first_at(pe, i, 0, consts_in, 16 * N_CONST)
                transposes(2, xn, i, 7)
                yield
                pe.wait_ge(xT_rdy[2], i + 1)
                group(ps[:, 7, 0:E], [(xnT[:, k, :], gw_sb[:, k, :]) for k in range(KD)], gate_ps)
                yield

            phase_a(pe, gated, scored, attended, routed, spectral(), None, None)

            spectral_chunk(2)
            pe.wait_ge(oh_rdy, 1)
            ohs = t_a.rearrange("p i e -> p (i e)")
            for n, m in enumerate((tri_sb, ones_sb)):
                pe.matmul(ps[:, 4 + n, 0:NT * E], m, ohs, start=True, stop=True).then_inc(cnt_ps, 1)

            spectral_chunk(3)
            pe.wait_ge(at_sb, 4 * KD)
            for m in range(KD):
                if m >= 2:
                    pe.wait_ge(m_sb, 2 * (m - 1))
                product(2 * (m % 2), [(ATr, chunk(m), C_sb)])
                product(2 * (m % 2) + 1, [(ATi, chunk(m), S_sb)], m_ps)
            pe.wait_ge(m_sb, 2 * KD)

            def rows_in(e, s, i):
                pe.wait_ge(xe_in[s], 16 * i + 16)
                for k in range(KD):
                    ins = pe.transpose(ps[:, 6 + s, k * CAP:(k + 1) * CAP], xe_sb[s][0:CAP, chunk(k)],
                                       id_sb[0:CAP, 0:CAP])
                ins.then_inc(xeT_ps, 1)

            def hidden(e, s, i):
                pe.wait_ge(xeT_rdy, e + 1)
                pe.wait_ge(w1_in[s], 16 * i + 16)
                for f in range(FT):
                    g, c = f // HB, f % HB
                    group(ps[:, g, c * CAPP:(c + 1) * CAPP],
                          [(w1_sb[s][:, k, chunk(f)], xeT[s][:, k, :]) for k in range(KD)],
                          h_ps if c == HB - 1 else None)

            def result(e, s, i):
                pe.wait_ge(w2_in[s], 16 * i + 16)
                wait(pe, y_rdy, e - 1)
                for f in range(FT):
                    if f % HB == 0:
                        pe.wait_ge(hT_rdy, NHB * e + (f // HB + 1))
                    ins = pe.matmul(ps[0:CAP, 4 + s, :], hT[s][:, f, :], w2_sb[s][:, f, :],
                                    start=(f == 0), stop=(f == FT - 1))
                ins.then_inc(y_ps, 1)

            def pair(i, last=False):
                for s in range(2):
                    hidden(2 * i + s, s, i)
                    if s == 0:
                        rows_in(2 * i + 1, 1, i)
                    elif not last:
                        rows_in(2 * i + 2, 0, i + 1)
                    result(2 * i + s, s, i)

            rows_in(0, 0, 0)
            pair(0)
            with pe.Fori(1, E // 2 - 1) as i:
                pair(i)
            pair(E // 2 - 1, True)


            def head(i):
                yield
                transposes(0, xn, NT + i, 5)
                yield
                pe.wait_ge(xT_rdy[0], NT + i + 1)
                for m in range(KD):
                    group(ps[:, 7, chunk(m)], [(WqT_sb[:, k, chunk(m)], xnT[:, k, :]) for k in range(KD)],
                          q_ps if m == KD - 1 else None)
                yield

            def keys(i, b, before):
                pe.wait_ge(ctxc_in[b % 2], 32 * i + 16 * (b // 2 + 1))
                for m in range(KD):
                    if before is not None:
                        ib, bp = before
                        if m < 2:
                            pe.wait_ge(v_ev, v_before(ib, bp) + (2 if m == 0 else len(v_chunks(bp % 2))))
                        else:
                            pe.wait_ge(pt_ev, SJ * (NB * ib + bp) + (m - 1))
                    group(ps[:, bK(m), 0:S],
                          [(WkT_sb[:, k, chunk(m)], ctxT_c[:, k, (b % 2) * S:(b % 2 + 1) * S]) for k in range(KD)],
                          k_ps)
                    if m == 1:
                        yield

            def cross(i, more):
                pe.wait_ge(Qbd_rdy, HQ * i + HQ)
                for b in range(NB):
                    bb = NB * i + b
                    s = b % 2
                    for g in range(HG):
                        pe.wait_ge(k_ev, KD * bb + (g + 1))
                        pe.matmul(ps[:, bS(g), 0:S], Qbd[:, b, g, :], kT_c[:, g, :],
                                  start=True, stop=True).then_inc(sc_ps, 1)
                    yield
                    for n, c in enumerate(v_chunks(s)):
                        r = v_rows(c)
                        if n == 0:
                            wait(pe, oT_c, HQ * bb)
                        else:
                            pe.wait_ge(exp_c, HG * bb + n)
                        if c == 2:
                            pe.wait_ge(ctxc_in[1], 32 * i + 16 * (b // 2 + 1))
                        group(ps[0:r, bV(n), :],
                              [(ctxT_c[:, k, c * P:c * P + r], WvT_sb[:, k, :]) for k in range(KD)], v_ps)
                        yield
                    if s == 1:
                        yield
                    pe.wait_ge(pn_rdy, HG * bb + HG)
                    for j, r in enumerate(key_rows(s)):
                        if j == 2:
                            pe.wait_ge(v_ev, v_before(i, b) + 1)
                        for g in range(HG):
                            ins = pe.transpose(ps[0:r, bT(j), chunk(g)], P_c[:, g, j * P:j * P + r], id_sb)
                        ins.then_inc(pt_ps, 1)
                    yield
                    if b < NB - 1:
                        yield from keys(i, b + 1, (i, b))
                    elif more:
                        yield from keys(i + 1, 0, (i, b))
                    else:
                        yield
                    yield
                    pe.wait_ge(pt_ev, SJ * bb + SJ)
                    pe.wait_ge(v_ev, v_before(i, b) + len(v_chunks(s)))
                    for g in range(HG):
                        group(ps[:, bPV, chunk(g)],
                              [(v_c[0:r, (2 * s + j) % 3, chunk(g)], PT_c[0:r, j, chunk(g)])
                               for j, r in enumerate(key_rows(s))], pv_ps if g == HG - 1 else None)
                    yield

            def group_sums(n, bank):
                pe.wait_ge(gs_rdy, n + 1)
                pe.matmul(ps[:, bank, 0:2 * H], gones_sb, gs, start=True, stop=True).then_inc(gst_ps, 1)

            def tail(i):
                pe.wait_ge(oT_c, NB * HQ * i + NB * HQ)
                group(ps[:, 6, :], [(oTc[:, chunk(k)], WoT_sb[:, k, :]) for k in range(KD)], wo_ps)
                yield
                group_sums(2 * i, 7)
                yield
                transposes(1, xn, 3 * i + NT, 5)
                yield
                pe.wait_ge(xT_rdy[1], 3 * i + (NT + 1))
                for a in range(3):
                    group(ps[:, (6, 7, 5)[a], :],
                          [(xnT[:, k, :], wqkv1_sb[:, k, a * D:(a + 1) * D]) for k in range(KD)],
                          qkv1_ps if a == 2 else None)
                yield
                pe.wait_ge(q1_rdy, i + 1)
                pe.wait_ge(k1_rdy, i + 1)
                for a in range(2):
                    for k in range(KD):
                        ins = pe.transpose(ps[:, 6 + a, chunk(k)], qk1[:, a, chunk(k)], id_sb)
                ins.then_inc(qkT1_ps, 1)
                yield
                pe.wait_ge(qkT1_rdy, 5 * i + 5)
                for g in range(HG):
                    for b in range(NB):
                        ins = pe.matmul(ps[q4[b], 5, chunk(g)], kT1[:, g, q4[b]], Qbd1[:, b, g, :],
                                        start=True, stop=True)
                ins.then_inc(st_ps, 1)
                yield
                yield
                pe.wait_ge(PTd_rdy, NB * i + NB)
                for g in range(HG):
                    for q in range(HQ):
                        h = HQ * g + q
                        ins = pe.matmul(ps[q4[q], 7, chunk(g)], v1[:, h * DH:(h + 1) * DH], PTd[:, h, :],
                                        start=True, stop=True)
                ins.then_inc(oT1_ps, 1)
                yield
                pe.wait_ge(oT1_rdy, i + 1)
                group(ps[:, 5, :], [(oT1[:, chunk(k)], ow_sb[:, k, :]) for k in range(KD)], ow_ps)
                yield
                group_sums(2 * i + 1, 6)
                yield
                transposes(1, xn, 3 * i + (NT + 1), 7)
                yield
                pe.wait_ge(xT_rdy[1], 3 * i + (NT + 2))
                pe.wait_ge(wF_in, 16 * WF)
                for f in range(FT2):
                    group(ps[:, 5 + f // 4, chunk(f % 4)],
                          [(fw1_sb[:, k, chunk(f)], xnT[:, k, :]) for k in range(KD)],
                          f1_ps if f == FT2 - 1 else None)
                yield
                pe.wait_ge(f1_rdy, i + 1)
                group(ps[:, 7, :], [(hT2[:, f, :], fw2_sb[:, f, :]) for f in range(FT2)], f2_ps)
                yield
                transposes(1, xn, 3 * i + (NT + 2), 5)
                yield
                pe.wait_ge(xT_rdy[1], 3 * i + (NT + 3))
                group(ps[:, 6, :], [(xnT[:, k, :], M_sb[:, k, :]) for k in range(KD)], spec_ps)
                yield

            pe.wait_ge(wK_in, 16 * WK)
            run(keys(0, 0, None))
            pe.wait_ge(wC_in, 16 * WC)
            phase_c(pe, head, cross, tail, None, None)



def constants():
    c = {}
    n = np.arange(D)
    ang = 2.0 * np.pi * ((n[:, None] * n[None, :]) % D) / D
    c["dftC"] = np.cos(ang).astype(np.float32)[:, 0:HD]
    c["dftS"] = np.sin(ang).astype(np.float32)[:, 0:HD]
    c["ident"] = np.eye(P, dtype=np.float32)
    p = np.arange(P)
    c["tri"] = (p[:, None] < p[None, :]).astype(np.float32)
    c["ones"] = np.ones((P, P), np.float32)
    c["gones"] = ((p[:, None] // T == p[None, :] // T) / float(T * D // H)).astype(np.float32)
    t = np.arange(T)
    c["causal"] = np.tile(np.where(t[None, :] <= t[:, None], 0.0, -1e30).astype(np.float32), (NB, 1))
    c["iotad"] = np.tile((E - np.arange(E)).astype(np.float32), (P, 1))
    freqs = (np.float32(32.0) ** (-np.arange(0, DH, 2, dtype=np.float32) / DH)).astype(np.float32)
    rot = (t.astype(np.float32)[:, None] * freqs[None, :]).astype(np.float32)
    cos, sin = np.cos(rot).astype(np.float32), np.sin(rot).astype(np.float32)
    c["cosT"] = np.tile(np.concatenate([cos, cos], 1), (NB, 1))
    c["sinS"] = np.tile(np.concatenate([-sin, sin], 1), (NB, 1))
    gam = (1.0 - np.exp(np.linspace(np.log(1.0 / 32.0), np.log(1.0 / 512.0), H))).astype(np.float32)
    dec = np.zeros((T, H, T), np.float32)
    d = t[None, :] - t[:, None]
    for h in range(H):
        dec[:, h, :] = np.where(d >= 0, gam[h].astype(np.float64) ** np.maximum(d, 0), 0.0)
    c["decay"] = np.tile(dec, (NB, 1, 1))
    return c


def columns(v):
    return v.reshape(-1, P).T


def kernel(**inputs):
    import concourse.bacc as _bacc
    from concourse.bass_utils import run_bass_kernel_spmd as _run

    a = {k: np.asarray(v) for k, v in inputs.items()}
    hd = DH // 2
    qkw = np.stack([a["L0_attn_q_norm_w"], a["L0_attn_k_norm_w"]])
    ctx = a["ctx_1024"]
    laid = {
        "x": a["x"].reshape(B * T, D),
        "ctx": ctx,
        "ctxT": ctx.transpose(0, 2, 1).reshape(B, KD, P, S),
        "wqkv0T": a["L0_attn_w_qkv"].T, "wproj0T": a["L0_attn_w_proj"].T,
        "qkw": qkw, "qkw_sw": np.concatenate([qkw[:, hd:], qkw[:, :hd]], 1),
        "gate_w": a["L0_ffn_gate_w"], "gate_b": a["L0_ffn_gate_b"],
        "w1": a["L0_ffn_w1"], "b1": a["L0_ffn_b1"].reshape(E, FT, P).transpose(2, 0, 1),
        "w2": a["L0_ffn_w2"], "b2": a["L0_ffn_b2"],
        "WqT": a["L1_xattn_Wq"].T, "bq": columns(a["L1_xattn_bq"]), "WkT": a["L1_xattn_Wk"].T, "bk": columns(a["L1_xattn_bk"]),
        "WvT": a["L1_xattn_Wv"].T, "bv": a["L1_xattn_bv"], "WoT": a["L1_xattn_Wo"].T, "bo": a["L1_xattn_bo"],
        "gng": columns(a["L1_attn_norm_g"]), "gnb": columns(a["L1_attn_norm_b"]),
        "wqkv1T": np.concatenate([a["L1_attn_qw"].T, a["L1_attn_kw"].T, a["L1_attn_vw"].T], 1),
        "owT": a["L1_attn_ow"].T, "ob": a["L1_attn_ob"],
        "fng": columns(a["L1_attn_ffn_norm_g"]), "fnb": columns(a["L1_attn_ffn_norm_b"]),
        "fw1T": a["L1_attn_w1"].T, "fb1": columns(a["L1_attn_b1"]), "fw2T": a["L1_attn_w2"].T, "fb2": a["L1_attn_b2"],
        "Wr": a["L1_ffn_w_freq_real"], "Wi": a["L1_ffn_w_freq_imag"], "fbias": a["L1_ffn_bias"],
        **constants(),
    }
    nc = _bacc.Bacc("TRN2", target_bir_lowering=False, num_devices=1)
    arrays, aps = {}, {}
    for name, v in laid.items():
        v = np.ascontiguousarray(v)
        arrays[f"in_{name}"] = v
        aps[name] = nc.dram_tensor(f"in_{name}", v.shape, mybir.dt.from_np(v.dtype), kind="ExternalInput").ap()
    aps["out"] = nc.dram_tensor("out_0", (B * T, D), fp32, kind="ExternalOutput").ap()
    aps["xe_dram"] = nc.dram_tensor("xe_rows", (E * CAP, D), fp32).ap()
    aps["y_dram"] = nc.dram_tensor("y_rows", (E * CAP, D), fp32).ap()
    perceiver_kernel(nc, **aps)
    r = _run(nc, [arrays], core_ids=[0])
    return np.asarray(r.results[0]["out_0"]).reshape(B, T, D)
```
